# Optimizing a Trainium2 kernel written in Bass

```python
import numpy as np
import jax
import jax.numpy as jnp

def _softmax(x, axis=-1):
    return jax.nn.softmax(x, axis=axis)

def _gelu(x):
    return jax.nn.gelu(x, approximate=True)

def _silu(x):
    return jax.nn.silu(x)

def _sigmoid(x):
    return jax.nn.sigmoid(x)

def _layernorm(x, axis=-1, eps=1e-05):
    m = jnp.mean(x, axis=axis, keepdims=True)
    v = jnp.var(x, axis=axis, keepdims=True)
    return (x - m) / jnp.sqrt(v + eps)

def _scatter_add(tgt, idx, src, axis=0):
    return tgt.at[idx].add(src)

def _segment_sum(src, seg, n):
    return jax.ops.segment_sum(src, seg, n)
kernel_name = 'mk_gnn_resnorm_d4_gnn_r32_5c7e2c'

def setup_inputs(seed: int=0):
    np.random.seed(seed)
    _w = jnp.asarray

    def _rec_inputs():
        import jax
        import jax.numpy as jnp
        _gk = jax.random.key(seed)
        x = -0.0001006 + 1 * jax.random.normal(jax.random.fold_in(_gk, 1), (3125, 96), jnp.float32)
        _s = jax.random.randint(jax.random.fold_in(_gk, 2), (50000,), 0, 3125, jnp.int32)
        _d = jax.random.randint(jax.random.fold_in(_gk, 3), (50000,), 0, 3125, jnp.int32)
        _loop = jnp.arange(3125, dtype=jnp.int32)
        src = jnp.concatenate([_s, _d, _loop])
        dst = jnp.concatenate([_d, _s, _loop])
        _o = jnp.argsort(dst, stable=True)
        src = src[_o]
        dst = dst[_o]
        edge_attr_96 = 5.93493e-05 + 1.00006 * jax.random.normal(jax.random.fold_in(_gk, 12), (103125, 96), jnp.float32)
        edge_weight = jax.random.uniform(jax.random.fold_in(_gk, 14), (103125,), jnp.float32, 0.0, 0.999998)
        return (x, src, dst, edge_attr_96, edge_weight)
    x, src, dst, edge_attr_96, edge_weight = _rec_inputs()

    def _L0_gnn_setup():
        import jax, jax.numpy as jnp
        import numpy as np
        N_NODES = 50000
        N_EDGES = 25000
        D_IN = 96
        D_OUT = 96
        key = jax.random.key(seed)
        k1, k2, k3, k4 = jax.random.split(key, 4)
        feat = jax.random.normal(k1, (N_NODES, D_IN), dtype=jnp.float32)
        std = (2.0 / (D_IN + D_OUT)) ** 0.5
        weight = jax.random.normal(k2, (D_IN, D_OUT), dtype=jnp.float32) * std
        bias = jnp.zeros((D_OUT,), dtype=jnp.float32)
        src = jax.random.randint(k3, (N_EDGES,), 0, N_NODES, dtype=jnp.int64)
        dst = jax.random.randint(k4, (N_EDGES,), 0, N_NODES, dtype=jnp.int64)
        return {'feat': feat, 'weight': weight, 'bias': bias, 'src': src, 'dst': dst}
    _L0_gnn_all = _L0_gnn_setup()
    _L0_gnn_in = {k: v for k, v in _L0_gnn_all.items() if k in ('weight', 'bias')}
    del _L0_gnn_all

    def _L1_gnn_setup():
        import jax, jax.numpy as jnp
        import numpy as np
        N_NODES = 50000
        N_EDGES = 25000
        D = 96

        def _gcn_conv(x, src, dst, ew, W, b):
            n = x.shape[0]
            loop = jnp.arange(n)
            src_a = jnp.concatenate([src, loop])
            dst_a = jnp.concatenate([dst, loop])
            w_a = jnp.concatenate([ew, jnp.ones((n,), ew.dtype)])
            deg = jax.ops.segment_sum(w_a, dst_a, num_segments=n)
            dis = jnp.where(deg > 0, jax.lax.rsqrt(deg), jnp.zeros_like(deg))
            norm = dis[src_a] * w_a * dis[dst_a]
            h = x @ W
            msg = h[src_a] * norm[:, None]
            out = jax.ops.segment_sum(msg, dst_a, num_segments=n)
            return out + b
        key = jax.random.key(seed)
        ks = jax.random.split(key, 10)
        x = jax.random.normal(ks[0], (N_NODES, D), dtype=jnp.float32)
        edge_index = jax.random.randint(ks[1], (2, N_EDGES), 0, N_NODES, dtype=jnp.int64)
        edge_weight = jax.random.uniform(ks[2], (N_EDGES,), dtype=jnp.float32)
        s = 1.0 / np.sqrt(D)
        W1 = jax.random.uniform(ks[3], (D, D), jnp.float32, -s, s)
        b1 = jnp.zeros((D,), jnp.float32)
        W2 = jax.random.uniform(ks[4], (D, D), jnp.float32, -s, s)
        b2 = jnp.zeros((D,), jnp.float32)
        W3 = jax.random.uniform(ks[5], (D, D), jnp.float32, -s, s)
        b3 = jnp.zeros((D,), jnp.float32)
        return {'x': x, 'edge_index': edge_index, 'edge_weight': edge_weight, 'W1': W1, 'b1': b1, 'W2': W2, 'b2': b2, 'W3': W3, 'b3': b3}
    _L1_gnn_all = _L1_gnn_setup()
    _L1_gnn_in = {k: v for k, v in _L1_gnn_all.items() if k in ('W1', 'b1', 'W2', 'b2', 'W3', 'b3')}
    del _L1_gnn_all

    def _L2_gnn_setup():
        import jax, jax.numpy as jnp
        import numpy as np
        EPS = 1e-05

        def _gcn_conv(x, edge_index, W, b):
            h = x @ W
            src, dst = (edge_index[0], edge_index[1])
            msgs = h[src]
            agg = jax.ops.segment_sum(msgs, dst, num_segments=x.shape[0])
            return agg + b

        def _graph_norm(x, weight, bias, mean_scale):
            mean = jnp.mean(x, axis=0, keepdims=True)
            xc = x - mean_scale * mean
            var = jnp.mean(xc * xc, axis=0, keepdims=True)
            return xc * jax.lax.rsqrt(var + EPS) * weight + bias
        key = jax.random.key(seed)
        ks = jax.random.split(key, 8)
        N, E, D = (50000, 25000, 96)
        x = jax.random.normal(ks[0], (N, D), dtype=jnp.float32)
        edge_index = jax.random.randint(ks[1], (2, E), 0, N, dtype=jnp.int32)
        s = 1.0 / np.sqrt(D)
        W1 = jax.random.normal(ks[2], (D, D), dtype=jnp.float32) * s
        b1 = jnp.zeros((D,), dtype=jnp.float32)
        W2 = jax.random.normal(ks[3], (D, D), dtype=jnp.float32) * s
        b2 = jnp.zeros((D,), dtype=jnp.float32)
        gn1_w = jnp.ones((D,), dtype=jnp.float32)
        gn1_b = jnp.zeros((D,), dtype=jnp.float32)
        gn1_a = jnp.ones((D,), dtype=jnp.float32)
        gn2_w = jnp.ones((D,), dtype=jnp.float32)
        gn2_b = jnp.zeros((D,), dtype=jnp.float32)
        gn2_a = jnp.ones((D,), dtype=jnp.float32)
        return {'x': x, 'edge_index': edge_index, 'W1': W1, 'b1': b1, 'W2': W2, 'b2': b2, 'gn1_w': gn1_w, 'gn1_b': gn1_b, 'gn1_a': gn1_a, 'gn2_w': gn2_w, 'gn2_b': gn2_b, 'gn2_a': gn2_a}
    _L2_gnn_all = _L2_gnn_setup()
    _L2_gnn_in = {k: v for k, v in _L2_gnn_all.items() if k in ('W1', 'b1', 'W2', 'b2', 'gn1_w', 'gn1_b', 'gn1_a', 'gn2_w', 'gn2_b', 'gn2_a')}
    del _L2_gnn_all

    def _L3_gnn_setup():
        import jax, jax.numpy as jnp
        import numpy as np
        N_NODES = 50000
        N_EDGES = 25000
        IN_DIM = 96
        NUM_HEADS = 8
        HEAD_DIM = IN_DIM // NUM_HEADS
        key = jax.random.key(seed)
        ks = jax.random.split(key, 11)
        s = 1.0 / np.sqrt(IN_DIM)
        return {'x': jax.random.normal(ks[0], (N_NODES, IN_DIM), dtype=jnp.float32), 'edge_index': jax.random.randint(ks[1], (2, N_EDGES), 0, N_NODES, dtype=jnp.int64), 'edge_attr': jax.random.normal(ks[2], (N_EDGES, IN_DIM), dtype=jnp.float32), 'Wq': jax.random.normal(ks[3], (IN_DIM, IN_DIM), dtype=jnp.float32) * s, 'bq': jax.random.normal(ks[4], (IN_DIM,), dtype=jnp.float32) * s, 'Wk': jax.random.normal(ks[5], (IN_DIM, IN_DIM), dtype=jnp.float32) * s, 'bk': jax.random.normal(ks[6], (IN_DIM,), dtype=jnp.float32) * s, 'We': jax.random.normal(ks[7], (IN_DIM, IN_DIM), dtype=jnp.float32) * s, 'be': jax.random.normal(ks[8], (IN_DIM,), dtype=jnp.float32) * s, 'Wv': jax.random.normal(ks[9], (IN_DIM, IN_DIM), dtype=jnp.float32) * s, 'bv': jax.random.normal(ks[10], (IN_DIM,), dtype=jnp.float32) * s}
    _L3_gnn_all = _L3_gnn_setup()
    _L3_gnn_in = {k: v for k, v in _L3_gnn_all.items() if k in ('Wq', 'bq', 'Wk', 'bk', 'We', 'be', 'Wv', 'bv')}
    del _L3_gnn_all
    return {'x': x, 'src': src, 'dst': dst, 'edge_attr_96': edge_attr_96, 'edge_weight': edge_weight, 'L0_gnn_weight': _L0_gnn_in['weight'], 'L0_gnn_bias': _L0_gnn_in['bias'], 'L1_gnn_W1': _L1_gnn_in['W1'], 'L1_gnn_b1': _L1_gnn_in['b1'], 'L1_gnn_W2': _L1_gnn_in['W2'], 'L1_gnn_b2': _L1_gnn_in['b2'], 'L1_gnn_W3': _L1_gnn_in['W3'], 'L1_gnn_b3': _L1_gnn_in['b3'], 'L2_gnn_W1': _L2_gnn_in['W1'], 'L2_gnn_b1': _L2_gnn_in['b1'], 'L2_gnn_W2': _L2_gnn_in['W2'], 'L2_gnn_b2': _L2_gnn_in['b2'], 'L2_gnn_gn1_w': _L2_gnn_in['gn1_w'], 'L2_gnn_gn1_b': _L2_gnn_in['gn1_b'], 'L2_gnn_gn1_a': _L2_gnn_in['gn1_a'], 'L2_gnn_gn2_w': _L2_gnn_in['gn2_w'], 'L2_gnn_gn2_b': _L2_gnn_in['gn2_b'], 'L2_gnn_gn2_a': _L2_gnn_in['gn2_a'], 'L3_gnn_Wq': _L3_gnn_in['Wq'], 'L3_gnn_bq': _L3_gnn_in['bq'], 'L3_gnn_Wk': _L3_gnn_in['Wk'], 'L3_gnn_bk': _L3_gnn_in['bk'], 'L3_gnn_We': _L3_gnn_in['We'], 'L3_gnn_be': _L3_gnn_in['be'], 'L3_gnn_Wv': _L3_gnn_in['Wv'], 'L3_gnn_bv': _L3_gnn_in['bv']}

def reference(x, src, dst, edge_attr_96, edge_weight, L0_gnn_weight, L0_gnn_bias, L1_gnn_W1, L1_gnn_b1, L1_gnn_W2, L1_gnn_b2, L1_gnn_W3, L1_gnn_b3, L2_gnn_W1, L2_gnn_b1, L2_gnn_W2, L2_gnn_b2, L2_gnn_gn1_w, L2_gnn_gn1_b, L2_gnn_gn1_a, L2_gnn_gn2_w, L2_gnn_gn2_b, L2_gnn_gn2_a, L3_gnn_Wq, L3_gnn_bq, L3_gnn_Wk, L3_gnn_bk, L3_gnn_We, L3_gnn_be, L3_gnn_Wv, L3_gnn_bv):
    import jax
    import jax.numpy as jnp

    def _L0_gnn_ref(feat, weight, bias, src, dst):
        import jax, jax.numpy as jnp
        import numpy as np
        N_NODES = 50000
        N_EDGES = 25000
        D_IN = 96
        D_OUT = 96
        N = feat.shape[0]
        ones = jnp.ones(src.shape[0], dtype=feat.dtype)
        out_deg = jax.ops.segment_sum(ones, src, num_segments=N)
        in_deg = jax.ops.segment_sum(ones, dst, num_segments=N)
        ci = jnp.clip(out_deg, 1.0, None) ** (-0.5)
        cj = jnp.clip(in_deg, 1.0, None) ** (-0.5)
        msg = feat[src] * ci[src, None]
        agg = jax.ops.segment_sum(msg, dst, num_segments=N) * cj[:, None]
        h = jnp.where(in_deg[:, None] > 0, agg, feat)
        return jnp.matmul(h, weight) + bias

    def _L1_gnn_ref(x, edge_index, edge_weight, W1, b1, W2, b2, W3, b3):
        import jax, jax.numpy as jnp
        import numpy as np
        N_NODES = 50000
        N_EDGES = 25000
        D = 96

        def _gcn_conv(x, src, dst, ew, W, b):
            n = x.shape[0]
            loop = jnp.arange(n)
            src_a = jnp.concatenate([src, loop])
            dst_a = jnp.concatenate([dst, loop])
            w_a = jnp.concatenate([ew, jnp.ones((n,), ew.dtype)])
            deg = jax.ops.segment_sum(w_a, dst_a, num_segments=n)
            dis = jnp.where(deg > 0, jax.lax.rsqrt(deg), jnp.zeros_like(deg))
            norm = dis[src_a] * w_a * dis[dst_a]
            h = x @ W
            msg = h[src_a] * norm[:, None]
            out = jax.ops.segment_sum(msg, dst_a, num_segments=n)
            return out + b
        src, dst = (edge_index[0], edge_index[1])
        h = _gcn_conv(x, src, dst, edge_weight, W1, b1)
        h = jax.nn.relu(h)
        h = _gcn_conv(h, src, dst, edge_weight, W2, b2)
        h = jax.nn.relu(h)
        h = _gcn_conv(h, src, dst, edge_weight, W3, b3)
        return h

    def _L2_gnn_ref(x, edge_index, W1, b1, W2, b2, gn1_w, gn1_b, gn1_a, gn2_w, gn2_b, gn2_a):
        import jax, jax.numpy as jnp
        import numpy as np
        EPS = 1e-05

        def _gcn_conv(x, edge_index, W, b):
            h = x @ W
            src, dst = (edge_index[0], edge_index[1])
            msgs = h[src]
            agg = jax.ops.segment_sum(msgs, dst, num_segments=x.shape[0])
            return agg + b

        def _graph_norm(x, weight, bias, mean_scale):
            mean = jnp.mean(x, axis=0, keepdims=True)
            xc = x - mean_scale * mean
            var = jnp.mean(xc * xc, axis=0, keepdims=True)
            return xc * jax.lax.rsqrt(var + EPS) * weight + bias
        identity = x
        h = _gcn_conv(x, edge_index, W1, b1)
        h = _graph_norm(h, gn1_w, gn1_b, gn1_a)
        h = jax.nn.relu(h)
        h = h + identity
        identity = h
        h2 = _gcn_conv(h, edge_index, W2, b2)
        h2 = _graph_norm(h2, gn2_w, gn2_b, gn2_a)
        h2 = jax.nn.relu(h2)
        h2 = h2 + identity
        return h2

    def _L3_gnn_ref(x, edge_index, edge_attr, Wq, bq, Wk, bk, We, be, Wv, bv):
        import jax, jax.numpy as jnp
        import numpy as np
        N_NODES = 50000
        N_EDGES = 25000
        IN_DIM = 96
        NUM_HEADS = 8
        HEAD_DIM = IN_DIM // NUM_HEADS
        N = x.shape[0]
        H, D = (NUM_HEADS, HEAD_DIM)
        Q_h = (x @ Wq + bq).reshape(N, H, D)
        K_h = (x @ Wk + bk).reshape(N, H, D)
        V_h = (x @ Wv + bv).reshape(N, H, D)
        E = (edge_attr @ We + be).reshape(-1, H, D)
        src_idx = edge_index[0]
        dst_idx = edge_index[1]
        src = K_h[src_idx]
        dest = Q_h[dst_idx]
        score = src * dest / jnp.sqrt(jnp.asarray(D, x.dtype))
        score = score * E
        score = jnp.exp(jnp.clip(score.sum(-1, keepdims=True), -5.0, 5.0))
        msg = V_h[src_idx] * score
        wV = jax.ops.segment_sum(msg, dst_idx, num_segments=N)
        Z = jax.ops.segment_sum(score, dst_idx, num_segments=N)
        h_out = wV / (Z + 1e-06)
        return h_out.reshape(N, H * D)
    edge_index = jnp.stack([src, dst])
    x = _layernorm(x + _L0_gnn_ref(x, L0_gnn_weight, L0_gnn_bias, src, dst), axis=-1)
    x = _layernorm(x + _L1_gnn_ref(x, edge_index, edge_weight, L1_gnn_W1, L1_gnn_b1, L1_gnn_W2, L1_gnn_b2, L1_gnn_W3, L1_gnn_b3), axis=-1)
    x = _layernorm(x + _L2_gnn_ref(x, edge_index, L2_gnn_W1, L2_gnn_b1, L2_gnn_W2, L2_gnn_b2, L2_gnn_gn1_w, L2_gnn_gn1_b, L2_gnn_gn1_a, L2_gnn_gn2_w, L2_gnn_gn2_b, L2_gnn_gn2_a), axis=-1)
    x = _layernorm(x + _L3_gnn_ref(x, edge_index, edge_attr_96, L3_gnn_Wq, L3_gnn_bq, L3_gnn_Wk, L3_gnn_bk, L3_gnn_We, L3_gnn_be, L3_gnn_Wv, L3_gnn_bv), axis=-1)
    return x

_drawn_inputs = setup_inputs


def setup_inputs(seed=0):
    import zlib

    import numpy as np

    out = dict(_drawn_inputs(seed))
    spreads = {'L0_gnn_bias': (0.0, 0.1),
     'L1_gnn_b1': (0.0, 0.315),
     'L1_gnn_b2': (0.0, 0.1),
     'L1_gnn_b3': (0.0, 0.1),
     'L2_gnn_b1': (0.0, 0.8),
     'L2_gnn_b2': (0.0, 0.8),
     'L2_gnn_gn1_w': (1.0, 0.2),
     'L2_gnn_gn1_b': (0.0, 0.1),
     'L2_gnn_gn1_a': (1.0, 0.2),
     'L2_gnn_gn2_w': (1.0, 0.2),
     'L2_gnn_gn2_b': (0.0, 0.1),
     'L2_gnn_gn2_a': (1.0, 0.2)}
    factors = {'edge_weight': 8.0, 'L1_gnn_W1': 6.996}
    for name, (base, spread) in spreads.items():
        noise = np.random.default_rng([zlib.crc32(name.encode()), seed]).standard_normal(out[name].shape)
        drawn = base * np.exp(spread * noise) if base else spread * noise
        out[name] = jnp.asarray(drawn.astype(out[name].dtype))
    for name, factor in factors.items():
        out[name] = (out[name] * factor).astype(out[name].dtype)
    return out
```

```python
from contextlib import ExitStack

import numpy as np

import concourse.bass as bass
from concourse import mybir

F32 = mybir.dt.float32
BF16 = mybir.dt.bfloat16
I32 = mybir.dt.int32
ALU = mybir.AluOpType
ACT = mybir.ActivationFunctionType
AX = mybir.AxisListType

P = 128
N = 3125
D = 96
E = 103125
HEADS = 8
HD = D // HEADS
NT = -(-N // P)
NPAD = NT * P
LAST = N - (NT - 1) * P
COLS = 3136
BANK = 512
NB = -(-N // BANK)
BLOCKS = [(b * BANK, min(N, (b + 1) * BANK)) for b in range(NB)]
HALF = (NB // 2) * BANK
PB = 5

G = 8
NG = -(-E // (P * G))
ET = NG * G
EPAD = ET * P
DUMP = NPAD * COLS
CELLS = DUMP + P * G
Q4 = 4
NQ = ET // Q4
ROWW = D + HEADS
NACC = 2
ACC_ROWS = NPAD + P
LN_EPS = 1e-5
GN_EPS = 1e-5

assert NG % 2 == 1 and NT % 5 == 0 and NQ % 2 == 0 and CELLS < 1 << 24


class Pool:

    def __init__(self, nc, stack):
        self.nc, self.stack = nc, stack

    def sb(self, name, shape, dt=F32):
        return self.stack.enter_context(self.nc.sbuf_tensor(name, shape, dt))

    def ps(self, name, shape):
        return self.stack.enter_context(self.nc.psum_tensor(name, shape, F32))

    def sem(self, name):
        return self.stack.enter_context(self.nc.semaphore(name))


def node_major(psum):
    return psum[:, 0:PB * BANK].rearrange("p (b c) -> p b c", c=BANK)[:, :, 0:PB * D]


def by_bank(tile):
    return tile[:, :, :].rearrange("p (b j) d -> p b (j d)", j=PB)


def node_major_by_node(psum):
    return node_major(psum).rearrange("p b (j d) -> p b j d", d=D)


def by_node(tile):
    return tile[:, :, :].rearrange("p (b j) d -> p b j d", j=PB)


def per_node_in_bank(column):
    return column.rearrange("p (b j) -> p b j", j=PB).unsqueeze(3).broadcast_to((P, NT // PB, PB, D))


def node_cols(t):
    return (t // PB) * BANK + (t % PB) * D


def per_node(column):
    return column.unsqueeze(2).broadcast_to((P, NT, D))


def per_feature(row):
    return row.unsqueeze(1).broadcast_to((P, NT, D))


def build_adjacency(nc, src_cols, dst_cols, w_cols, src_flat, dst_flat, key_dram, dstf_dram, adj):
    ctx = ExitStack()
    with ctx:
        mem = Pool(nc, ctx)
        zero = mem.sb("zero", [P, COLS])
        src_i = mem.sb("src_i", [P, ET], I32)
        dst_i = mem.sb("dst_i", [P, ET], I32)
        w = mem.sb("w", [P, ET])
        rest = mem.sb("rest", [P, ET])
        srcf = mem.sb("srcf", [P, ET])
        dstf = mem.sb("dstf", [P, ET])
        key = mem.sb("key", [P, ET])
        key_off = mem.sb("key_off", [P, ET])
        wv = mem.sb("wv", [P, ET, 5], BF16)
        fsrc_i = mem.sb("fsrc_i", [P, ET], I32)
        fdst_i = mem.sb("fdst_i", [P, ET], I32)
        fsrc = mem.sb("fsrc", [P, ET])
        fdst = mem.sb("fdst", [P, ET])
        fkey = mem.sb("fkey", [P, ET])
        dump_i = mem.sb("dump_i", [P, G], I32)
        dump = mem.sb("dump", [P, G])
        before = mem.sb("before", [P, P], BF16)
        one = mem.sb("one", [P, 1], BF16)
        keyrow = mem.sb("keyrow", [P, 2, G * P])
        SPAN = G * P + P
        eq = mem.sb("eq", [P, 2, G * SPAN], BF16)
        eq_before = mem.sb("eq_before", [P, 2, G, P], BF16)
        first_off = mem.sb("first_off", [P, G])
        cell = [mem.sb(f"cell{s}", [P, G], I32) for s in range(2)]
        pay = [mem.sb(f"pay{s}", [P, G, 2]) for s in range(2)]
        sums = [mem.ps(f"sums{s}", [P, G, 5]) for s in range(2)]

        loaded = mem.sem("loaded")
        zero_ready = mem.sem("zero_ready")
        zeroed = mem.sem("zeroed")
        flat_keys = mem.sem("flat_keys")
        keys_stored = mem.sem("keys_stored")
        consts_ready = mem.sem("consts_ready")
        row_landed = [mem.sem(f"row_landed{s}") for s in range(2)]
        eq_ready = mem.sem("eq_ready")
        sums_ready = mem.sem("sums_ready")
        sums_free = mem.sem("sums_free")
        pay_ready = mem.sem("pay_ready")
        groups_landed = mem.sem("groups_landed")
        cell_landed = [mem.sem(f"cell_landed{k}") for k in range(G)]
        block = ctx.enter_context(nc.Block())

        @block.sync
        def _(sp):
            for tile, source in ((fsrc_i, src_flat), (fdst_i, dst_flat), (src_i, src_cols),
                                 (dst_i, dst_cols), (w, w_cols)):
                sp.dma_start(tile[:], source).then_inc(loaded, 16)
            sp.wait_ge(flat_keys, 1)
            sp.dma_start(key_dram.rearrange("(p a) -> p a", p=P), fkey[:]).then_inc(keys_stored, 16)
            sp.dma_start(dstf_dram.rearrange("(p a) -> p a", p=P), fdst[:]).then_inc(keys_stored, 16)
            sp.wait_ge(keys_stored, 32)

            def load(g, s):
                keys = key_dram[bass.ds(g * (G * P), G * P)].partition_broadcast(P)
                sp.dma_start(keyrow[:, s, :], keys).then_inc(row_landed[s], 16)

            load(0, 0)
            load(1, 1)
            with sp.Fori(1, NG // 2) as i:
                for s in range(2):
                    sp.wait_ge(eq_ready, 2 * i + s - 1)
                    load(2 * i + s, s)
            sp.wait_ge(eq_ready, NG - 2)
            load(NG - 1, 0)

        @block.scalar
        def _(act):
            act.wait_ge(zero_ready, 1)
            zeros = zero[:, :].unsqueeze(1).broadcast_to((P, 2, COLS))
            rows = adj[0:DUMP, :].rearrange("(t p c) two -> t p (c two)", p=P, c=COLS)
            with act.Fori(0, NT) as t:
                act.dma_start(rows[bass.ds(t, 1)].squeeze(0).rearrange("p (a c) -> p a c", a=2),
                              zeros).then_inc(zeroed, 16)
            act.dma_start(adj[DUMP:CELLS, :].rearrange("(p a) two -> p (a two)", p=P),
                          zero[:, 0:2 * G]).then_inc(zeroed, 16)

        @block.gpsimd
        def _(pool):
            nc.gpsimd.iota(dump_i[:], pattern=[[P, G]], base=DUMP, channel_multiplier=1).then_inc(consts_ready, 1)
            nc.gpsimd.memset(before[:], 1.0)
            pool.drain()
            nc.gpsimd.affine_select(out=before[:], in_=before[:], compare_op=ALU.is_gt, fill=0.0, base=0,
                                    pattern=[[1, P]], channel_multiplier=-1).then_inc(consts_ready, 1)
            pool.wait_ge(zeroed, 16 * (NT + 1))
            last_cell = pool.to_reg(CELLS - 1)

            def scatter(g, s, first=False):
                pool.wait_ge(pay_ready, g + 1)
                if not first:
                    for k in range(G):
                        pool.wait_ge(cell_landed[k], 16 * g)
                pool.sem_inc(groups_landed, 1)
                for k in range(G):
                    nc.gpsimd.indirect_dma_start(
                        out=adj, out_offset=bass.IndirectOffsetOnAxis(ap=cell[s][:, k:k + 1], axis=0),
                        in_=pay[s][:, k, :], in_offset=None, bounds_check=last_cell, oob_is_err=True,
                        compute_op=ALU.add).then_inc(cell_landed[k], 16)

            scatter(0, 0, True)
            with pool.Fori(0, NG // 2) as i:
                scatter(2 * i + 1, 1)
                scatter(2 * i + 2, 0)
            for k in range(G):
                pool.wait_ge(cell_landed[k], 16 * NG)

        @block.tensor
        def _(pe):
            pe.wait_ge(consts_ready, 2)

            def add_equals(g, s):
                pe.wait_ge(eq_ready, g + 1)
                pe.wait_ge(sums_free, g + 1)
                eqs = eq[:, s, :].rearrange("p (k e) -> p k e", e=SPAN)
                flat = eq[:, s, :]
                for i in range(G):
                    out = sums[s][:, i, :]

                    def equals(j):
                        at = j * G * P + i * P
                        return flat[:, at:at + P]

                    def values(j, lo):
                        return wv[:, bass.ds(g * G + j, 1), lo:5].squeeze(1)

                    nc.tensor.matmul(out[:, 0:1], eq_before[:, s, i, :], one[:], start=True, stop=False)
                    nc.tensor.matmul(out[:, 1:5], equals(i), values(i, 1), start=False, stop=False)
                    for n, j in enumerate(j for j in range(G) if j != i):
                        lo = 0 if j < i else 1
                        last = nc.tensor.matmul(out[:, lo:5], equals(j), values(j, lo),
                                                start=False, stop=n == G - 2)
                last.then_inc(sums_ready, 1)

            add_equals(0, 0)
            with pe.Fori(0, NG // 2) as i:
                add_equals(2 * i + 1, 1)
                add_equals(2 * i + 2, 0)

        @block.vector
        def _(dve):
            nc.vector.memset(zero[:], 0.0).then_inc(zero_ready, 1)
            nc.vector.memset(one[:], 1.0)
            nc.vector.memset(wv[:, :, 0:2], 1.0)
            dve.wait_ge(loaded, 80)
            nc.vector.tensor_copy(fsrc[:], fsrc_i[:])
            nc.vector.tensor_copy(fdst[:], fdst_i[:])
            nc.vector.tensor_copy(srcf[:], src_i[:])
            nc.vector.tensor_copy(dstf[:], dst_i[:])
            dve.drain()
            nc.vector.scalar_tensor_tensor(fkey[:], fsrc[:], float(COLS), fdst[:], ALU.mult, ALU.add).then_inc(flat_keys, 1)
            nc.vector.scalar_tensor_tensor(key[:], srcf[:], float(COLS), dstf[:], ALU.mult, ALU.add)
            dve.wait_ge(consts_ready, 2)
            nc.vector.tensor_copy(dump[:], dump_i[:])
            nc.vector.tensor_copy(wv[:, :, 2], w[:])
            dve.drain()
            nc.vector.tensor_tensor(key_off[:].rearrange("p (g k) -> p g k", k=G),
                                    key[:].rearrange("p (g k) -> p g k", k=G),
                                    dump[:].unsqueeze(1).broadcast_to((P, NG, G)), ALU.subtract)
            nc.vector.tensor_tensor(rest[:], w[:], wv[:, :, 2], ALU.subtract)
            dve.drain()
            nc.vector.tensor_copy(wv[:, :, 3], rest[:])
            dve.drain()
            nc.vector.tensor_tensor(w[:], rest[:], wv[:, :, 3], ALU.subtract)
            dve.drain()
            nc.vector.tensor_copy(wv[:, :, 4], w[:])
            dve.sem_inc(sums_free, 2)

            def compare(g, s, use, first=False):
                dve.wait_ge(row_landed[s], 16 * (use + 1))
                if not first:
                    dve.wait_ge(sums_ready, g - 1)
                for k in range(G):
                    nc.vector.tensor_scalar(eq[:, s, k * G * P:(k + 1) * G * P], keyrow[:, s, :],
                                            key[:, bass.ds(g * G + k, 1)], None, ALU.is_equal)
                dve.drain()
                own = eq[:, s, :].rearrange("p (k e) -> p k e", e=SPAN)[:, :, 0:P]
                nc.vector.tensor_tensor(eq_before[:, s, :, :], own,
                                        before[:].unsqueeze(1).broadcast_to((P, G, P)),
                                        ALU.mult).then_inc(eq_ready, 1)

            def finish(g, s, first=False):
                dve.wait_ge(sums_ready, g + 1)
                if not first:
                    dve.wait_ge(groups_landed, g)
                nc.vector.tensor_copy(pay[s][:, :, 0], sums[s][:, :, 1])
                nc.vector.reduce_sum(pay[s][:, :, 1], sums[s][:, :, 2:5], axis=AX.X)
                nc.vector.scalar_tensor_tensor(first_off[:], sums[s][:, :, 0], 0.5,
                                               key_off[:, bass.ds(g * G, G)], ALU.is_lt,
                                               ALU.mult).then_inc(sums_free, 1)
                dve.drain()
                nc.vector.tensor_tensor(cell[s][:], first_off[:], dump[:], ALU.add).then_inc(pay_ready, 1)
                dve.drain()

            compare(0, 0, 0, True)
            compare(1, 1, 0, True)
            finish(0, 0, True)
            with dve.Fori(0, NG // 2 - 1) as i:
                compare(2 * i + 2, 0, i + 1)
                finish(2 * i + 1, 1)
                compare(2 * i + 3, 1, i + 1)
                finish(2 * i + 2, 0)
            compare(NG - 1, 0, NG // 2)
            finish(NG - 2, 1)
            finish(NG - 1, 0)


def layer_norm_stats(nc, dve, act_mem, x, mean, sd, var_ready, sd_ready, n):
    st, dif, var = act_mem
    with dve.Fori(0, NT // 5) as i:
        for j in range(5):
            nc.vector.bn_stats(st[:, bass.ds(5 * i + j, 1), :].squeeze(1), x[:, bass.ds(5 * i + j, 1), :].squeeze(1))
    dve.drain()
    nc.vector.tensor_tensor(mean[:], st[:, :, 1], st[:, :, 4], ALU.add)
    nc.vector.tensor_tensor(dif[:], st[:, :, 1], st[:, :, 4], ALU.subtract)
    nc.vector.tensor_tensor(var[:], st[:, :, 2], st[:, :, 5], ALU.add)
    dve.drain()
    nc.vector.tensor_scalar(mean[:], mean[:], 0.5, None, ALU.mult)
    nc.vector.tensor_tensor(dif[:], dif[:], dif[:], ALU.mult)
    nc.vector.tensor_scalar(var[:], var[:], 1.0 / D, None, ALU.mult)
    dve.drain()
    nc.vector.scalar_tensor_tensor(var[:], dif[:], 0.25, var[:], ALU.mult, ALU.add).then_inc(var_ready, 1)
    dve.wait_ge(sd_ready, n)
    nc.vector.reciprocal(sd[:], sd[:])
    dve.drain()


def layer_norm(nc, dve, act_mem, x, out, mean, sd, var_ready, sd_ready, n):
    layer_norm_stats(nc, dve, act_mem, x, mean, sd, var_ready, sd_ready, n)
    nc.vector.tensor_tensor(x[:], x[:], per_node(mean[:]), ALU.subtract)
    dve.drain()
    return nc.vector.tensor_tensor(out[:], x[:], per_node(sd[:]), ALU.mult)


def first_layer(nc, x_nm, adj, adj_count, adj_weight, ws, biases, ident, x, w_deg, eps):
    ctx = ExitStack()
    with ctx:
        mem = Pool(nc, ctx)
        pair = mem.sb("pair", [P, 2, COLS, 2])
        count = mem.sb("count", [P, 2, COLS])
        weight = mem.sb("weight", [P, 2, COLS])
        xT = mem.sb("xT", [D, NPAD])
        agg = mem.sb("agg", [P, NPAD])
        xw = mem.sb("xw", [P, NT, D])
        w0 = mem.sb("w0", [D, D])
        bias = mem.sb("bias0", [P, D])
        lhs = [mem.sb(f"lhs{s}", [P, D + 2]) for s in range(2)]
        lhs_w = mem.sb("lhs_w", [P, D + 2])
        odeg = [mem.sb(f"odeg{s}", [P, 1]) for s in range(2)]
        osd = [mem.sb(f"osd{s}", [P, 1]) for s in range(2)]
        degs = mem.sb("degs", [P, NT, 2])
        has_in = mem.sb("has_in", [P, NT])
        no_in = mem.sb("no_in", [P, NT])
        cj = mem.sb("cj", [P, NT])
        stats = (mem.sb("st", [P, NT, 6]), mem.sb("dif", [P, NT]), mem.sb("var", [P, NT]))
        mean = mem.sb("mean", [P, NT])
        sd = mem.sb("sd", [P, NT])
        acc = mem.ps("acc", [P, NB * BANK])
        small = mem.ps("small", [P, NT, 2])

        loaded = mem.sem("loaded")
        set_up = mem.sem("set_up")
        ident_ready = mem.sem("ident_ready")
        pair_landed = [mem.sem(f"pair_landed{s}") for s in range(2)]
        stored = [mem.sem(f"stored{s}") for s in range(2)]
        counts_ready = mem.sem("counts_ready")
        weights_ready = mem.sem("weights_ready")
        odeg_ready = mem.sem("odeg_ready")
        osd_ready = mem.sem("osd_ready")
        lhs_ready = mem.sem("lhs_ready")
        tiles_done = mem.sem("tiles_done")
        xT_ps = mem.sem("xT_ps")
        xT_ready = mem.sem("xT_ready")
        xw_ps = mem.sem("xw_ps")
        xw_ready = mem.sem("xw_ready")
        agg_ready = mem.sem("agg_ready")
        deg_ps = mem.sem("deg_ps")
        cj_max = mem.sem("cj_max")
        cj_sqrt = mem.sem("cj_sqrt")
        out_ps = mem.sem("out_ps")
        var_ready = mem.sem("var_ready")
        sd_ready = mem.sem("sd_ready")
        block = ctx.enter_context(nc.Block())
        rows = adj[0:DUMP, :].rearrange("(t p c) two -> t p c two", p=P, c=COLS)
        count_rows = adj_count.rearrange("(t p) c -> t p c", p=P)
        weight_rows = adj_weight.rearrange("(t p) c -> t p c", p=P)

        @block.sync
        def _(sp):
            sp.dma_start(x[:], x_nm).then_inc(loaded, 16)
            sp.dma_start(w0[:], ws).then_inc(loaded, 16)
            sp.dma_start(bias[:], biases.partition_broadcast(P)).then_inc(loaded, 16)

            def load(t, s):
                sp.dma_start(pair[:, s], rows[bass.ds(t, 1)].squeeze(0)).then_inc(pair_landed[s], 16)

            def store(t, s):
                sp.wait_ge(counts_ready, t + 1)
                sp.dma_start(count_rows[bass.ds(t, 1)].squeeze(0), count[:, s]).then_inc(stored[s], 16)
                sp.wait_ge(weights_ready, t + 1)
                sp.dma_start(weight_rows[bass.ds(t, 1)].squeeze(0), weight[:, s]).then_inc(stored[s], 16)

            load(0, 0)
            load(1, 1)
            with sp.Fori(0, NT // 2 - 1) as i:
                for s in range(2):
                    store(2 * i + s, s)
                    load(2 * i + s + 2, s)
            store(NT - 3, 0)
            load(NT - 1, 0)
            store(NT - 2, 1)
            store(NT - 1, 0)
            sp.wait_ge(stored[0], 32 * (NT // 2 + 1))
            sp.wait_ge(stored[1], 32 * (NT // 2))

        @block.gpsimd
        def _(pool):
            nc.gpsimd.memset(ident[:], 0.0)
            pool.drain()
            nc.gpsimd.affine_select(out=ident[:], in_=ident[:], compare_op=ALU.not_equal, fill=1.0, base=0,
                                    pattern=[[-1, P]], channel_multiplier=1).then_inc(ident_ready, 1)

        @block.scalar
        def _(act):
            act.wait_ge(set_up, 1)
            act.wait_ge(xT_ps, 1)
            nc.scalar.copy(xT[:], acc[0:D, 0:NPAD]).then_inc(xT_ready, 1)

            def split(t, s, use, first=False):
                act.wait_ge(pair_landed[s], 16 * (use + 1))
                if not first:
                    act.wait_ge(stored[s], 32 * use)
                    act.wait_ge(tiles_done, t - 1)
                nc.scalar.activation(count[:, s, :], pair[:, s, :, 0], ACT.Copy).then_inc(counts_ready, 1)
                act.wait_ge(odeg_ready, t + 1)
                nc.scalar.activation(osd[s][:], odeg[s][:], ACT.Sqrt).then_inc(osd_ready, 1)

            split(0, 0, 0, True)
            split(1, 1, 0, True)
            with act.Fori(1, NT // 2) as i:
                for s in range(2):
                    split(2 * i + s, s, i)
            split(NT - 1, 0, NT // 2)

            act.wait_ge(tiles_done, NT)
            nc.scalar.copy(agg[0:D + 2, 0:HALF], acc[0:D + 2, 0:HALF]).then_inc(agg_ready, 1)
            act.wait_ge(cj_max, 1)
            nc.scalar.activation(cj[:], cj[:], ACT.Sqrt).then_inc(cj_sqrt, 1)
            act.wait_ge(var_ready, 1)
            nc.scalar.activation(sd[:], stats[2][:], ACT.Sqrt, bias=eps[:, 0:1]).then_inc(sd_ready, 1)

        @block.tensor
        def _(pe):
            pe.wait_ge(loaded, 48)
            pe.wait_ge(ident_ready, 1)
            for t in range(NT):
                last = nc.tensor.transpose(acc[0:D, t * P:(t + 1) * P], x[:, t, :], ident[:])
            last.then_inc(xT_ps, 1)
            pe.wait_ge(xT_ready, 1)
            for t in range(NT):
                at = node_cols(t)
                last = nc.tensor.matmul(acc[:, at:at + D], xT[:, t * P:(t + 1) * P], w0[:], start=True, stop=True)
            last.then_inc(xw_ps, 1)
            pe.wait_ge(xw_ready, 1)

            def multiply(t, s, first=False, ends=False):
                pe.wait_ge(lhs_ready, t + 1)
                pe.wait_ge(counts_ready, t + 1)
                pe.wait_ge(weights_ready, t + 1)
                for lo, hi in BLOCKS:
                    nc.tensor.matmul(acc[0:D + 2, lo:hi], lhs[s][:], count[:, s, lo:hi], start=first, stop=False)
                for lo, hi in BLOCKS:
                    last = nc.tensor.matmul(acc[0:D + 2, lo:hi], lhs_w[:], weight[:, s, lo:hi], start=False, stop=ends)
                last.then_inc(tiles_done, 1)

            multiply(0, 0, True)
            multiply(1, 1)
            with pe.Fori(1, NT // 2) as i:
                for s in range(2):
                    multiply(2 * i + s, s)
            multiply(NT - 1, 0, ends=True)

            pe.wait_ge(agg_ready, 2)
            for t in range(NT):
                last = nc.tensor.matmul(small[:, t, :], agg[D:D + 2, t * P:(t + 1) * P], ident[D:D + 2, D:D + 2],
                                        start=True, stop=True)
            last.then_inc(deg_ps, 1)
            for t in range(NT):
                at = node_cols(t)
                last = nc.tensor.matmul(acc[:, at:at + D], agg[0:D, t * P:(t + 1) * P], w0[:], start=True, stop=True)
            last.then_inc(out_ps, 1)

        @block.vector
        def _(dve):
            nc.vector.memset(eps[:, 0:1], LN_EPS)
            nc.vector.memset(agg[0:D + 2, N:NPAD], 0.0)
            for s in range(2):
                nc.vector.memset(lhs[s][:, D:D + 1], 1.0)
                nc.vector.memset(lhs[s][:, D + 1:D + 2], 0.0)
            nc.vector.memset(lhs_w[:, 0:D + 1], 0.0)
            nc.vector.memset(lhs_w[:, D + 1:D + 2], 1.0).then_inc(set_up, 1)
            dve.wait_ge(loaded, 48)
            dve.wait_ge(xw_ps, 1)
            nc.vector.tensor_copy(by_bank(xw), node_major(acc)).then_inc(xw_ready, 1)

            def scale(t, s, use, first=False):
                dve.wait_ge(pair_landed[s], 16 * (use + 1))
                if not first:
                    dve.wait_ge(stored[s], 32 * use)
                    dve.wait_ge(tiles_done, t - 1)
                nc.vector.tensor_copy(weight[:, s, :], pair[:, s, :, 1]).then_inc(weights_ready, 1)
                dve.wait_ge(counts_ready, t + 1)
                nc.vector.reduce_sum(odeg[s][:], count[:, s, 0:N], axis=AX.X)
                dve.drain()
                nc.vector.tensor_scalar(odeg[s][:], odeg[s][:], 1.0, None, ALU.max).then_inc(odeg_ready, 1)
                dve.wait_ge(osd_ready, t + 1)
                nc.vector.reciprocal(osd[s][:], osd[s][:])
                dve.drain()
                nc.vector.tensor_scalar(lhs[s][:, 0:D], x[:, bass.ds(t, 1), :].squeeze(1), osd[s][:], None,
                                        ALU.mult).then_inc(lhs_ready, 1)

            scale(0, 0, 0, True)
            scale(1, 1, 0, True)
            with dve.Fori(1, NT // 2) as i:
                for s in range(2):
                    scale(2 * i + s, s, i)
            scale(NT - 1, 0, NT // 2)

            dve.wait_ge(tiles_done, NT)
            nc.vector.tensor_copy(agg[0:D + 2, HALF:N], acc[0:D + 2, HALF:N]).then_inc(agg_ready, 1)
            dve.wait_ge(deg_ps, 1)
            nc.vector.tensor_copy(degs[:], small[:])
            dve.drain()
            nc.vector.tensor_copy(w_deg[:], degs[:, :, 1])
            nc.vector.tensor_scalar(has_in[:], degs[:, :, 0], 0.0, None, ALU.is_gt)
            nc.vector.tensor_scalar(no_in[:], degs[:, :, 0], 0.0, None, ALU.is_le)
            nc.vector.tensor_scalar(cj[:], degs[:, :, 0], 1.0, None, ALU.max).then_inc(cj_max, 1)
            dve.drain()
            nc.vector.tensor_tensor(xw[:], xw[:], per_node(no_in[:]), ALU.mult)
            dve.drain()
            nc.vector.tensor_tensor(xw[:], xw[:], per_feature(bias[:]), ALU.add)
            dve.drain()
            nc.vector.tensor_tensor(x[:], xw[:], x[:], ALU.add)
            dve.wait_ge(cj_sqrt, 1)
            nc.vector.reciprocal(cj[:], cj[:])
            dve.drain()
            nc.vector.tensor_tensor(cj[:], cj[:], has_in[:], ALU.mult)
            dve.drain()
            dve.wait_ge(out_ps, 1)
            nc.vector.tensor_copy(by_bank(xw), node_major(acc))
            dve.drain()
            nc.vector.tensor_tensor(xw[:], xw[:], per_node(cj[:]), ALU.mult)
            dve.drain()
            nc.vector.tensor_tensor(xw[:], xw[:], x[:], ALU.add)
            dve.drain()
            layer_norm(nc, dve, stats, xw, x, mean, sd, var_ready, sd_ready, 1)
            dve.drain()


def convolutions(nc, adj_count, adj_weight, weights, rows, columns, ident, x, w_deg, eps):
    W_PASSES, C_PASSES = 3, 2
    SLOTS = 5
    ctx = ExitStack()
    with ctx:
        mem = Pool(nc, ctx)
        table = mem.sb("table", [P, SLOTS, COLS])
        g = mem.sb("g", [P, NT, D])
        tmp = mem.sb("tmp", [P, NT, D])
        agg = mem.sb("agg2", [D, NPAD])
        xT = mem.sb("xT2", [D, NPAD])
        lhs = [mem.sb(f"clhs{j}", [P, D]) for j in range(SLOTS)]
        wsb = [mem.sb(f"cw{k}", [D, D]) for k in range(W_PASSES + C_PASSES)]
        bias_row = [mem.sb(f"cb{k}", [P, D]) for k in range(W_PASSES)]
        cols = mem.sb("cols", [D, 8])
        zero = mem.sb("zero2", [P, BANK], BF16)
        dis = mem.sb("dis", [P, NT])
        pos = mem.sb("pos", [P, NT])
        stats = (mem.sb("st2", [P, NT, 6]), mem.sb("dif2", [P, NT]), mem.sb("var2", [P, NT]))
        mean = mem.sb("mean2", [P, NT])
        sd = mem.sb("sd2", [P, NT])
        gst = mem.sb("gst", [D, NB, 6])
        gmv = mem.sb("gmv", [D, 2])
        gs = mem.sb("gs", [D, 8])
        acc = mem.ps("acc2", [P, NB * BANK])

        loaded = mem.sem("loaded")
        set_up = mem.sem("set_up")
        dis_max = mem.sem("dis_max")
        dis_sqrt = mem.sem("dis_sqrt")
        table_landed = [mem.sem(f"table_landed{j}") for j in range(SLOTS)]
        g_ready = mem.sem("g_ready")
        lhs_ready = mem.sem("lhs_ready")
        tiles_done = mem.sem("tiles_done")
        sums_ready = mem.sem("sums_ready")
        agg_ready = mem.sem("agg_ready")
        product_ps = mem.sem("product_ps")
        product_read = mem.sem("product_read")
        gvar_ready = mem.sem("gvar_ready")
        gsd_ready = mem.sem("gsd_ready")
        gscale_ready = mem.sem("gscale_ready")
        relu_ready = mem.sem("relu_ready")
        hT_ready = mem.sem("hT_ready")
        turned_ps = mem.sem("turned_ps")
        turned_read = mem.sem("turned_read")
        var_ready = mem.sem("var_ready")
        sd_ready = mem.sem("sd_ready")
        block = ctx.enter_context(nc.Block())
        PASSES = W_PASSES + C_PASSES
        tables = [adj_weight] * W_PASSES + [adj_count] * C_PASSES

        @block.sync
        def _(sp):
            for k in range(PASSES):
                sp.dma_start(wsb[k][:], weights[k]).then_inc(loaded, 16)
            for k in range(W_PASSES):
                sp.dma_start(bias_row[k][:], rows[k].partition_broadcast(P)).then_inc(loaded, 16)
            for k in range(8):
                sp.dma_start(cols[:, k:k + 1], columns[k].unsqueeze(1)).then_inc(loaded, 16)

            def load(k, i, j):
                tile = tables[k].rearrange("(t p) c -> t p c", p=P)[bass.ds(SLOTS * i + j, 1)].squeeze(0)
                sp.dma_start(table[:, j, 0:N], tile[:, 0:N]).then_inc(table_landed[j], 16)

            for j in range(SLOTS):
                load(0, 0, j)
            for k in range(PASSES):
                with sp.Fori(1 if k == 0 else 0, NT // SLOTS) as i:
                    for j in range(SLOTS):
                        sp.wait_ge(tiles_done, k * NT + SLOTS * i + j - SLOTS + 1)
                        load(k, i, j)

        @block.scalar
        def _(act):
            act.wait_ge(dis_max, 1)
            nc.scalar.activation(dis[:], dis[:], ACT.Sqrt).then_inc(dis_sqrt, 1)

            for k in range(PASSES):
                act.wait_ge(g_ready, k + 1)

                def hand_over(i):
                    for j in range(SLOTS):
                        if not (k == 0 and isinstance(i, int)):
                            act.wait_ge(tiles_done, k * NT + SLOTS * i + j - SLOTS + 1)
                        nc.scalar.copy(lhs[j][:], g[:, bass.ds(SLOTS * i + j, 1), :].squeeze(1)).then_inc(lhs_ready, 1)

                hand_over(0)
                with act.Fori(1, NT // SLOTS) as i:
                    hand_over(i)
                act.wait_ge(sums_ready, k + 1)
                nc.scalar.copy(agg[:, 0:HALF], acc[0:D, 0:HALF]).then_inc(agg_ready, 1)
                if k >= W_PASSES:
                    n = k - W_PASSES
                    act.wait_ge(gvar_ready, n + 1)
                    nc.scalar.activation(gs[:, 1:2], gs[:, 0:1], ACT.Sqrt, bias=eps[0:D, 1:2]).then_inc(gsd_ready, 1)
                    act.wait_ge(gscale_ready, n + 1)
                    nc.scalar.activation(agg[:, 0:N], acc[0:D, 0:N], ACT.Relu, bias=gs[:, 4:5],
                                         scale=gs[:, 3:4]).then_inc(relu_ready, 1)
                if k in (W_PASSES - 1, PASSES - 1):
                    act.wait_ge(var_ready, 1 if k < W_PASSES else 2)
                    nc.scalar.activation(sd[:], stats[2][:], ACT.Sqrt, bias=eps[:, 0:1]).then_inc(sd_ready, 1)

        @block.tensor
        def _(pe):
            pe.wait_ge(loaded, 16 * (PASSES + W_PASSES + 8))
            pe.wait_ge(set_up, 1)
            products = turns = 0
            for k in range(PASSES):
                if products:
                    pe.wait_ge(product_read, min(products, W_PASSES))
                if turns:
                    pe.wait_ge(turned_read, turns)
                for lo, hi in BLOCKS:
                    nc.tensor.matmul(acc[0:D, lo:hi], zero[:, 0:D], zero[:, 0:hi - lo], start=True, stop=False)
                with pe.Fori(0, NT // SLOTS) as i:
                    for j in range(SLOTS):
                        pe.wait_ge(table_landed[j], 16 * (k * (NT // SLOTS) + i + 1))
                        pe.wait_ge(lhs_ready, k * NT + SLOTS * i + j + 1)
                        for lo, hi in BLOCKS:
                            last = nc.tensor.matmul(acc[0:D, lo:hi], lhs[j][:], table[:, j, lo:hi], start=False, stop=False)
                        last.then_inc(tiles_done, 1)
                if k < W_PASSES:
                    for t in range(NT):
                        n = min(P, N - t * P)
                        ends = (t + 1) * P % BANK == 0 or t == NT - 1
                        last = nc.tensor.matmul(acc[0:D, t * P:t * P + n], g[:, t, :], ident[:, 0:n], start=False, stop=ends)
                    last.then_inc(sums_ready, 1)
                else:
                    for lo, hi in BLOCKS:
                        last = nc.tensor.matmul(acc[0:D, lo:hi], zero[:, 0:D], zero[:, 0:hi - lo], start=False, stop=True)
                    last.then_inc(sums_ready, 1)
                pe.wait_ge(agg_ready, 2 * (k + 1))
                products += 1
                if k < W_PASSES:
                    for t in range(NT):
                        at = node_cols(t)
                        last = nc.tensor.matmul(acc[:, at:at + D], agg[:, t * P:(t + 1) * P], wsb[k][:], start=True, stop=True)
                    last.then_inc(product_ps, 1)
                else:
                    for lo, hi in BLOCKS:
                        last = nc.tensor.matmul(acc[0:D, lo:hi], wsb[k][:], agg[:, lo:hi], start=True, stop=True)
                    last.then_inc(product_ps, 1)
                if k == W_PASSES - 1:
                    pe.wait_ge(g_ready, k + 2)
                    pe.wait_ge(product_read, products)
                    for t in range(NT):
                        last = nc.tensor.transpose(acc[0:D, t * P:(t + 1) * P], x[:, t, :], ident[:])
                    last.then_inc(turned_ps, 1)
                    turns += 1
                if k >= W_PASSES:
                    pe.wait_ge(hT_ready, k - W_PASSES + 1)
                    for t in range(NT):
                        at = node_cols(t)
                        last = nc.tensor.transpose(acc[:, at:at + D], agg[:, t * P:(t + 1) * P], ident[0:D, 0:D])
                    last.then_inc(turned_ps, 1)
                    turns += 1

        @block.vector
        def _(dve):
            nc.vector.memset(zero[:], 0.0)
            nc.vector.memset(eps[:, 1:2], GN_EPS)
            nc.vector.memset(agg[:, N:NPAD], 0.0)
            nc.vector.tensor_scalar(w_deg[:], w_deg[:], 1.0, None, ALU.add)
            dve.drain()
            nc.vector.tensor_scalar(pos[:], w_deg[:], 0.0, None, ALU.is_gt)
            nc.vector.tensor_scalar(dis[:], w_deg[:], 1e-30, None, ALU.max).then_inc(dis_max, 1)
            dve.drain()
            dve.sem_inc(set_up, 1)
            dve.wait_ge(dis_sqrt, 1)
            nc.vector.reciprocal(dis[:], dis[:])
            dve.drain()
            nc.vector.tensor_tensor(dis[:], dis[:], pos[:], ALU.mult)
            dve.drain()
            nc.vector.tensor_tensor(g[:], x[:], per_node(dis[:]), ALU.mult).then_inc(g_ready, 1)
            dve.wait_ge(loaded, 16 * (PASSES + W_PASSES + 8))

            for k in range(PASSES):
                dve.wait_ge(sums_ready, k + 1)
                nc.vector.tensor_copy(agg[:, HALF:N], acc[0:D, HALF:N]).then_inc(agg_ready, 1)
                dve.wait_ge(product_ps, k + 1)
                if k < W_PASSES:
                    nc.vector.tensor_tensor(by_node(tmp), node_major_by_node(acc), per_node_in_bank(dis[:]),
                                            ALU.mult).then_inc(product_read, 1)
                    dve.drain()
                    nc.vector.tensor_tensor(tmp[:], tmp[:], per_feature(bias_row[k][:]), ALU.add)
                    dve.drain()
                    if k < W_PASSES - 1:
                        nc.vector.scalar_tensor_tensor(g[:], tmp[:], 0.0, per_node(dis[:]), ALU.max,
                                                       ALU.mult).then_inc(g_ready, 1)
                    else:
                        nc.vector.tensor_tensor(tmp[:], tmp[:], x[:], ALU.add)
                        dve.drain()
                        layer_norm(nc, dve, stats, tmp, x, mean, sd, var_ready, sd_ready, 1)
                        dve.drain()
                        nc.vector.tensor_copy(g[:], x[:]).then_inc(g_ready, 1)
                        dve.wait_ge(turned_ps, 1)
                        nc.vector.tensor_copy(xT[:], acc[0:D, 0:NPAD]).then_inc(turned_read, 1)
                        dve.drain()
                    continue
                n = k - W_PASSES
                b, gw, gb, ga = (cols[:, 4 * n + c:4 * n + c + 1] for c in range(4))
                for c, (lo, hi) in enumerate(BLOCKS):
                    nc.vector.bn_stats(gst[:, c, :], acc[0:D, lo:hi])
                dve.drain()
                nc.vector.bn_aggr(gmv[:], gst[:].rearrange("p c s -> p (c s)"))
                dve.drain()
                nc.vector.tensor_tensor(gs[:, 5:6], gmv[:, 0:1], b, ALU.add)
                dve.drain()
                nc.vector.tensor_tensor(gs[:, 6:7], gs[:, 5:6], ga, ALU.mult)
                dve.drain()
                nc.vector.tensor_tensor(gs[:, 7:8], gs[:, 5:6], gs[:, 6:7], ALU.subtract)
                dve.drain()
                nc.vector.tensor_tensor(gs[:, 7:8], gs[:, 7:8], gs[:, 7:8], ALU.mult)
                dve.drain()
                nc.vector.tensor_tensor(gs[:, 0:1], gs[:, 7:8], gmv[:, 1:2], ALU.add).then_inc(gvar_ready, 1)
                dve.wait_ge(gsd_ready, n + 1)
                nc.vector.reciprocal(gs[:, 2:3], gs[:, 1:2])
                dve.drain()
                nc.vector.tensor_tensor(gs[:, 3:4], gs[:, 2:3], gw, ALU.mult)
                nc.vector.tensor_tensor(gs[:, 4:5], b, gs[:, 6:7], ALU.subtract)
                dve.drain()
                nc.vector.tensor_tensor(gs[:, 4:5], gs[:, 4:5], gs[:, 3:4], ALU.mult)
                dve.drain()
                nc.vector.tensor_tensor(gs[:, 4:5], gs[:, 4:5], gb, ALU.add).then_inc(gscale_ready, 1)
                dve.wait_ge(relu_ready, n + 1)
                nc.vector.tensor_tensor(agg[:, 0:N], agg[:, 0:N], xT[:, 0:N], ALU.add).then_inc(hT_ready, 1)
                dve.drain()
                if n == 0:
                    nc.vector.tensor_copy(xT[:, 0:N], agg[:, 0:N])
                    dve.wait_ge(turned_ps, 2)
                    nc.vector.tensor_copy(by_bank(g), node_major(acc)).then_inc(turned_read, 1)
                    dve.drain()
                    dve.sem_inc(g_ready, 1)
                else:
                    dve.wait_ge(turned_ps, 3)
                    nc.vector.tensor_copy(by_bank(tmp), node_major(acc)).then_inc(turned_read, 1)
                    dve.drain()
                    nc.vector.tensor_tensor(tmp[:], tmp[:], x[:], ALU.add)
                    dve.drain()
                    layer_norm(nc, dve, stats, tmp, x, mean, sd, var_ready, sd_ready, 2)
                    dve.drain()


def attention(nc, attr_T, src_cols, dst_cols, dstf_dram, we, kvq_w, kvq_b, kv_dram, q_dram, sums_dram, ident, x, eps, out):
    ctx = ExitStack()
    with ctx:
        mem = Pool(nc, ctx)
        src_i = mem.sb("asrc_i", [P, ET], I32)
        dst_i = mem.sb("adst_i", [P, ET], I32)
        dstf = mem.sb("adstf", [P, ET])
        dst_off = mem.sb("adst_off", [P, ET])
        dump_i = mem.sb("adump_i", [P, 1], I32)
        dump = mem.sb("adump", [P, 1])
        before = mem.sb("abefore", [P, P])
        zero = mem.sb("azero", [P, 26 * ROWW])
        xT = mem.sb("axT", [D + 1, NPAD])
        wkvq = mem.sb("awkvq", [D + 1, 3 * D])
        wes = mem.sb("awe", [D + 1, D])
        kvq = mem.sb("akvq", [P, NT, 3 * D])
        attr = mem.sb("attr", [D + 1, 2, Q4 * P])
        drow = mem.sb("drow", [P, 2, Q4 * P])
        eq = mem.sb("aeq", [P, 2, Q4, P])
        eqb = mem.sb("aeqb", [P, Q4, P])
        earlier = mem.sb("aearlier", [P, Q4])
        first_off = mem.sb("afirst_off", [P, Q4])
        src4 = [mem.sb(f"src4_{s}", [P, Q4], I32) for s in range(2)]
        dst4 = [mem.sb(f"dst4_{s}", [P, Q4], I32) for s in range(2)]
        row4 = [mem.sb(f"row4_{s}", [P, Q4], I32) for s in range(2)]
        kv = [mem.sb(f"kv{s}", [P, Q4, 2 * D]) for s in range(2)]
        qg = [mem.sb(f"qg{s}", [P, Q4, D]) for s in range(2)]
        prod = mem.sb("prod", [P, Q4, D])
        score = mem.sb("score", [P, Q4, HEADS])
        msg = [mem.sb(f"msg{s}", [P, Q4, ROWW]) for s in range(2)]
        pay = [mem.sb(f"apay{s}", [P, Q4, ROWW]) for s in range(2)]
        stats = (mem.sb("st3", [P, NT, 6]), mem.sb("dif3", [P, NT]), mem.sb("var3", [P, NT]))
        mean = mem.sb("mean3", [P, NT])
        sd = mem.sb("sd3", [P, NT])
        total = [mem.sb(f"total{a}", [P, NT, ROWW]) for a in range(NACC)]
        z = mem.sb("z", [P, NT, HEADS])
        acc = mem.ps("acc3", [P, 4 * BANK])
        ps_e = [mem.ps(f"ps_e{s}", [P, Q4, D]) for s in range(2)]
        ps_m = [mem.ps(f"ps_m{s}", [P, Q4, ROWW]) for s in range(2)]

        loaded = mem.sem("loaded")
        consts_ready = mem.sem("consts_ready")
        zero_ready = mem.sem("zero_ready")
        zeroed = mem.sem("zeroed")
        xT_ps = mem.sem("xT_ps")
        xT_ready = mem.sem("xT_ready")
        kvq_ps = mem.sem("kvq_ps")
        kvq_read = [mem.sem("kvq_read_act"), mem.sem("kvq_read_dve")]
        tables_stored = mem.sem("tables_stored")
        attr_ones = mem.sem("attr_ones")
        edges_landed = [mem.sem(f"edges_landed{s}") for s in range(2)]
        kv_landed = [mem.sem(f"kv_landed{s}") for s in range(2)]
        prep_ready = mem.sem("prep_ready")
        e_ready = mem.sem("e_ready")
        clip_ready = mem.sem("clip_ready")
        exp_ready = mem.sem("exp_ready")
        msg_ready = mem.sem("msg_ready")
        sums_ready = mem.sem("sums_ready")
        pay_ready = mem.sem("pay_ready")
        row_landed = [mem.sem(f"arow_landed{k}") for k in range(Q4)]
        sums_back = mem.sem("sums_back")
        var_ready = mem.sem("var_ready")
        sd_ready = mem.sem("sd_ready")
        out_ready = mem.sem("out_ready")
        out_stored = mem.sem("out_stored")
        past_waits = mem.sem("past_waits")
        block = ctx.enter_context(nc.Block())
        H = 4 * BANK // P
        CLIP = 5.0 * float(np.sqrt(np.float32(HD)))

        @block.sync
        def _(sp):
            for tile, source in ((src_i[:], src_cols), (dst_i[:], dst_cols), (wes[:], we), (wkvq[0:D, :], kvq_w),
                                 (wkvq[D:D + 1, :], kvq_b)):
                sp.dma_start(tile, source).then_inc(loaded, 16)
            sp.wait_ge(kvq_read[0], NT // 2 + 1)
            sp.wait_ge(kvq_read[1], NT // 2)
            sp.dma_start(kv_dram.rearrange("(t p) c -> p t c", p=P), kvq[:, :, 0:2 * D]).then_inc(tables_stored, 16)
            sp.dma_start(q_dram.rearrange("(t p) c -> p t c", p=P), kvq[:, :, 2 * D:3 * D]).then_inc(tables_stored, 16)
            sp.wait_ge(attr_ones, 1)

            def load(q, s, first=False):
                if not first:
                    sp.wait_ge(prep_ready, q - 1)
                    sp.wait_ge(e_ready, q - 1)
                sp.dma_start(attr[0:D, s, :], attr_T[:, bass.ds(q * (Q4 * P), Q4 * P)]).then_inc(edges_landed[s], 16)
                sp.dma_start(drow[:, s, :], dstf_dram[bass.ds(q * (Q4 * P), Q4 * P)].partition_broadcast(P)).then_inc(edges_landed[s], 16)

            load(0, 0, True)
            load(1, 1, True)
            with sp.Fori(1, NQ // 2) as i:
                for s in range(2):
                    load(2 * i + s, s)
            for k in range(Q4):
                sp.wait_ge(row_landed[k], 16 * NQ)
            for a in range(NACC):
                sp.dma_start(total[a][:], sums_dram[a][0:NPAD, :].rearrange("(t p) c -> p t c", p=P)).then_inc(sums_back, 16)
            sp.wait_ge(out_ready, 1)
            sp.dma_start(out[0:(NT - 1) * P, :].rearrange("(t p) d -> p t d", p=P), kvq[:, 0:NT - 1, 0:D]).then_inc(out_stored, 16)
            sp.dma_start(out[(NT - 1) * P:N, :], kvq[0:LAST, NT - 1, 0:D]).then_inc(out_stored, 16)
            sp.wait_ge(out_stored, 32)

        @block.gpsimd
        def _(pool):
            nc.gpsimd.iota(dump_i[:], pattern=[[1, 1]], base=NPAD, channel_multiplier=1)
            nc.gpsimd.memset(before[:], 1.0)
            pool.drain()
            nc.gpsimd.affine_select(out=before[:], in_=before[:], compare_op=ALU.is_gt, fill=0.0, base=0,
                                    pattern=[[-1, P]], channel_multiplier=1).then_inc(consts_ready, 1)
            pool.wait_ge(tables_stored, 32)
            pool.wait_ge(zeroed, 16 * NACC)
            last_node = pool.to_reg(NPAD - 1)
            last_row = pool.to_reg(ACC_ROWS - 1)

            def gather(q, s, k):
                nc.gpsimd.indirect_dma_start(
                    out=kv[s][:, k, :], out_offset=None, in_=kv_dram,
                    in_offset=bass.IndirectOffsetOnAxis(ap=src4[s][:, k:k + 1], axis=0),
                    bounds_check=last_node, oob_is_err=True).then_inc(kv_landed[s], 16)
                nc.gpsimd.indirect_dma_start(
                    out=qg[s][:, k, :], out_offset=None, in_=q_dram,
                    in_offset=bass.IndirectOffsetOnAxis(ap=dst4[s][:, k:k + 1], axis=0),
                    bounds_check=last_node, oob_is_err=True).then_inc(kv_landed[s], 16)

            def scatter(q, s, k):
                if k >= NACC:
                    pool.wait_ge(row_landed[k - NACC], 16 * (q + 1))
                elif not isinstance(q, int) or q > 0:
                    pool.wait_ge(row_landed[k + Q4 - NACC], 16 * q)
                pool.sem_inc(past_waits, 1)
                nc.gpsimd.indirect_dma_start(
                    out=sums_dram[k % NACC], out_offset=bass.IndirectOffsetOnAxis(ap=row4[s][:, k:k + 1], axis=0),
                    in_=pay[s][:, k, :], in_offset=None, bounds_check=last_row, oob_is_err=True,
                    compute_op=ALU.add).then_inc(row_landed[k], 16)

            def step(q, s, first=False):
                pool.wait_ge(prep_ready, q + 1)
                if not first:
                    pool.wait_ge(msg_ready, q - 1)
                pool.sem_inc(past_waits, 1)
                for k in range(Q4):
                    gather(q, s, k)
                    if not isinstance(q, int) or q > 0:
                        if k == 0:
                            pool.wait_ge(pay_ready, q)
                        scatter(q - 1, 1 - s, k)

            step(0, 0, True)
            step(1, 1, True)
            with pool.Fori(1, NQ // 2) as i:
                for s in range(2):
                    step(2 * i + s, s)
            pool.wait_ge(pay_ready, NQ)
            for k in range(Q4):
                scatter(NQ - 1, 1, k)

        @block.scalar
        def _(act):
            act.wait_ge(zero_ready, 1)
            for a in range(NACC):
                act.dma_start(sums_dram[a].rearrange("(p r) c -> p (r c)", p=P), zero[:]).then_inc(zeroed, 16)
            act.wait_ge(xT_ps, 1)
            nc.scalar.copy(xT[0:D, 0:H * P], acc[0:D, 0:H * P]).then_inc(xT_ready, 1)
            act.wait_ge(xT_ps, 2)
            nc.scalar.copy(xT[0:D, H * P:NPAD], acc[0:D, 0:NPAD - H * P]).then_inc(xT_ready, 1)
            for t in range(0, NT, 2):
                act.wait_ge(kvq_ps, t + 1)
                at = (t % 4) * BANK
                nc.scalar.copy(kvq[:, t, :], acc[:, at:at + 3 * D]).then_inc(kvq_read[0], 1)

            def step(q, s, first=False):
                act.wait_ge(clip_ready, q + 1)
                nc.scalar.activation(msg[s][:, :, D:ROWW], score[:], ACT.Exp, scale=1.0 / float(np.sqrt(np.float32(HD)))).then_inc(exp_ready, 1)
                act.wait_ge(sums_ready, q + 1)
                if not first:
                    for k in range(Q4):
                        act.wait_ge(row_landed[k], 16 * (q - 1))
                nc.scalar.copy(pay[s][:], ps_m[s][:]).then_inc(pay_ready, 1)

            step(0, 0, True)
            step(1, 1, True)
            with act.Fori(1, NQ // 2) as i:
                for s in range(2):
                    step(2 * i + s, s)
            act.wait_ge(var_ready, 1)
            nc.scalar.activation(sd[:], stats[2][:], ACT.Sqrt, bias=eps[:, 0:1]).then_inc(sd_ready, 1)

        @block.tensor
        def _(pe):
            for t in range(NT):
                if t == H:
                    last.then_inc(xT_ps, 1)
                    pe.wait_ge(xT_ready, 1)
                at = t % H * P
                last = nc.tensor.transpose(acc[0:D, at:at + P], x[:, t, :], ident[:])
            last.then_inc(xT_ps, 1)
            pe.wait_ge(xT_ready, 2)
            pe.wait_ge(attr_ones, 1)
            pe.wait_ge(loaded, 80)
            for t in range(NT):
                if t >= 4:
                    pe.wait_ge(kvq_read[t % 2], t // 2 - 1)
                at = (t % 4) * BANK
                nc.tensor.matmul(acc[:, at:at + 3 * D], xT[:, t * P:(t + 1) * P], wkvq[:], start=True, stop=True).then_inc(kvq_ps, 1)

            def edges(q, s, use, first=False):
                pe.wait_ge(edges_landed[s], 32 * (use + 1))
                if not first:
                    pe.wait_ge(msg_ready, q - 1)
                for k in range(Q4):
                    last = nc.tensor.matmul(ps_e[s][:, k, :], attr[:, s, k * P:(k + 1) * P], wes[:], start=True, stop=True)
                last.then_inc(e_ready, 1)

            def add_up(q, s, first=False):
                pe.wait_ge(msg_ready, q + 1)
                if not first:
                    pe.wait_ge(pay_ready, q - 1)
                for k in range(Q4):
                    last = nc.tensor.matmul(ps_m[s][:, k, :], eq[:, s, k, :], msg[s][:, k, :], start=True, stop=True)
                last.then_inc(sums_ready, 1)

            edges(0, 0, 0, True)
            edges(1, 1, 0, True)
            add_up(0, 0, True)
            edges(2, 0, 1)
            add_up(1, 1, True)
            with pe.Fori(1, NQ // 2 - 1) as i:
                edges(2 * i + 1, 1, i)
                add_up(2 * i, 0)
                edges(2 * i + 2, 0, i + 1)
                add_up(2 * i + 1, 1)
            edges(NQ - 1, 1, NQ // 2 - 1)
            add_up(NQ - 2, 0)
            add_up(NQ - 1, 1)

        @block.vector
        def _(dve):
            nc.vector.memset(zero[:], 0.0).then_inc(zero_ready, 1)
            nc.vector.memset(attr[D:D + 1, :, :], 1.0)
            nc.vector.memset(xT[D:D + 1, :], 1.0).then_inc(attr_ones, 1)
            dve.wait_ge(loaded, 80)
            dve.wait_ge(consts_ready, 1)
            nc.vector.tensor_copy(dstf[:], dst_i[:])
            nc.vector.tensor_copy(dump[:], dump_i[:])
            dve.drain()
            nc.vector.tensor_scalar(dst_off[:], dstf[:], dump[:], None, ALU.subtract)
            for t in range(1, NT, 2):
                dve.wait_ge(kvq_ps, t + 1)
                at = (t % 4) * BANK
                nc.vector.tensor_copy(kvq[:, t, :], acc[:, at:at + 3 * D]).then_inc(kvq_read[1], 1)

            def prepare(q, s, use, first=False):
                dve.wait_ge(edges_landed[s], 32 * (use + 1))
                if not first:
                    dve.wait_ge(sums_ready, q - 1)
                    for k in range(Q4):
                        dve.wait_ge(row_landed[k], 16 * (q - 1))
                nc.vector.tensor_copy(src4[s][:], src_i[:, bass.ds(q * Q4, Q4)])
                nc.vector.tensor_copy(dst4[s][:], dst_i[:, bass.ds(q * Q4, Q4)])
                for k in range(Q4):
                    nc.vector.tensor_scalar(eq[:, s, k, :], drow[:, s, k * P:(k + 1) * P], dstf[:, bass.ds(q * Q4 + k, 1)],
                                            None, ALU.is_equal)
                dve.drain()
                nc.vector.tensor_tensor(eqb[:], eq[:, s, :, :], before[:].unsqueeze(1).broadcast_to((P, Q4, P)), ALU.mult)
                dve.drain()
                nc.vector.reduce_sum(earlier[:], eqb[:], axis=AX.X)
                dve.drain()
                nc.vector.scalar_tensor_tensor(first_off[:], earlier[:], 0.5, dst_off[:, bass.ds(q * Q4, Q4)], ALU.is_lt, ALU.mult)
                dve.drain()
                nc.vector.tensor_scalar(row4[s][:], first_off[:], dump[:], None, ALU.add).then_inc(prep_ready, 1)

            def attend(q, s, use, first=False):
                dve.wait_ge(kv_landed[s], 32 * Q4 * (use + 1))
                nc.vector.tensor_tensor(prod[:], kv[s][:, :, 0:D], qg[s][:], ALU.mult)
                dve.drain()
                dve.wait_ge(e_ready, q + 1)
                nc.vector.tensor_tensor(prod[:], prod[:], ps_e[s][:], ALU.mult)
                dve.drain()
                nc.vector.reduce_sum(score[:].rearrange("p k h -> p (k h)"), prod[:].rearrange("p k (h c) -> p (k h) c", c=HD), axis=AX.X)
                dve.drain()
                nc.vector.tensor_scalar(score[:], score[:], CLIP, -CLIP, ALU.min, ALU.max).then_inc(clip_ready, 1)
                dve.wait_ge(exp_ready, q + 1)
                nc.vector.tensor_tensor(msg[s][:, :, 0:D].rearrange("p k (h c) -> p k h c", c=HD),
                                        kv[s][:, :, D:2 * D].rearrange("p k (h c) -> p k h c", c=HD),
                                        msg[s][:, :, D:ROWW].unsqueeze(3).broadcast_to((P, Q4, HEADS, HD)),
                                        ALU.mult).then_inc(msg_ready, 1)

            prepare(0, 0, 0, True)
            prepare(1, 1, 0, True)
            attend(0, 0, 0)
            prepare(2, 0, 1)
            attend(1, 1, 0)
            with dve.Fori(1, NQ // 2 - 1) as i:
                prepare(2 * i + 1, 1, i)
                attend(2 * i, 0, i)
                prepare(2 * i + 2, 0, i + 1)
                attend(2 * i + 1, 1, i)
            prepare(NQ - 1, 1, NQ // 2 - 1)
            attend(NQ - 2, 0, NQ // 2 - 1)
            attend(NQ - 1, 1, NQ // 2 - 1)

            dve.wait_ge(sums_back, 16 * NACC)
            nc.vector.tensor_tensor(total[0][:], total[0][:], total[1][:], ALU.add)
            dve.drain()
            nc.vector.tensor_scalar(z[:], total[0][:, :, D:ROWW], 1e-6, None, ALU.add)
            dve.drain()
            nc.vector.reciprocal(z[:], z[:])
            dve.drain()
            res = total[1][:, :, 0:D]
            for t in range(0, NT, 5):
                nc.vector.tensor_tensor(res[:, t:t + 5].rearrange("p t (h c) -> p t h c", c=HD),
                                        total[0][:, t:t + 5, 0:D].rearrange("p t (h c) -> p t h c", c=HD),
                                        z[:, t:t + 5].unsqueeze(3).broadcast_to((P, 5, HEADS, HD)), ALU.mult)
            dve.drain()
            nc.vector.tensor_tensor(x[:], x[:], res, ALU.add)
            dve.drain()
            layer_norm(nc, dve, stats, x, kvq[:, :, 0:D], mean, sd, var_ready, sd_ready, 1).then_inc(out_ready, 1)


def build(nc, a):
    def dram(name, shape):
        return nc.dram_tensor(name, shape, F32).ap()

    adj = dram("adj", [CELLS, 2])
    adj_count = dram("adj_count", [NPAD, COLS])
    adj_weight = dram("adj_weight", [NPAD, COLS])
    key_dram = dram("key_dram", [EPAD])
    dstf_dram = dram("dstf_dram", [EPAD])
    kv_dram = dram("kv_dram", [NPAD, 2 * D])
    q_dram = dram("q_dram", [NPAD, D])
    sums_dram = [dram(f"sums_dram{i}", [ACC_ROWS, ROWW]) for i in range(NACC)]
    build_adjacency(nc, a["src_cols"], a["dst_cols"], a["w_cols"], a["src_flat"], a["dst_flat"], key_dram, dstf_dram, adj)
    with (
        nc.sbuf_tensor("ident", [P, P], F32) as ident,
        nc.sbuf_tensor("x", [P, NT, D], F32) as x,
        nc.sbuf_tensor("w_deg", [P, NT], F32) as w_deg,
        nc.sbuf_tensor("eps", [P, 2], F32) as eps,
    ):
        first_layer(nc, a["x_nm"], adj, adj_count, adj_weight, a["L0_gnn_weight"], a["L0_gnn_bias"], ident, x, w_deg, eps)
        convolutions(nc, adj_count, adj_weight,
                     [a[k] for k in ("L1_gnn_W1", "L1_gnn_W2", "L1_gnn_W3", "L2_gnn_W1", "L2_gnn_W2")],
                     [a[k] for k in ("L1_gnn_b1", "L1_gnn_b2", "L1_gnn_b3")],
                     [a[f"L2_gnn_{k}"] for k in ("b1", "gn1_w", "gn1_b", "gn1_a", "b2", "gn2_w", "gn2_b", "gn2_a")],
                     ident, x, w_deg, eps)
        attention(nc, a["attr_T"], a["src_cols"], a["dst_cols"], dstf_dram, a["we"], a["kvq_w"], a["kvq_b"], kv_dram, q_dram,
                  sums_dram, ident, x, eps, a["out"])


def kernel(**inputs):
    import concourse.bacc as bacc
    from concourse.bass_utils import run_bass_kernel_spmd

    given = {k: np.asarray(v) for k, v in inputs.items()}

    def edge_list(values, fill):
        padded = np.full((EPAD,), fill, values.dtype)
        padded[:E] = values
        return padded

    src, dst, w = edge_list(given["src"], 0), edge_list(given["dst"], N), edge_list(given["edge_weight"], 0)
    attr = np.zeros((D, EPAD), np.float32)
    attr[:, :E] = given["edge_attr_96"].T
    x = np.zeros((NPAD, D), np.float32)
    x[:N] = given["x"]
    arrays = {
        "src_cols": np.ascontiguousarray(src.reshape(ET, P).T),
        "dst_cols": np.ascontiguousarray(dst.reshape(ET, P).T),
        "w_cols": np.ascontiguousarray(w.reshape(ET, P).T),
        "src_flat": src.reshape(P, ET),
        "dst_flat": dst.reshape(P, ET),
        "attr_T": attr,
        "x_nm": np.ascontiguousarray(x.reshape(NT, P, D).transpose(1, 0, 2)),
        "we": np.concatenate([given["L3_gnn_We"], given["L3_gnn_be"][None]]),
        "kvq_w": np.concatenate([given["L3_gnn_Wk"], given["L3_gnn_Wv"], given["L3_gnn_Wq"]], axis=1),
        "kvq_b": np.concatenate([given["L3_gnn_bk"], given["L3_gnn_bv"], given["L3_gnn_bq"]])[None],
    }
    for name, value in given.items():
        if name.startswith(("L0", "L1", "L2")):
            arrays[name] = np.ascontiguousarray(value)
    nc = bacc.Bacc("TRN2", target_bir_lowering=False, num_devices=1)
    aps = {}
    for name, value in arrays.items():
        aps[name] = nc.dram_tensor(f"in_{name}", value.shape, mybir.dt.from_np(value.dtype), kind="ExternalInput").ap()
    aps["out"] = nc.dram_tensor("out_x", (N, D), F32, kind="ExternalOutput").ap()
    build(nc, aps)
    result = run_bass_kernel_spmd(nc, [{f"in_{k}": v for k, v in arrays.items()}], core_ids=[0])
    return result.results[0]["out_x"]
```

```python
from contextlib import ExitStack

import numpy as np

import concourse.bass as bass
from concourse import mybir

F32 = mybir.dt.float32
BF16 = mybir.dt.bfloat16
I32 = mybir.dt.int32
ALU = mybir.AluOpType
ACT = mybir.ActivationFunctionType
AX = mybir.AxisListType

P = 128
N = 3125
D = 96
E = 103125
HEADS = 8
HD = D // HEADS
NT = -(-N // P)
NPAD = NT * P
LAST = N - (NT - 1) * P
COLS = 3136
BANK = 512
NB = -(-N // BANK)
BLOCKS = [(b * BANK, min(N, (b + 1) * BANK)) for b in range(NB)]
HALF = (NB // 2) * BANK
PB = 5

G = 8
NG = -(-E // (P * G))
ET = NG * G
EPAD = ET * P
DUMP = NPAD * COLS
CELLS = DUMP + P * G
Q4 = 4
NQ = ET // Q4
ROWW = D + HEADS
NACC = 2
Q_ROWS = NPAD + P
ACC_ROWS = NPAD + P
LN_EPS = 1e-5
GN_EPS = 1e-5

assert NG % 2 == 1 and NT % 5 == 0 and NQ % 2 == 0 and CELLS < 1 << 24


class Pool:

    def __init__(self, nc, stack):
        self.nc, self.stack = nc, stack

    def sb(self, name, shape, dt=F32):
        return self.stack.enter_context(self.nc.sbuf_tensor(name, shape, dt))

    def ps(self, name, shape):
        return self.stack.enter_context(self.nc.psum_tensor(name, shape, F32))

    def sem(self, name):
        return self.stack.enter_context(self.nc.semaphore(name))


def node_major(psum):
    return psum[:, 0:PB * BANK].rearrange("p (b c) -> p b c", c=BANK)[:, :, 0:PB * D]


def by_bank(tile):
    return tile[:, :, :].rearrange("p (b j) d -> p b (j d)", j=PB)


def node_major_by_node(psum):
    return node_major(psum).rearrange("p b (j d) -> p b j d", d=D)


def by_node(tile):
    return tile[:, :, :].rearrange("p (b j) d -> p b j d", j=PB)


def per_node_in_bank(column):
    return column.rearrange("p (b j) -> p b j", j=PB).unsqueeze(3).broadcast_to((P, NT // PB, PB, D))


def node_cols(t):
    return (t // PB) * BANK + (t % PB) * D


def per_node(column):
    return column.unsqueeze(2).broadcast_to((P, NT, D))


def per_feature(row):
    return row.unsqueeze(1).broadcast_to((P, NT, D))


def build_adjacency(nc, src_i, dst_i, w_cols, src_flat, dst_flat, key_dram, dstf_dram, adj):
    ctx = ExitStack()
    with ctx:
        mem = Pool(nc, ctx)
        zero = mem.sb("zero", [P, COLS])
        w = mem.sb("w", [P, ET])
        rest = mem.sb("rest", [P, ET])
        srcf = mem.sb("srcf", [P, ET])
        dstf = mem.sb("dstf", [P, ET])
        key = mem.sb("key", [P, ET])
        key_off = mem.sb("key_off", [P, ET])
        wv = mem.sb("wv", [P, ET, 5], BF16)
        fsrc_i = mem.sb("fsrc_i", [P, ET], I32)
        fdst_i = mem.sb("fdst_i", [P, ET], I32)
        fsrc = mem.sb("fsrc", [P, ET])
        fdst = mem.sb("fdst", [P, ET])
        fkey = mem.sb("fkey", [P, ET])
        dump_i = mem.sb("dump_i", [P, G], I32)
        dump = mem.sb("dump", [P, G])
        before = mem.sb("before", [P, P], BF16)
        one = mem.sb("one", [P, 1], BF16)
        keyrow = mem.sb("keyrow", [P, 2, G * P])
        SPAN = G * P + P
        eq = mem.sb("eq", [P, 2, G * SPAN], BF16)
        eq_before = mem.sb("eq_before", [P, 2, G, P], BF16)
        first_off = mem.sb("first_off", [P, G])
        cell = [mem.sb(f"cell{s}", [P, G], I32) for s in range(2)]
        pay = [mem.sb(f"pay{s}", [P, G, 2]) for s in range(2)]
        sums = [mem.ps(f"sums{s}", [P, G, 5]) for s in range(2)]

        loaded = mem.sem("loaded")
        zero_ready = mem.sem("zero_ready")
        zeroed = mem.sem("zeroed")
        flat_keys = mem.sem("flat_keys")
        keys_stored = mem.sem("keys_stored")
        consts_ready = mem.sem("consts_ready")
        row_landed = [mem.sem(f"row_landed{s}") for s in range(2)]
        eq_ready = mem.sem("eq_ready")
        sums_ready = mem.sem("sums_ready")
        sums_free = mem.sem("sums_free")
        pay_ready = mem.sem("pay_ready")
        groups_landed = mem.sem("groups_landed")
        cell_landed = [mem.sem(f"cell_landed{k}") for k in range(G)]
        block = ctx.enter_context(nc.Block())

        @block.sync
        def _(sp):
            for tile, source in ((fsrc_i, src_flat), (fdst_i, dst_flat), (w, w_cols)):
                sp.dma_start(tile[:], source).then_inc(loaded, 16)
            sp.wait_ge(flat_keys, 1)
            sp.dma_start(key_dram.rearrange("(p a) -> p a", p=P), fkey[:]).then_inc(keys_stored, 16)
            sp.dma_start(dstf_dram.rearrange("(p a) -> p a", p=P), fdst[:]).then_inc(keys_stored, 16)
            sp.wait_ge(keys_stored, 32)

            def load(g, s):
                keys = key_dram[bass.ds(g * (G * P), G * P)].partition_broadcast(P)
                sp.dma_start(keyrow[:, s, :], keys).then_inc(row_landed[s], 16)

            load(0, 0)
            load(1, 1)
            with sp.Fori(1, NG // 2) as i:
                for s in range(2):
                    sp.wait_ge(eq_ready, 2 * i + s - 1)
                    load(2 * i + s, s)
            sp.wait_ge(eq_ready, NG - 2)
            load(NG - 1, 0)

        @block.scalar
        def _(act):
            act.wait_ge(zero_ready, 1)
            zeros = zero[:, :].unsqueeze(1).broadcast_to((P, 2, COLS))
            rows = adj[0:DUMP, :].rearrange("(t p c) two -> t p (c two)", p=P, c=COLS)
            with act.Fori(0, NT) as t:
                act.dma_start(rows[bass.ds(t, 1)].squeeze(0).rearrange("p (a c) -> p a c", a=2),
                              zeros).then_inc(zeroed, 16)
            act.dma_start(adj[DUMP:CELLS, :].rearrange("(p a) two -> p (a two)", p=P),
                          zero[:, 0:2 * G]).then_inc(zeroed, 16)

        @block.gpsimd
        def _(pool):
            nc.gpsimd.iota(dump_i[:], pattern=[[P, G]], base=DUMP, channel_multiplier=1).then_inc(consts_ready, 1)
            nc.gpsimd.memset(before[:], 1.0)
            pool.drain()
            nc.gpsimd.affine_select(out=before[:], in_=before[:], compare_op=ALU.is_gt, fill=0.0, base=0,
                                    pattern=[[1, P]], channel_multiplier=-1).then_inc(consts_ready, 1)
            pool.wait_ge(zeroed, 16 * (NT + 1))
            last_cell = pool.to_reg(CELLS - 1)

            def scatter(g, s, first=False):
                pool.wait_ge(pay_ready, g + 1)
                if not first:
                    for k in range(G):
                        pool.wait_ge(cell_landed[k], 16 * g)
                pool.sem_inc(groups_landed, 1)
                for k in range(G):
                    nc.gpsimd.indirect_dma_start(
                        out=adj, out_offset=bass.IndirectOffsetOnAxis(ap=cell[s][:, k:k + 1], axis=0),
                        in_=pay[s][:, k, :], in_offset=None, bounds_check=last_cell, oob_is_err=True,
                        compute_op=ALU.add).then_inc(cell_landed[k], 16)

            scatter(0, 0, True)
            with pool.Fori(0, NG // 2) as i:
                scatter(2 * i + 1, 1)
                scatter(2 * i + 2, 0)
            for k in range(G):
                pool.wait_ge(cell_landed[k], 16 * NG)

        @block.tensor
        def _(pe):
            pe.wait_ge(consts_ready, 2)

            def add_equals(g, s):
                pe.wait_ge(eq_ready, g + 1)
                pe.wait_ge(sums_free, g + 1)
                eqs = eq[:, s, :].rearrange("p (k e) -> p k e", e=SPAN)
                flat = eq[:, s, :]
                for i in range(G):
                    out = sums[s][:, i, :]

                    def equals(j):
                        at = j * G * P + i * P
                        return flat[:, at:at + P]

                    def values(j, lo):
                        return wv[:, bass.ds(g * G + j, 1), lo:5].squeeze(1)

                    nc.tensor.matmul(out[:, 0:1], eq_before[:, s, i, :], one[:], start=True, stop=False)
                    nc.tensor.matmul(out[:, 1:5], equals(i), values(i, 1), start=False, stop=False)
                    for n, j in enumerate(j for j in range(G) if j != i):
                        lo = 0 if j < i else 1
                        last = nc.tensor.matmul(out[:, lo:5], equals(j), values(j, lo),
                                                start=False, stop=n == G - 2)
                last.then_inc(sums_ready, 1)

            add_equals(0, 0)
            with pe.Fori(0, NG // 2) as i:
                add_equals(2 * i + 1, 1)
                add_equals(2 * i + 2, 0)

        @block.vector
        def _(dve):
            nc.vector.memset(zero[:], 0.0).then_inc(zero_ready, 1)
            nc.vector.memset(one[:], 1.0)
            nc.vector.memset(wv[:, :, 0:2], 1.0)
            dve.wait_ge(loaded, 48)
            nc.vector.tensor_copy(fsrc[:], fsrc_i[:])
            nc.vector.tensor_copy(fdst[:], fdst_i[:])
            nc.vector.tensor_copy(srcf[:], src_i[:])
            nc.vector.tensor_copy(dstf[:], dst_i[:])
            dve.drain()
            nc.vector.scalar_tensor_tensor(fkey[:], fsrc[:], float(COLS), fdst[:], ALU.mult, ALU.add).then_inc(flat_keys, 1)
            nc.vector.scalar_tensor_tensor(key[:], srcf[:], float(COLS), dstf[:], ALU.mult, ALU.add)
            dve.wait_ge(consts_ready, 2)
            nc.vector.tensor_copy(dump[:], dump_i[:])
            nc.vector.tensor_copy(wv[:, :, 2], w[:])
            dve.drain()
            nc.vector.tensor_tensor(key_off[:].rearrange("p (g k) -> p g k", k=G),
                                    key[:].rearrange("p (g k) -> p g k", k=G),
                                    dump[:].unsqueeze(1).broadcast_to((P, NG, G)), ALU.subtract)
            nc.vector.tensor_tensor(rest[:], w[:], wv[:, :, 2], ALU.subtract)
            dve.drain()
            nc.vector.tensor_copy(wv[:, :, 3], rest[:])
            dve.drain()
            nc.vector.tensor_tensor(w[:], rest[:], wv[:, :, 3], ALU.subtract)
            dve.drain()
            nc.vector.tensor_copy(wv[:, :, 4], w[:])
            dve.sem_inc(sums_free, 2)

            def compare(g, s, use, first=False):
                dve.wait_ge(row_landed[s], 16 * (use + 1))
                if not first:
                    dve.wait_ge(sums_ready, g - 1)
                for k in range(G):
                    nc.vector.tensor_scalar(eq[:, s, k * G * P:(k + 1) * G * P], keyrow[:, s, :],
                                            key[:, bass.ds(g * G + k, 1)], None, ALU.is_equal)
                dve.drain()
                own = eq[:, s, :].rearrange("p (k e) -> p k e", e=SPAN)[:, :, 0:P]
                nc.vector.tensor_tensor(eq_before[:, s, :, :], own,
                                        before[:].unsqueeze(1).broadcast_to((P, G, P)),
                                        ALU.mult).then_inc(eq_ready, 1)

            def finish(g, s, first=False):
                dve.wait_ge(sums_ready, g + 1)
                if not first:
                    dve.wait_ge(groups_landed, g)
                nc.vector.tensor_copy(pay[s][:, :, 0], sums[s][:, :, 1])
                nc.vector.reduce_sum(pay[s][:, :, 1], sums[s][:, :, 2:5], axis=AX.X)
                nc.vector.scalar_tensor_tensor(first_off[:], sums[s][:, :, 0], 0.5,
                                               key_off[:, bass.ds(g * G, G)], ALU.is_lt,
                                               ALU.mult).then_inc(sums_free, 1)
                dve.drain()
                nc.vector.tensor_tensor(cell[s][:], first_off[:], dump[:], ALU.add).then_inc(pay_ready, 1)
                dve.drain()

            compare(0, 0, 0, True)
            compare(1, 1, 0, True)
            finish(0, 0, True)
            with dve.Fori(0, NG // 2 - 1) as i:
                compare(2 * i + 2, 0, i + 1)
                finish(2 * i + 1, 1)
                compare(2 * i + 3, 1, i + 1)
                finish(2 * i + 2, 0)
            compare(NG - 1, 0, NG // 2)
            finish(NG - 2, 1)
            finish(NG - 1, 0)


def layer_norm_stats(nc, dve, act_mem, x, mean, sd, var_ready, sd_ready, n):
    st, dif, var = act_mem
    with dve.Fori(0, NT // 5) as i:
        for j in range(5):
            nc.vector.bn_stats(st[:, bass.ds(5 * i + j, 1), :].squeeze(1), x[:, bass.ds(5 * i + j, 1), :].squeeze(1))
    dve.drain()
    nc.vector.tensor_tensor(mean[:], st[:, :, 1], st[:, :, 4], ALU.add)
    nc.vector.tensor_tensor(dif[:], st[:, :, 1], st[:, :, 4], ALU.subtract)
    nc.vector.tensor_tensor(var[:], st[:, :, 2], st[:, :, 5], ALU.add)
    dve.drain()
    nc.vector.tensor_scalar(mean[:], mean[:], 0.5, None, ALU.mult)
    nc.vector.tensor_tensor(dif[:], dif[:], dif[:], ALU.mult)
    nc.vector.tensor_scalar(var[:], var[:], 1.0 / D, None, ALU.mult)
    dve.drain()
    nc.vector.scalar_tensor_tensor(var[:], dif[:], 0.25, var[:], ALU.mult, ALU.add).then_inc(var_ready, 1)
    dve.wait_ge(sd_ready, n)
    nc.vector.reciprocal(sd[:], sd[:])
    dve.drain()


def layer_norm(nc, dve, act_mem, x, out, mean, sd, var_ready, sd_ready, n):
    layer_norm_stats(nc, dve, act_mem, x, mean, sd, var_ready, sd_ready, n)
    nc.vector.tensor_tensor(x[:], x[:], per_node(mean[:]), ALU.subtract)
    dve.drain()
    return nc.vector.tensor_tensor(out[:], x[:], per_node(sd[:]), ALU.mult)


def first_layer(nc, x_nm, adj, adj_count, adj_weight, ws, biases, ident, x, w_deg, eps):
    ctx = ExitStack()
    with ctx:
        mem = Pool(nc, ctx)
        pair = mem.sb("pair", [P, 2, COLS, 2])
        count = mem.sb("count", [P, 2, COLS])
        weight = mem.sb("weight", [P, 2, COLS])
        xT = mem.sb("xT", [D, NPAD])
        agg = mem.sb("agg", [P, NPAD])
        xw = mem.sb("xw", [P, NT, D])
        w0 = mem.sb("w0", [D, D])
        bias = mem.sb("bias0", [P, D])
        lhs = [mem.sb(f"lhs{s}", [P, D + 2]) for s in range(2)]
        lhs_w = mem.sb("lhs_w", [P, D + 2])
        odeg = [mem.sb(f"odeg{s}", [P, 1]) for s in range(2)]
        osd = [mem.sb(f"osd{s}", [P, 1]) for s in range(2)]
        degs = mem.sb("degs", [P, NT, 2])
        has_in = mem.sb("has_in", [P, NT])
        no_in = mem.sb("no_in", [P, NT])
        cj = mem.sb("cj", [P, NT])
        stats = (mem.sb("st", [P, NT, 6]), mem.sb("dif", [P, NT]), mem.sb("var", [P, NT]))
        mean = mem.sb("mean", [P, NT])
        sd = mem.sb("sd", [P, NT])
        acc = mem.ps("acc", [P, NB * BANK])
        small = mem.ps("small", [P, NT, 2])

        loaded = mem.sem("loaded")
        set_up = mem.sem("set_up")
        ident_ready = mem.sem("ident_ready")
        pair_landed = [mem.sem(f"pair_landed{s}") for s in range(2)]
        stored = [mem.sem(f"stored{s}") for s in range(2)]
        counts_ready = mem.sem("counts_ready")
        weights_ready = mem.sem("weights_ready")
        odeg_ready = mem.sem("odeg_ready")
        osd_ready = mem.sem("osd_ready")
        lhs_ready = mem.sem("lhs_ready")
        tiles_done = mem.sem("tiles_done")
        xT_ps = mem.sem("xT_ps")
        xT_ready = mem.sem("xT_ready")
        xw_ps = mem.sem("xw_ps")
        xw_ready = mem.sem("xw_ready")
        agg_ready = mem.sem("agg_ready")
        deg_ps = mem.sem("deg_ps")
        cj_max = mem.sem("cj_max")
        cj_sqrt = mem.sem("cj_sqrt")
        out_ps = mem.sem("out_ps")
        var_ready = mem.sem("var_ready")
        sd_ready = mem.sem("sd_ready")
        block = ctx.enter_context(nc.Block())
        rows = adj[0:DUMP, :].rearrange("(t p c) two -> t p c two", p=P, c=COLS)
        count_rows = adj_count.rearrange("(t p) c -> t p c", p=P)
        weight_rows = adj_weight.rearrange("(t p) c -> t p c", p=P)

        @block.sync
        def _(sp):
            sp.dma_start(x[:], x_nm).then_inc(loaded, 16)
            sp.dma_start(w0[:], ws).then_inc(loaded, 16)
            sp.dma_start(bias[:], biases.partition_broadcast(P)).then_inc(loaded, 16)

            def load(t, s):
                sp.dma_start(pair[:, s], rows[bass.ds(t, 1)].squeeze(0)).then_inc(pair_landed[s], 16)

            def store(t, s):
                sp.wait_ge(counts_ready, t + 1)
                sp.dma_start(count_rows[bass.ds(t, 1)].squeeze(0), count[:, s]).then_inc(stored[s], 16)
                sp.wait_ge(weights_ready, t + 1)
                sp.dma_start(weight_rows[bass.ds(t, 1)].squeeze(0), weight[:, s]).then_inc(stored[s], 16)

            load(0, 0)
            load(1, 1)
            with sp.Fori(0, NT // 2 - 1) as i:
                for s in range(2):
                    store(2 * i + s, s)
                    load(2 * i + s + 2, s)
            store(NT - 3, 0)
            load(NT - 1, 0)
            store(NT - 2, 1)
            store(NT - 1, 0)
            sp.wait_ge(stored[0], 32 * (NT // 2 + 1))
            sp.wait_ge(stored[1], 32 * (NT // 2))

        @block.gpsimd
        def _(pool):
            nc.gpsimd.memset(ident[:], 0.0)
            pool.drain()
            nc.gpsimd.affine_select(out=ident[:], in_=ident[:], compare_op=ALU.not_equal, fill=1.0, base=0,
                                    pattern=[[-1, P]], channel_multiplier=1).then_inc(ident_ready, 1)

        @block.scalar
        def _(act):
            act.wait_ge(set_up, 1)
            act.wait_ge(xT_ps, 1)
            nc.scalar.copy(xT[:], acc[0:D, 0:NPAD]).then_inc(xT_ready, 1)

            def split(t, s, use, first=False):
                act.wait_ge(pair_landed[s], 16 * (use + 1))
                if not first:
                    act.wait_ge(stored[s], 32 * use)
                    act.wait_ge(tiles_done, t - 1)
                nc.scalar.activation(count[:, s, :], pair[:, s, :, 0], ACT.Copy).then_inc(counts_ready, 1)
                act.wait_ge(odeg_ready, t + 1)
                nc.scalar.activation(osd[s][:], odeg[s][:], ACT.Sqrt).then_inc(osd_ready, 1)

            split(0, 0, 0, True)
            split(1, 1, 0, True)
            with act.Fori(1, NT // 2) as i:
                for s in range(2):
                    split(2 * i + s, s, i)
            split(NT - 1, 0, NT // 2)

            act.wait_ge(tiles_done, NT)
            nc.scalar.copy(agg[0:D + 2, 0:HALF], acc[0:D + 2, 0:HALF]).then_inc(agg_ready, 1)
            act.wait_ge(cj_max, 1)
            nc.scalar.activation(cj[:], cj[:], ACT.Sqrt).then_inc(cj_sqrt, 1)
            act.wait_ge(var_ready, 1)
            nc.scalar.activation(sd[:], stats[2][:], ACT.Sqrt, bias=eps[:, 0:1]).then_inc(sd_ready, 1)

        @block.tensor
        def _(pe):
            pe.wait_ge(loaded, 48)
            pe.wait_ge(ident_ready, 1)
            for t in range(NT):
                last = nc.tensor.transpose(acc[0:D, t * P:(t + 1) * P], x[:, t, :], ident[:])
            last.then_inc(xT_ps, 1)
            pe.wait_ge(xT_ready, 1)
            for t in range(NT):
                at = node_cols(t)
                last = nc.tensor.matmul(acc[:, at:at + D], xT[:, t * P:(t + 1) * P], w0[:], start=True, stop=True)
            last.then_inc(xw_ps, 1)
            pe.wait_ge(xw_ready, 1)

            def multiply(t, s, first=False, ends=False):
                pe.wait_ge(lhs_ready, t + 1)
                pe.wait_ge(counts_ready, t + 1)
                pe.wait_ge(weights_ready, t + 1)
                for lo, hi in BLOCKS:
                    nc.tensor.matmul(acc[0:D + 2, lo:hi], lhs[s][:], count[:, s, lo:hi], start=first, stop=False)
                for lo, hi in BLOCKS:
                    last = nc.tensor.matmul(acc[0:D + 2, lo:hi], lhs_w[:], weight[:, s, lo:hi], start=False, stop=ends)
                last.then_inc(tiles_done, 1)

            multiply(0, 0, True)
            multiply(1, 1)
            with pe.Fori(1, NT // 2) as i:
                for s in range(2):
                    multiply(2 * i + s, s)
            multiply(NT - 1, 0, ends=True)

            pe.wait_ge(agg_ready, 2)
            for t in range(NT):
                last = nc.tensor.matmul(small[:, t, :], agg[D:D + 2, t * P:(t + 1) * P], ident[D:D + 2, D:D + 2],
                                        start=True, stop=True)
            last.then_inc(deg_ps, 1)
            for t in range(NT):
                at = node_cols(t)
                last = nc.tensor.matmul(acc[:, at:at + D], agg[0:D, t * P:(t + 1) * P], w0[:], start=True, stop=True)
            last.then_inc(out_ps, 1)

        @block.vector
        def _(dve):
            nc.vector.memset(eps[:, 0:1], LN_EPS)
            nc.vector.memset(agg[0:D + 2, N:NPAD], 0.0)
            for s in range(2):
                nc.vector.memset(lhs[s][:, D:D + 1], 1.0)
                nc.vector.memset(lhs[s][:, D + 1:D + 2], 0.0)
            nc.vector.memset(lhs_w[:, 0:D + 1], 0.0)
            nc.vector.memset(lhs_w[:, D + 1:D + 2], 1.0).then_inc(set_up, 1)
            dve.wait_ge(loaded, 48)
            dve.wait_ge(xw_ps, 1)
            nc.vector.tensor_copy(by_bank(xw), node_major(acc)).then_inc(xw_ready, 1)

            def scale(t, s, use, first=False):
                dve.wait_ge(pair_landed[s], 16 * (use + 1))
                if not first:
                    dve.wait_ge(stored[s], 32 * use)
                    dve.wait_ge(tiles_done, t - 1)
                nc.vector.tensor_copy(weight[:, s, :], pair[:, s, :, 1]).then_inc(weights_ready, 1)
                dve.wait_ge(counts_ready, t + 1)
                nc.vector.reduce_sum(odeg[s][:], count[:, s, 0:N], axis=AX.X)
                dve.drain()
                nc.vector.tensor_scalar(odeg[s][:], odeg[s][:], 1.0, None, ALU.max).then_inc(odeg_ready, 1)
                dve.wait_ge(osd_ready, t + 1)
                nc.vector.reciprocal(osd[s][:], osd[s][:])
                dve.drain()
                nc.vector.tensor_scalar(lhs[s][:, 0:D], x[:, bass.ds(t, 1), :].squeeze(1), osd[s][:], None,
                                        ALU.mult).then_inc(lhs_ready, 1)

            scale(0, 0, 0, True)
            scale(1, 1, 0, True)
            with dve.Fori(1, NT // 2) as i:
                for s in range(2):
                    scale(2 * i + s, s, i)
            scale(NT - 1, 0, NT // 2)

            dve.wait_ge(tiles_done, NT)
            nc.vector.tensor_copy(agg[0:D + 2, HALF:N], acc[0:D + 2, HALF:N]).then_inc(agg_ready, 1)
            dve.wait_ge(deg_ps, 1)
            nc.vector.tensor_copy(degs[:], small[:])
            dve.drain()
            nc.vector.tensor_copy(w_deg[:], degs[:, :, 1])
            nc.vector.tensor_scalar(has_in[:], degs[:, :, 0], 0.0, None, ALU.is_gt)
            nc.vector.tensor_scalar(no_in[:], degs[:, :, 0], 0.0, None, ALU.is_le)
            nc.vector.tensor_scalar(cj[:], degs[:, :, 0], 1.0, None, ALU.max).then_inc(cj_max, 1)
            dve.drain()
            nc.vector.tensor_tensor(xw[:], xw[:], per_node(no_in[:]), ALU.mult)
            dve.drain()
            nc.vector.tensor_tensor(xw[:], xw[:], per_feature(bias[:]), ALU.add)
            dve.drain()
            nc.vector.tensor_tensor(x[:], xw[:], x[:], ALU.add)
            dve.wait_ge(cj_sqrt, 1)
            nc.vector.reciprocal(cj[:], cj[:])
            dve.drain()
            nc.vector.tensor_tensor(cj[:], cj[:], has_in[:], ALU.mult)
            dve.drain()
            dve.wait_ge(out_ps, 1)
            nc.vector.tensor_copy(by_bank(xw), node_major(acc))
            dve.drain()
            nc.vector.tensor_tensor(xw[:], xw[:], per_node(cj[:]), ALU.mult)
            dve.drain()
            nc.vector.tensor_tensor(xw[:], xw[:], x[:], ALU.add)
            dve.drain()
            layer_norm(nc, dve, stats, xw, x, mean, sd, var_ready, sd_ready, 1)
            dve.drain()


def convolutions(nc, adj_count, adj_weight, weights, rows, columns, ident, x, w_deg, eps):
    W_PASSES, C_PASSES = 3, 2
    SLOTS = 5
    ctx = ExitStack()
    with ctx:
        mem = Pool(nc, ctx)
        table = mem.sb("table", [P, SLOTS, COLS])
        g = mem.sb("g", [P, NT, D])
        tmp = mem.sb("tmp", [P, NT, D])
        agg = mem.sb("agg2", [D, NPAD])
        xT = mem.sb("xT2", [D, NPAD])
        lhs = [mem.sb(f"clhs{j}", [P, D]) for j in range(SLOTS)]
        wsb = [mem.sb(f"cw{k}", [D, D]) for k in range(W_PASSES + C_PASSES)]
        bias_row = [mem.sb(f"cb{k}", [P, D]) for k in range(W_PASSES)]
        cols = mem.sb("cols", [D, 8])
        zero = mem.sb("zero2", [P, BANK], BF16)
        dis = mem.sb("dis", [P, NT])
        pos = mem.sb("pos", [P, NT])
        stats = (mem.sb("st2", [P, NT, 6]), mem.sb("dif2", [P, NT]), mem.sb("var2", [P, NT]))
        mean = mem.sb("mean2", [P, NT])
        sd = mem.sb("sd2", [P, NT])
        gst = mem.sb("gst", [D, NB, 6])
        gmv = mem.sb("gmv", [D, 2])
        gs = mem.sb("gs", [D, 8])
        acc = mem.ps("acc2", [P, NB * BANK])

        loaded = mem.sem("loaded")
        set_up = mem.sem("set_up")
        dis_max = mem.sem("dis_max")
        dis_sqrt = mem.sem("dis_sqrt")
        table_landed = [mem.sem(f"table_landed{j}") for j in range(SLOTS)]
        g_ready = mem.sem("g_ready")
        lhs_ready = mem.sem("lhs_ready")
        tiles_done = mem.sem("tiles_done")
        sums_ready = mem.sem("sums_ready")
        agg_ready = mem.sem("agg_ready")
        product_ps = mem.sem("product_ps")
        product_read = mem.sem("product_read")
        gvar_ready = mem.sem("gvar_ready")
        gsd_ready = mem.sem("gsd_ready")
        gscale_ready = mem.sem("gscale_ready")
        relu_ready = mem.sem("relu_ready")
        hT_ready = mem.sem("hT_ready")
        turned_ps = mem.sem("turned_ps")
        turned_read = mem.sem("turned_read")
        var_ready = mem.sem("var_ready")
        sd_ready = mem.sem("sd_ready")
        block = ctx.enter_context(nc.Block())
        PASSES = W_PASSES + C_PASSES
        tables = [adj_weight] * W_PASSES + [adj_count] * C_PASSES

        @block.sync
        def _(sp):
            for k in range(PASSES):
                sp.dma_start(wsb[k][:], weights[k]).then_inc(loaded, 16)
            for k in range(W_PASSES):
                sp.dma_start(bias_row[k][:], rows[k].partition_broadcast(P)).then_inc(loaded, 16)
            for k in range(8):
                sp.dma_start(cols[:, k:k + 1], columns[k].unsqueeze(1)).then_inc(loaded, 16)

            def load(k, i, j):
                tile = tables[k].rearrange("(t p) c -> t p c", p=P)[bass.ds(SLOTS * i + j, 1)].squeeze(0)
                sp.dma_start(table[:, j, 0:N], tile[:, 0:N]).then_inc(table_landed[j], 16)

            for j in range(SLOTS):
                load(0, 0, j)
            for k in range(PASSES):
                with sp.Fori(1 if k == 0 else 0, NT // SLOTS) as i:
                    for j in range(SLOTS):
                        sp.wait_ge(tiles_done, k * NT + SLOTS * i + j - SLOTS + 1)
                        load(k, i, j)

        @block.scalar
        def _(act):
            act.wait_ge(dis_max, 1)
            nc.scalar.activation(dis[:], dis[:], ACT.Sqrt).then_inc(dis_sqrt, 1)

            for k in range(PASSES):
                act.wait_ge(g_ready, k + 1)

                def hand_over(i):
                    for j in range(SLOTS):
                        if not (k == 0 and isinstance(i, int)):
                            act.wait_ge(tiles_done, k * NT + SLOTS * i + j - SLOTS + 1)
                        nc.scalar.copy(lhs[j][:], g[:, bass.ds(SLOTS * i + j, 1), :].squeeze(1)).then_inc(lhs_ready, 1)

                hand_over(0)
                with act.Fori(1, NT // SLOTS) as i:
                    hand_over(i)
                act.wait_ge(sums_ready, k + 1)
                nc.scalar.copy(agg[:, 0:HALF], acc[0:D, 0:HALF]).then_inc(agg_ready, 1)
                if k >= W_PASSES:
                    n = k - W_PASSES
                    act.wait_ge(gvar_ready, n + 1)
                    nc.scalar.activation(gs[:, 1:2], gs[:, 0:1], ACT.Sqrt, bias=eps[0:D, 1:2]).then_inc(gsd_ready, 1)
                    act.wait_ge(gscale_ready, n + 1)
                    nc.scalar.activation(agg[:, 0:N], acc[0:D, 0:N], ACT.Relu, bias=gs[:, 4:5],
                                         scale=gs[:, 3:4]).then_inc(relu_ready, 1)
                if k in (W_PASSES - 1, PASSES - 1):
                    act.wait_ge(var_ready, 1 if k < W_PASSES else 2)
                    nc.scalar.activation(sd[:], stats[2][:], ACT.Sqrt, bias=eps[:, 0:1]).then_inc(sd_ready, 1)

        @block.tensor
        def _(pe):
            pe.wait_ge(loaded, 16 * (PASSES + W_PASSES + 8))
            pe.wait_ge(set_up, 1)
            products = turns = 0
            for k in range(PASSES):
                if products:
                    pe.wait_ge(product_read, min(products, W_PASSES))
                if turns:
                    pe.wait_ge(turned_read, turns)
                for lo, hi in BLOCKS:
                    nc.tensor.matmul(acc[0:D, lo:hi], zero[:, 0:D], zero[:, 0:hi - lo], start=True, stop=False)
                with pe.Fori(0, NT // SLOTS) as i:
                    for j in range(SLOTS):
                        pe.wait_ge(table_landed[j], 16 * (k * (NT // SLOTS) + i + 1))
                        pe.wait_ge(lhs_ready, k * NT + SLOTS * i + j + 1)
                        for lo, hi in BLOCKS:
                            last = nc.tensor.matmul(acc[0:D, lo:hi], lhs[j][:], table[:, j, lo:hi], start=False, stop=False)
                        last.then_inc(tiles_done, 1)
                if k < W_PASSES:
                    for t in range(NT):
                        n = min(P, N - t * P)
                        ends = (t + 1) * P % BANK == 0 or t == NT - 1
                        last = nc.tensor.matmul(acc[0:D, t * P:t * P + n], g[:, t, :], ident[:, 0:n], start=False, stop=ends)
                    last.then_inc(sums_ready, 1)
                else:
                    for lo, hi in BLOCKS:
                        last = nc.tensor.matmul(acc[0:D, lo:hi], zero[:, 0:D], zero[:, 0:hi - lo], start=False, stop=True)
                    last.then_inc(sums_ready, 1)
                pe.wait_ge(agg_ready, 2 * (k + 1))
                products += 1
                if k < W_PASSES:
                    for t in range(NT):
                        at = node_cols(t)
                        last = nc.tensor.matmul(acc[:, at:at + D], agg[:, t * P:(t + 1) * P], wsb[k][:], start=True, stop=True)
                    last.then_inc(product_ps, 1)
                else:
                    for lo, hi in BLOCKS:
                        last = nc.tensor.matmul(acc[0:D, lo:hi], wsb[k][:], agg[:, lo:hi], start=True, stop=True)
                    last.then_inc(product_ps, 1)
                if k == W_PASSES - 1:
                    pe.wait_ge(g_ready, k + 2)
                    pe.wait_ge(product_read, products)
                    for t in range(NT):
                        last = nc.tensor.transpose(acc[0:D, t * P:(t + 1) * P], x[:, t, :], ident[:])
                    last.then_inc(turned_ps, 1)
                    turns += 1
                if k >= W_PASSES:
                    pe.wait_ge(hT_ready, k - W_PASSES + 1)
                    for t in range(NT):
                        at = node_cols(t)
                        last = nc.tensor.transpose(acc[:, at:at + D], agg[:, t * P:(t + 1) * P], ident[0:D, 0:D])
                    last.then_inc(turned_ps, 1)
                    turns += 1

        @block.vector
        def _(dve):
            nc.vector.memset(zero[:], 0.0)
            nc.vector.memset(eps[:, 1:2], GN_EPS)
            nc.vector.memset(agg[:, N:NPAD], 0.0)
            nc.vector.tensor_scalar(w_deg[:], w_deg[:], 1.0, None, ALU.add)
            dve.drain()
            nc.vector.tensor_scalar(pos[:], w_deg[:], 0.0, None, ALU.is_gt)
            nc.vector.tensor_scalar(dis[:], w_deg[:], 1e-30, None, ALU.max).then_inc(dis_max, 1)
            dve.drain()
            dve.sem_inc(set_up, 1)
            dve.wait_ge(dis_sqrt, 1)
            nc.vector.reciprocal(dis[:], dis[:])
            dve.drain()
            nc.vector.tensor_tensor(dis[:], dis[:], pos[:], ALU.mult)
            dve.drain()
            nc.vector.tensor_tensor(g[:], x[:], per_node(dis[:]), ALU.mult).then_inc(g_ready, 1)
            dve.wait_ge(loaded, 16 * (PASSES + W_PASSES + 8))

            for k in range(PASSES):
                dve.wait_ge(sums_ready, k + 1)
                nc.vector.tensor_copy(agg[:, HALF:N], acc[0:D, HALF:N]).then_inc(agg_ready, 1)
                dve.wait_ge(product_ps, k + 1)
                if k < W_PASSES:
                    nc.vector.tensor_tensor(by_node(tmp), node_major_by_node(acc), per_node_in_bank(dis[:]),
                                            ALU.mult).then_inc(product_read, 1)
                    dve.drain()
                    nc.vector.tensor_tensor(tmp[:], tmp[:], per_feature(bias_row[k][:]), ALU.add)
                    dve.drain()
                    if k < W_PASSES - 1:
                        nc.vector.scalar_tensor_tensor(g[:], tmp[:], 0.0, per_node(dis[:]), ALU.max,
                                                       ALU.mult).then_inc(g_ready, 1)
                    else:
                        nc.vector.tensor_tensor(tmp[:], tmp[:], x[:], ALU.add)
                        dve.drain()
                        layer_norm(nc, dve, stats, tmp, x, mean, sd, var_ready, sd_ready, 1)
                        dve.drain()
                        nc.vector.tensor_copy(g[:], x[:]).then_inc(g_ready, 1)
                        dve.wait_ge(turned_ps, 1)
                        nc.vector.tensor_copy(xT[:], acc[0:D, 0:NPAD]).then_inc(turned_read, 1)
                        dve.drain()
                    continue
                n = k - W_PASSES
                b, gw, gb, ga = (cols[:, 4 * n + c:4 * n + c + 1] for c in range(4))
                for c, (lo, hi) in enumerate(BLOCKS):
                    nc.vector.bn_stats(gst[:, c, :], acc[0:D, lo:hi])
                dve.drain()
                nc.vector.bn_aggr(gmv[:], gst[:].rearrange("p c s -> p (c s)"))
                dve.drain()
                nc.vector.tensor_tensor(gs[:, 5:6], gmv[:, 0:1], b, ALU.add)
                dve.drain()
                nc.vector.tensor_tensor(gs[:, 6:7], gs[:, 5:6], ga, ALU.mult)
                dve.drain()
                nc.vector.tensor_tensor(gs[:, 7:8], gs[:, 5:6], gs[:, 6:7], ALU.subtract)
                dve.drain()
                nc.vector.tensor_tensor(gs[:, 7:8], gs[:, 7:8], gs[:, 7:8], ALU.mult)
                dve.drain()
                nc.vector.tensor_tensor(gs[:, 0:1], gs[:, 7:8], gmv[:, 1:2], ALU.add).then_inc(gvar_ready, 1)
                dve.wait_ge(gsd_ready, n + 1)
                nc.vector.reciprocal(gs[:, 2:3], gs[:, 1:2])
                dve.drain()
                nc.vector.tensor_tensor(gs[:, 3:4], gs[:, 2:3], gw, ALU.mult)
                nc.vector.tensor_tensor(gs[:, 4:5], b, gs[:, 6:7], ALU.subtract)
                dve.drain()
                nc.vector.tensor_tensor(gs[:, 4:5], gs[:, 4:5], gs[:, 3:4], ALU.mult)
                dve.drain()
                nc.vector.tensor_tensor(gs[:, 4:5], gs[:, 4:5], gb, ALU.add).then_inc(gscale_ready, 1)
                dve.wait_ge(relu_ready, n + 1)
                nc.vector.tensor_tensor(agg[:, 0:N], agg[:, 0:N], xT[:, 0:N], ALU.add).then_inc(hT_ready, 1)
                dve.drain()
                if n == 0:
                    nc.vector.tensor_copy(xT[:, 0:N], agg[:, 0:N])
                    dve.wait_ge(turned_ps, 2)
                    nc.vector.tensor_copy(by_bank(g), node_major(acc)).then_inc(turned_read, 1)
                    dve.drain()
                    dve.sem_inc(g_ready, 1)
                else:
                    dve.wait_ge(turned_ps, 3)
                    nc.vector.tensor_copy(by_bank(tmp), node_major(acc)).then_inc(turned_read, 1)
                    dve.drain()
                    nc.vector.tensor_tensor(tmp[:], tmp[:], x[:], ALU.add)
                    dve.drain()
                    layer_norm(nc, dve, stats, tmp, x, mean, sd, var_ready, sd_ready, 2)
                    dve.drain()


def find_windows(nc, src_i, dst_i, dst_cols, src_cols, rel, node_in_window, first_node, windowed):
    ctx = ExitStack()
    with ctx:
        mem = Pool(nc, ctx)
        dstf = mem.sb("wdstf", [P, ET])
        lane_i = mem.sb("lane_i", [P, 1], I32)
        lane = mem.sb("lane", [P, 1])
        ones = mem.sb("wones", [P, P])
        base = mem.sb("wbase", [P, NQ])
        extreme = mem.sb("extreme", [P, 2])
        outside = mem.sb("outside", [P, 2])
        ps_base = mem.ps("ps_base", [P, NQ])
        ps_out = mem.ps("ps_out", [1, 2])
        loaded = mem.sem("loaded")
        lane_ready = mem.sem("lane_ready")
        dst_ready = mem.sem("dst_ready")
        base_ps = mem.sem("base_ps")
        outside_ready = mem.sem("outside_ready")
        out_ps = mem.sem("out_ps")
        block = ctx.enter_context(nc.Block())

        @block.sync
        def _(sp):
            sp.dma_start(dst_i[:], dst_cols).then_inc(loaded, 16)
            sp.dma_start(src_i[:], src_cols).then_inc(loaded, 16)

        @block.gpsimd
        def _(pool):
            nc.gpsimd.iota(lane_i[:], pattern=[[1, 1]], base=0, channel_multiplier=1).then_inc(lane_ready, 1)

        @block.tensor
        def _(pe):
            pe.wait_ge(dst_ready, 1)
            nc.tensor.matmul(ps_base[:], ones[0:1, :], dstf[0:1, :].rearrange("p (q k) -> p q k", k=Q4)[:, :, 0],
                             start=True, stop=True).then_inc(base_ps, 1)
            pe.wait_ge(outside_ready, 1)
            nc.tensor.matmul(ps_out[:], ones[:, 0:1], outside[:], start=True, stop=True).then_inc(out_ps, 1)

        @block.vector
        def _(dve):
            nc.vector.memset(ones[:], 1.0)
            dve.wait_ge(loaded, 32)
            nc.vector.tensor_copy(dstf[:], dst_i[:]).then_inc(dst_ready, 1)
            dve.wait_ge(lane_ready, 1)
            nc.vector.tensor_copy(lane[:], lane_i[:])
            dve.wait_ge(base_ps, 1)
            nc.vector.tensor_copy(base[:], ps_base[:])
            nc.vector.tensor_copy(first_node[:], ps_base[0:1, :])
            dve.drain()
            nc.vector.tensor_scalar(node_in_window[:], base[:], lane[:], None, ALU.add)
            nc.vector.tensor_tensor(rel[:].rearrange("p (q k) -> p q k", k=Q4), dstf[:].rearrange("p (q k) -> p q k", k=Q4),
                                    base[:].unsqueeze(2).broadcast_to((P, NQ, Q4)), ALU.subtract)
            dve.drain()
            nc.vector.tensor_reduce(extreme[:, 0:1], rel[:], AX.X, ALU.min)
            nc.vector.tensor_reduce(extreme[:, 1:2], rel[:], AX.X, ALU.max)
            dve.drain()
            nc.vector.tensor_scalar(outside[:, 0:1], extreme[:, 0:1], 0.0, None, ALU.is_lt)
            nc.vector.tensor_scalar(outside[:, 1:2], extreme[:, 1:2], P - 1.0, None, ALU.is_gt).then_inc(outside_ready, 1)
            dve.wait_ge(out_ps, 1)
            nc.vector.reduce_sum(extreme[0:1, 0:1], ps_out[:], axis=AX.X)
            dve.drain()
            nc.vector.tensor_scalar(windowed[:], extreme[0:1, 0:1], 0.5, None, ALU.is_lt)


def attention_tables(nc, kvq_w, kvq_b, kv_dram, q_dram, ident, x):
    ctx = ExitStack()
    with ctx:
        mem = Pool(nc, ctx)
        xT = mem.sb("axT", [D + 1, NPAD])
        wkvq = mem.sb("awkvq", [D + 1, 3 * D])
        kvq = mem.sb("akvq", [P, NT, 3 * D])
        zero = mem.sb("tzero", [P, D])
        acc = mem.ps("acc3", [P, 4 * BANK])
        loaded = mem.sem("loaded")
        ones_ready = mem.sem("ones_ready")
        xT_ps = mem.sem("xT_ps")
        xT_ready = mem.sem("xT_ready")
        kvq_ps = mem.sem("kvq_ps")
        kvq_read = [mem.sem("kvq_read_act"), mem.sem("kvq_read_dve")]
        tables_stored = mem.sem("tables_stored")
        block = ctx.enter_context(nc.Block())
        H = 4 * BANK // P

        @block.sync
        def _(sp):
            sp.dma_start(wkvq[0:D, :], kvq_w).then_inc(loaded, 16)
            sp.dma_start(wkvq[D:D + 1, :], kvq_b).then_inc(loaded, 16)
            sp.wait_ge(ones_ready, 1)
            sp.dma_start(q_dram[NPAD:Q_ROWS, :], zero[:]).then_inc(tables_stored, 16)
            sp.wait_ge(kvq_read[0], NT // 2 + 1)
            sp.wait_ge(kvq_read[1], NT // 2)
            sp.dma_start(kv_dram.rearrange("(t p) c -> p t c", p=P), kvq[:, :, 0:2 * D]).then_inc(tables_stored, 16)
            sp.dma_start(q_dram[0:NPAD, :].rearrange("(t p) c -> p t c", p=P), kvq[:, :, 2 * D:3 * D]).then_inc(tables_stored, 16)
            sp.wait_ge(tables_stored, 48)

        @block.scalar
        def _(act):
            act.wait_ge(xT_ps, 1)
            nc.scalar.copy(xT[0:D, 0:H * P], acc[0:D, 0:H * P]).then_inc(xT_ready, 1)
            act.wait_ge(xT_ps, 2)
            nc.scalar.copy(xT[0:D, H * P:NPAD], acc[0:D, 0:NPAD - H * P]).then_inc(xT_ready, 1)
            for t in range(0, NT, 2):
                act.wait_ge(kvq_ps, t + 1)
                at = (t % 4) * BANK
                nc.scalar.copy(kvq[:, t, :], acc[:, at:at + 3 * D]).then_inc(kvq_read[0], 1)

        @block.tensor
        def _(pe):
            for t in range(NT):
                if t == H:
                    last.then_inc(xT_ps, 1)
                    pe.wait_ge(xT_ready, 1)
                at = t % H * P
                last = nc.tensor.transpose(acc[0:D, at:at + P], x[:, t, :], ident[:])
            last.then_inc(xT_ps, 1)
            pe.wait_ge(xT_ready, 2)
            pe.wait_ge(ones_ready, 1)
            pe.wait_ge(loaded, 32)
            for t in range(NT):
                if t >= 4:
                    pe.wait_ge(kvq_read[t % 2], t // 2 - 1)
                at = (t % 4) * BANK
                nc.tensor.matmul(acc[:, at:at + 3 * D], xT[:, t * P:(t + 1) * P], wkvq[:], start=True, stop=True).then_inc(kvq_ps, 1)

        @block.vector
        def _(dve):
            nc.vector.memset(zero[:], 0.0)
            nc.vector.memset(xT[D:D + 1, :], 1.0).then_inc(ones_ready, 1)
            for t in range(1, NT, 2):
                dve.wait_ge(kvq_ps, t + 1)
                at = (t % 4) * BANK
                nc.vector.tensor_copy(kvq[:, t, :], acc[:, at:at + 3 * D]).then_inc(kvq_read[1], 1)


def attention_windowed(nc, attr_T, we, src_i, rel, node_in_window, first_node, dstf_dram, kv_dram, q_dram, ident, total):
    ctx = ExitStack()
    with ctx:
        mem = Pool(nc, ctx)
        iota_i = mem.sb("viota_i", [P, P], I32)
        iota = mem.sb("viota", [P, P])
        wes = mem.sb("vwe", [D + 1, D])
        attr = mem.sb("vattr", [D + 1, 2, Q4 * P])
        drow = mem.sb("vdrow", [P, 2, Q4 * P])
        q_rows = mem.sb("q_rows", [P, 2, D])
        hot = [mem.sb(f"hot{s}", [P, Q4, P]) for s in range(2)]
        hot_T = [mem.sb(f"hot_T{s}", [P, Q4, P]) for s in range(2)]
        src4 = [mem.sb(f"vsrc4_{s}", [P, Q4], I32) for s in range(2)]
        kv = [mem.sb(f"vkv{s}", [P, Q4, 2 * D]) for s in range(2)]
        prod = mem.sb("vprod", [P, Q4, D])
        score = mem.sb("vscore", [P, Q4, HEADS])
        msg = [mem.sb(f"vmsg{s}", [P, Q4, ROWW]) for s in range(2)]
        sums_T = mem.sb("sums_T", [ROWW, Q_ROWS])
        ps_e = [mem.ps(f"vps_e{s}", [P, Q4, D]) for s in range(2)]
        ps_q = [mem.ps(f"vps_q{s}", [P, Q4, D]) for s in range(2)]
        ps_s = [mem.ps(f"vps_s{s}", [ROWW, P]) for s in range(2)]
        ps_t = mem.ps("vps_t", [P, 2, BANK])

        loaded = mem.sem("loaded")
        iota_ready = mem.sem("iota_ready")
        ones_ready = mem.sem("ones_ready")
        edges_landed = [mem.sem(f"edges_landed{s}") for s in range(2)]
        src_ready = mem.sem("src_ready")
        kv_landed = [mem.sem(f"kv_landed{s}") for s in range(2)]
        hot_ready = mem.sem("hot_ready")
        eq_ready = mem.sem("eq_ready")
        clip_ready = mem.sem("clip_ready")
        exp_ready = mem.sem("exp_ready")
        msg_ready = mem.sem("msg_ready")
        sums_ready = mem.sem("sums_ready")
        sums_added = mem.sem("sums_added")
        turned_ps = mem.sem("turned_ps")
        turned_read = mem.sem("turned_read")
        past_waits = mem.sem("past_waits")
        block = ctx.enter_context(nc.Block())
        CLIP = 5.0 * float(np.sqrt(np.float32(HD)))

        @block.sync
        def _(sp):
            sp.dma_start(wes[:], we).then_inc(loaded, 16)
            sp.wait_ge(ones_ready, 1)

            def load(q, s, first=False):
                if not first:
                    sp.wait_ge(hot_ready, q - 1)
                    sp.wait_ge(eq_ready, q - 1)
                sp.dma_start(attr[0:D, s, :], attr_T[:, bass.ds(q * (Q4 * P), Q4 * P)]).then_inc(edges_landed[s], 16)
                sp.dma_start(drow[:, s, :], dstf_dram[bass.ds(q * (Q4 * P), Q4 * P)].partition_broadcast(P)).then_inc(edges_landed[s], 16)
                at = sp.value_load(first_node[0:1, bass.ds(q, 1)], min_val=0, max_val=N)
                sp.dma_start(q_rows[:, s, :], q_dram[bass.ds(at, P), :]).then_inc(edges_landed[s], 16)

            load(0, 0, True)
            load(1, 1, True)
            with sp.Fori(1, NQ // 2) as i:
                for s in range(2):
                    load(2 * i + s, s)

        @block.gpsimd
        def _(pool):
            nc.gpsimd.iota(iota_i[:], pattern=[[1, P]], base=0, channel_multiplier=0).then_inc(iota_ready, 1)
            last_node = pool.to_reg(NPAD - 1)

            def gather(q, s, first=False):
                pool.wait_ge(src_ready, q + 1)
                if not first:
                    pool.wait_ge(msg_ready, q - 1)
                pool.sem_inc(past_waits, 1)
                for k in range(Q4):
                    nc.gpsimd.indirect_dma_start(
                        out=kv[s][:, k, :], out_offset=None, in_=kv_dram,
                        in_offset=bass.IndirectOffsetOnAxis(ap=src4[s][:, k:k + 1], axis=0),
                        bounds_check=last_node, oob_is_err=True).then_inc(kv_landed[s], 16)

            gather(0, 0, True)
            gather(1, 1, True)
            with pool.Fori(1, NQ // 2) as i:
                for s in range(2):
                    gather(2 * i + s, s)

        @block.scalar
        def _(act):
            def indices(q, s, use, first=False):
                if not first:
                    act.wait_ge(kv_landed[s], 16 * Q4 * use)
                nc.scalar.copy(src4[s][:], src_i[:, bass.ds(q * Q4, Q4)]).then_inc(src_ready, 1)

            def weigh(q, s):
                act.wait_ge(clip_ready, q + 1)
                nc.scalar.activation(msg[s][:, :, D:ROWW], score[:], ACT.Exp,
                                     scale=1.0 / float(np.sqrt(np.float32(HD)))).then_inc(exp_ready, 1)

            indices(0, 0, 0, True)
            indices(1, 1, 0, True)
            with act.Fori(0, NQ // 2 - 1) as i:
                for s in range(2):
                    indices(2 * i + 2 + s, s, i + 1)
                    weigh(2 * i + s, s)
            weigh(NQ - 2, 0)
            weigh(NQ - 1, 1)

        @block.tensor
        def _(pe):
            pe.wait_ge(loaded, 16)

            def edges(q, s, use, first=False):
                pe.wait_ge(edges_landed[s], 48 * (use + 1))
                pe.wait_ge(hot_ready, q + 1)
                if not first:
                    pe.wait_ge(msg_ready, q - 1)
                for k in range(Q4):
                    nc.tensor.matmul(ps_e[s][:, k, :], attr[:, s, k * P:(k + 1) * P], wes[:], start=True, stop=True)
                for k in range(Q4):
                    last = nc.tensor.matmul(ps_q[s][:, k, :], hot_T[s][:, k, :], q_rows[:, s, :], start=True, stop=True)
                last.then_inc(eq_ready, 1)

            def add_up(q, s, first=False):
                pe.wait_ge(msg_ready, q + 1)
                if not first:
                    pe.wait_ge(sums_added, q - 1)
                for k in range(Q4):
                    last = nc.tensor.matmul(ps_s[s][:], msg[s][:, k, :], hot[s][:, k, :], start=k == 0, stop=k == Q4 - 1)
                last.then_inc(sums_ready, 1)

            edges(0, 0, 0, True)
            edges(1, 1, 0, True)
            add_up(0, 0, True)
            edges(2, 0, 1)
            add_up(1, 1, True)
            with pe.Fori(1, NQ // 2 - 1) as i:
                edges(2 * i + 1, 1, i)
                add_up(2 * i, 0)
                edges(2 * i + 2, 0, i + 1)
                add_up(2 * i + 1, 1)
            edges(NQ - 1, 1, NQ // 2 - 1)
            add_up(NQ - 2, 0)
            add_up(NQ - 1, 1)
            pe.wait_ge(sums_added, NQ)
            for n, t in enumerate(range(0, NT, 4)):
                if n >= 2:
                    pe.wait_ge(turned_read, n - 1)
                for u in range(t, min(t + 4, NT)):
                    last = nc.tensor.transpose(ps_t[:, n % 2, (u - t) * ROWW:(u - t + 1) * ROWW], sums_T[:, u * P:(u + 1) * P],
                                               ident[0:ROWW, 0:ROWW])
                last.then_inc(turned_ps, 1)

        @block.vector
        def _(dve):
            nc.vector.memset(sums_T[:], 0.0)
            nc.vector.memset(attr[D:D + 1, :, :], 1.0).then_inc(ones_ready, 1)
            dve.wait_ge(iota_ready, 1)
            nc.vector.tensor_copy(iota[:], iota_i[:])
            dve.drain()

            def prepare(q, s, use, first=False):
                dve.wait_ge(edges_landed[s], 48 * (use + 1))
                if not first:
                    dve.wait_ge(sums_ready, q - 1)
                nc.vector.tensor_scalar(hot_T[s][:].rearrange("p k e -> p (k e)"), drow[:, s, :], node_in_window[:, bass.ds(q, 1)],
                                        None, ALU.is_equal)
                nc.vector.tensor_tensor(hot[s][:], iota[:].unsqueeze(1).broadcast_to((P, Q4, P)),
                                        rel[:, bass.ds(q * Q4, Q4)].unsqueeze(2).broadcast_to((P, Q4, P)),
                                        ALU.is_equal).then_inc(hot_ready, 1)

            def attend(q, s, use):
                dve.wait_ge(kv_landed[s], 16 * Q4 * (use + 1))
                dve.wait_ge(eq_ready, q + 1)
                nc.vector.tensor_tensor(prod[:], kv[s][:, :, 0:D], ps_q[s][:], ALU.mult)
                dve.drain()
                nc.vector.tensor_tensor(prod[:], prod[:], ps_e[s][:], ALU.mult)
                dve.drain()
                nc.vector.reduce_sum(score[:].rearrange("p k h -> p (k h)"), prod[:].rearrange("p k (h c) -> p (k h) c", c=HD), axis=AX.X)
                dve.drain()
                nc.vector.tensor_scalar(score[:], score[:], CLIP, -CLIP, ALU.min, ALU.max).then_inc(clip_ready, 1)

            def weigh(q, s):
                dve.wait_ge(exp_ready, q + 1)
                nc.vector.tensor_tensor(msg[s][:, :, 0:D].rearrange("p k (h c) -> p k h c", c=HD),
                                        kv[s][:, :, D:2 * D].rearrange("p k (h c) -> p k h c", c=HD),
                                        msg[s][:, :, D:ROWW].unsqueeze(3).broadcast_to((P, Q4, HEADS, HD)),
                                        ALU.mult).then_inc(msg_ready, 1)

            def add(q, s):
                at = dve.value_load(first_node[0:1, bass.ds(q, 1)], min_val=0, max_val=N)
                dve.wait_ge(sums_ready, q + 1)
                nc.vector.tensor_tensor(sums_T[:, bass.ds(at, P)], sums_T[:, bass.ds(at, P)], ps_s[s][:], ALU.add).then_inc(sums_added, 1)

            prepare(0, 0, 0, True)
            prepare(1, 1, 0, True)
            attend(0, 0, 0)
            weigh(0, 0)
            prepare(2, 0, 1)
            attend(1, 1, 0)
            add(0, 0)
            weigh(1, 1)
            with dve.Fori(1, NQ // 2 - 1) as i:
                prepare(2 * i + 1, 1, i)
                attend(2 * i, 0, i)
                add(2 * i - 1, 1)
                weigh(2 * i, 0)
                prepare(2 * i + 2, 0, i + 1)
                attend(2 * i + 1, 1, i)
                add(2 * i, 0)
                weigh(2 * i + 1, 1)
            prepare(NQ - 1, 1, NQ // 2 - 1)
            attend(NQ - 2, 0, NQ // 2 - 1)
            add(NQ - 3, 1)
            weigh(NQ - 2, 0)
            attend(NQ - 1, 1, NQ // 2 - 1)
            add(NQ - 2, 0)
            weigh(NQ - 1, 1)
            add(NQ - 1, 1)
            for n, t in enumerate(range(0, NT, 4)):
                m = min(4, NT - t)
                dve.wait_ge(turned_ps, n + 1)
                nc.vector.tensor_copy(total[:, t:t + m, :].rearrange("p t c -> p (t c)"), ps_t[:, n % 2, 0:m * ROWW]).then_inc(turned_read, 1)


def attention_general(nc, attr_T, we, src_i, dst_i, dstf_dram, kv_dram, q_dram, sums_dram, total):
    ctx = ExitStack()
    with ctx:
        mem = Pool(nc, ctx)
        dstf = mem.sb("adstf", [P, ET])
        dst_off = mem.sb("adst_off", [P, ET])
        dump_i = mem.sb("adump_i", [P, 1], I32)
        dump = mem.sb("adump", [P, 1])
        before = mem.sb("abefore", [P, P])
        zero = mem.sb("azero", [P, 26 * ROWW])
        wes = mem.sb("awe", [D + 1, D])
        attr = mem.sb("attr", [D + 1, 2, Q4 * P])
        drow = mem.sb("drow", [P, 2, Q4 * P])
        eq = mem.sb("aeq", [P, 2, Q4, P])
        eqb = mem.sb("aeqb", [P, Q4, P])
        earlier = mem.sb("aearlier", [P, Q4])
        first_off = mem.sb("afirst_off", [P, Q4])
        src4 = [mem.sb(f"src4_{s}", [P, Q4], I32) for s in range(2)]
        dst4 = [mem.sb(f"dst4_{s}", [P, Q4], I32) for s in range(2)]
        row4 = [mem.sb(f"row4_{s}", [P, Q4], I32) for s in range(2)]
        kv = [mem.sb(f"kv{s}", [P, Q4, 2 * D]) for s in range(2)]
        qg = [mem.sb(f"qg{s}", [P, Q4, D]) for s in range(2)]
        prod = mem.sb("prod", [P, Q4, D])
        score = mem.sb("score", [P, Q4, HEADS])
        msg = [mem.sb(f"msg{s}", [P, Q4, ROWW]) for s in range(2)]
        pay = [mem.sb(f"apay{s}", [P, Q4, ROWW]) for s in range(2)]
        other = mem.sb("other", [P, NT, ROWW])
        ps_e = [mem.ps(f"ps_e{s}", [P, Q4, D]) for s in range(2)]
        ps_m = [mem.ps(f"ps_m{s}", [P, Q4, ROWW]) for s in range(2)]

        loaded = mem.sem("loaded")
        consts_ready = mem.sem("consts_ready")
        zero_ready = mem.sem("zero_ready")
        zeroed = mem.sem("zeroed")
        attr_ones = mem.sem("attr_ones")
        edges_landed = [mem.sem(f"edges_landed{s}") for s in range(2)]
        kv_landed = [mem.sem(f"kv_landed{s}") for s in range(2)]
        prep_ready = mem.sem("prep_ready")
        e_ready = mem.sem("e_ready")
        clip_ready = mem.sem("clip_ready")
        exp_ready = mem.sem("exp_ready")
        msg_ready = mem.sem("msg_ready")
        sums_ready = mem.sem("sums_ready")
        pay_ready = mem.sem("pay_ready")
        row_landed = [mem.sem(f"arow_landed{k}") for k in range(Q4)]
        sums_back = mem.sem("sums_back")
        past_waits = mem.sem("past_waits")
        block = ctx.enter_context(nc.Block())
        CLIP = 5.0 * float(np.sqrt(np.float32(HD)))

        @block.sync
        def _(sp):
            sp.dma_start(wes[:], we).then_inc(loaded, 16)
            sp.wait_ge(attr_ones, 1)

            def load(q, s, first=False):
                if not first:
                    sp.wait_ge(prep_ready, q - 1)
                    sp.wait_ge(e_ready, q - 1)
                sp.dma_start(attr[0:D, s, :], attr_T[:, bass.ds(q * (Q4 * P), Q4 * P)]).then_inc(edges_landed[s], 16)
                sp.dma_start(drow[:, s, :], dstf_dram[bass.ds(q * (Q4 * P), Q4 * P)].partition_broadcast(P)).then_inc(edges_landed[s], 16)

            load(0, 0, True)
            load(1, 1, True)
            with sp.Fori(1, NQ // 2) as i:
                for s in range(2):
                    load(2 * i + s, s)
            for k in range(Q4):
                sp.wait_ge(row_landed[k], 16 * NQ)
            for tile, sums in ((total, sums_dram[0]), (other, sums_dram[1])):
                sp.dma_start(tile[:], sums[0:NPAD, :].rearrange("(t p) c -> p t c", p=P)).then_inc(sums_back, 16)

        @block.gpsimd
        def _(pool):
            nc.gpsimd.iota(dump_i[:], pattern=[[1, 1]], base=NPAD, channel_multiplier=1)
            nc.gpsimd.memset(before[:], 1.0)
            pool.drain()
            nc.gpsimd.affine_select(out=before[:], in_=before[:], compare_op=ALU.is_gt, fill=0.0, base=0,
                                    pattern=[[-1, P]], channel_multiplier=1).then_inc(consts_ready, 1)
            pool.wait_ge(zeroed, 16 * NACC)
            last_node = pool.to_reg(NPAD - 1)
            last_row = pool.to_reg(ACC_ROWS - 1)

            def gather(q, s, k):
                nc.gpsimd.indirect_dma_start(
                    out=kv[s][:, k, :], out_offset=None, in_=kv_dram,
                    in_offset=bass.IndirectOffsetOnAxis(ap=src4[s][:, k:k + 1], axis=0),
                    bounds_check=last_node, oob_is_err=True).then_inc(kv_landed[s], 16)
                nc.gpsimd.indirect_dma_start(
                    out=qg[s][:, k, :], out_offset=None, in_=q_dram,
                    in_offset=bass.IndirectOffsetOnAxis(ap=dst4[s][:, k:k + 1], axis=0),
                    bounds_check=last_node, oob_is_err=True).then_inc(kv_landed[s], 16)

            def scatter(q, s, k):
                if k >= NACC:
                    pool.wait_ge(row_landed[k - NACC], 16 * (q + 1))
                elif not isinstance(q, int) or q > 0:
                    pool.wait_ge(row_landed[k + Q4 - NACC], 16 * q)
                pool.sem_inc(past_waits, 1)
                nc.gpsimd.indirect_dma_start(
                    out=sums_dram[k % NACC], out_offset=bass.IndirectOffsetOnAxis(ap=row4[s][:, k:k + 1], axis=0),
                    in_=pay[s][:, k, :], in_offset=None, bounds_check=last_row, oob_is_err=True,
                    compute_op=ALU.add).then_inc(row_landed[k], 16)

            def step(q, s, first=False):
                pool.wait_ge(prep_ready, q + 1)
                if not first:
                    pool.wait_ge(msg_ready, q - 1)
                pool.sem_inc(past_waits, 1)
                for k in range(Q4):
                    gather(q, s, k)
                    if not isinstance(q, int) or q > 0:
                        if k == 0:
                            pool.wait_ge(pay_ready, q)
                        scatter(q - 1, 1 - s, k)

            step(0, 0, True)
            step(1, 1, True)
            with pool.Fori(1, NQ // 2) as i:
                for s in range(2):
                    step(2 * i + s, s)
            pool.wait_ge(pay_ready, NQ)
            for k in range(Q4):
                scatter(NQ - 1, 1, k)

        @block.scalar
        def _(act):
            act.wait_ge(zero_ready, 1)
            for a in range(NACC):
                act.dma_start(sums_dram[a].rearrange("(p r) c -> p (r c)", p=P), zero[:]).then_inc(zeroed, 16)
            def step(q, s, first=False):
                act.wait_ge(clip_ready, q + 1)
                nc.scalar.activation(msg[s][:, :, D:ROWW], score[:], ACT.Exp, scale=1.0 / float(np.sqrt(np.float32(HD)))).then_inc(exp_ready, 1)
                act.wait_ge(sums_ready, q + 1)
                if not first:
                    for k in range(Q4):
                        act.wait_ge(row_landed[k], 16 * (q - 1))
                nc.scalar.copy(pay[s][:], ps_m[s][:]).then_inc(pay_ready, 1)

            step(0, 0, True)
            step(1, 1, True)
            with act.Fori(1, NQ // 2) as i:
                for s in range(2):
                    step(2 * i + s, s)

        @block.tensor
        def _(pe):
            pe.wait_ge(loaded, 16)

            def edges(q, s, use, first=False):
                pe.wait_ge(edges_landed[s], 32 * (use + 1))
                if not first:
                    pe.wait_ge(msg_ready, q - 1)
                for k in range(Q4):
                    last = nc.tensor.matmul(ps_e[s][:, k, :], attr[:, s, k * P:(k + 1) * P], wes[:], start=True, stop=True)
                last.then_inc(e_ready, 1)

            def add_up(q, s, first=False):
                pe.wait_ge(msg_ready, q + 1)
                if not first:
                    pe.wait_ge(pay_ready, q - 1)
                for k in range(Q4):
                    last = nc.tensor.matmul(ps_m[s][:, k, :], eq[:, s, k, :], msg[s][:, k, :], start=True, stop=True)
                last.then_inc(sums_ready, 1)

            edges(0, 0, 0, True)
            edges(1, 1, 0, True)
            add_up(0, 0, True)
            edges(2, 0, 1)
            add_up(1, 1, True)
            with pe.Fori(1, NQ // 2 - 1) as i:
                edges(2 * i + 1, 1, i)
                add_up(2 * i, 0)
                edges(2 * i + 2, 0, i + 1)
                add_up(2 * i + 1, 1)
            edges(NQ - 1, 1, NQ // 2 - 1)
            add_up(NQ - 2, 0)
            add_up(NQ - 1, 1)

        @block.vector
        def _(dve):
            nc.vector.memset(zero[:], 0.0).then_inc(zero_ready, 1)
            nc.vector.memset(attr[D:D + 1, :, :], 1.0).then_inc(attr_ones, 1)
            dve.wait_ge(consts_ready, 1)
            nc.vector.tensor_copy(dstf[:], dst_i[:])
            nc.vector.tensor_copy(dump[:], dump_i[:])
            dve.drain()
            nc.vector.tensor_scalar(dst_off[:], dstf[:], dump[:], None, ALU.subtract)

            def prepare(q, s, use, first=False):
                dve.wait_ge(edges_landed[s], 32 * (use + 1))
                if not first:
                    dve.wait_ge(sums_ready, q - 1)
                    for k in range(Q4):
                        dve.wait_ge(row_landed[k], 16 * (q - 1))
                nc.vector.tensor_copy(src4[s][:], src_i[:, bass.ds(q * Q4, Q4)])
                nc.vector.tensor_copy(dst4[s][:], dst_i[:, bass.ds(q * Q4, Q4)])
                for k in range(Q4):
                    nc.vector.tensor_scalar(eq[:, s, k, :], drow[:, s, k * P:(k + 1) * P], dstf[:, bass.ds(q * Q4 + k, 1)],
                                            None, ALU.is_equal)
                dve.drain()
                nc.vector.tensor_tensor(eqb[:], eq[:, s, :, :], before[:].unsqueeze(1).broadcast_to((P, Q4, P)), ALU.mult)
                dve.drain()
                nc.vector.reduce_sum(earlier[:], eqb[:], axis=AX.X)
                dve.drain()
                nc.vector.scalar_tensor_tensor(first_off[:], earlier[:], 0.5, dst_off[:, bass.ds(q * Q4, Q4)], ALU.is_lt, ALU.mult)
                dve.drain()
                nc.vector.tensor_scalar(row4[s][:], first_off[:], dump[:], None, ALU.add).then_inc(prep_ready, 1)

            def attend(q, s, use, first=False):
                dve.wait_ge(kv_landed[s], 32 * Q4 * (use + 1))
                nc.vector.tensor_tensor(prod[:], kv[s][:, :, 0:D], qg[s][:], ALU.mult)
                dve.drain()
                dve.wait_ge(e_ready, q + 1)
                nc.vector.tensor_tensor(prod[:], prod[:], ps_e[s][:], ALU.mult)
                dve.drain()
                nc.vector.reduce_sum(score[:].rearrange("p k h -> p (k h)"), prod[:].rearrange("p k (h c) -> p (k h) c", c=HD), axis=AX.X)
                dve.drain()
                nc.vector.tensor_scalar(score[:], score[:], CLIP, -CLIP, ALU.min, ALU.max).then_inc(clip_ready, 1)
                dve.wait_ge(exp_ready, q + 1)
                nc.vector.tensor_tensor(msg[s][:, :, 0:D].rearrange("p k (h c) -> p k h c", c=HD),
                                        kv[s][:, :, D:2 * D].rearrange("p k (h c) -> p k h c", c=HD),
                                        msg[s][:, :, D:ROWW].unsqueeze(3).broadcast_to((P, Q4, HEADS, HD)),
                                        ALU.mult).then_inc(msg_ready, 1)

            prepare(0, 0, 0, True)
            prepare(1, 1, 0, True)
            attend(0, 0, 0)
            prepare(2, 0, 1)
            attend(1, 1, 0)
            with dve.Fori(1, NQ // 2 - 1) as i:
                prepare(2 * i + 1, 1, i)
                attend(2 * i, 0, i)
                prepare(2 * i + 2, 0, i + 1)
                attend(2 * i + 1, 1, i)
            prepare(NQ - 1, 1, NQ // 2 - 1)
            attend(NQ - 2, 0, NQ // 2 - 1)
            attend(NQ - 1, 1, NQ // 2 - 1)

            dve.wait_ge(sums_back, 16 * NACC)
            nc.vector.tensor_tensor(total[:], total[:], other[:], ALU.add)


def attention_out(nc, total, x, eps, out):
    ctx = ExitStack()
    with ctx:
        mem = Pool(nc, ctx)
        stats = (mem.sb("st3", [P, NT, 6]), mem.sb("dif3", [P, NT]), mem.sb("var3", [P, NT]))
        mean = mem.sb("mean3", [P, NT])
        sd = mem.sb("sd3", [P, NT])
        z = mem.sb("z", [P, NT, HEADS])
        res = mem.sb("res", [P, NT, D])
        result = mem.sb("result", [P, NT, D])
        var_ready = mem.sem("var_ready")
        sd_ready = mem.sem("sd_ready")
        out_ready = mem.sem("out_ready")
        out_stored = mem.sem("out_stored")
        block = ctx.enter_context(nc.Block())

        @block.sync
        def _(sp):
            sp.wait_ge(out_ready, 1)
            sp.dma_start(out[0:(NT - 1) * P, :].rearrange("(t p) d -> p t d", p=P), result[:, 0:NT - 1, :]).then_inc(out_stored, 16)
            sp.dma_start(out[(NT - 1) * P:N, :], result[0:LAST, NT - 1, :]).then_inc(out_stored, 16)
            sp.wait_ge(out_stored, 32)

        @block.scalar
        def _(act):
            act.wait_ge(var_ready, 1)
            nc.scalar.activation(sd[:], stats[2][:], ACT.Sqrt, bias=eps[:, 0:1]).then_inc(sd_ready, 1)

        @block.vector
        def _(dve):
            nc.vector.tensor_scalar(z[:], total[:, :, D:ROWW], 1e-6, None, ALU.add)
            dve.drain()
            nc.vector.reciprocal(z[:], z[:])
            dve.drain()
            for h in range(HEADS):
                nc.vector.tensor_tensor(res[:, :, h * HD:(h + 1) * HD], total[:, :, h * HD:(h + 1) * HD],
                                        z[:, :, h:h + 1].broadcast_to((P, NT, HD)), ALU.mult)
            dve.drain()
            nc.vector.tensor_tensor(x[:], x[:], res[:], ALU.add)
            dve.drain()
            layer_norm(nc, dve, stats, x, result, mean, sd, var_ready, sd_ready, 1).then_inc(out_ready, 1)


def build(nc, a):
    def dram(name, shape):
        return nc.dram_tensor(name, shape, F32).ap()

    adj = dram("adj", [CELLS, 2])
    adj_count = dram("adj_count", [NPAD, COLS])
    adj_weight = dram("adj_weight", [NPAD, COLS])
    key_dram = dram("key_dram", [EPAD])
    dstf_dram = dram("dstf_dram", [EPAD])
    kv_dram = dram("kv_dram", [NPAD, 2 * D])
    q_dram = dram("q_dram", [Q_ROWS, D])
    sums_dram = [dram(f"sums_dram{i}", [ACC_ROWS, ROWW]) for i in range(NACC)]
    with (
        nc.sbuf_tensor("ident", [P, P], F32) as ident,
        nc.sbuf_tensor("x", [P, NT, D], F32) as x,
        nc.sbuf_tensor("w_deg", [P, NT], F32) as w_deg,
        nc.sbuf_tensor("eps", [P, 2], F32) as eps,
        nc.sbuf_tensor("src_i", [P, ET], I32) as src_i,
        nc.sbuf_tensor("dst_i", [P, ET], I32) as dst_i,
        nc.sbuf_tensor("rel", [P, ET], F32) as rel,
        nc.sbuf_tensor("node_in_window", [P, NQ], F32) as node_in_window,
        nc.sbuf_tensor("first_node", [1, NQ], I32) as first_node,
        nc.sbuf_tensor("windowed", [1, 1], I32) as windowed,
    ):
        find_windows(nc, src_i, dst_i, a["dst_cols"], a["src_cols"], rel, node_in_window, first_node, windowed)
        build_adjacency(nc, src_i, dst_i, a["w_cols"], a["src_flat"], a["dst_flat"], key_dram, dstf_dram, adj)
        first_layer(nc, a["x_nm"], adj, adj_count, adj_weight, a["L0_gnn_weight"], a["L0_gnn_bias"], ident, x, w_deg, eps)
        convolutions(nc, adj_count, adj_weight,
                     [a[k] for k in ("L1_gnn_W1", "L1_gnn_W2", "L1_gnn_W3", "L2_gnn_W1", "L2_gnn_W2")],
                     [a[k] for k in ("L1_gnn_b1", "L1_gnn_b2", "L1_gnn_b3")],
                     [a[f"L2_gnn_{k}"] for k in ("b1", "gn1_w", "gn1_b", "gn1_a", "b2", "gn2_w", "gn2_b", "gn2_a")],
                     ident, x, w_deg, eps)
        attention_tables(nc, a["kvq_w"], a["kvq_b"], kv_dram, q_dram, ident, x)
        with nc.sbuf_tensor("total", [P, NT, ROWW], F32) as total:
            in_windows = nc.values_load(windowed[0:1, 0:1], min_val=0, max_val=1)
            with nc.If(in_windows == 1):
                attention_windowed(nc, a["attr_T"], a["we"], src_i, rel, node_in_window, first_node, dstf_dram, kv_dram, q_dram,
                                   ident, total)
            with nc.Else():
                attention_general(nc, a["attr_T"], a["we"], src_i, dst_i, dstf_dram, kv_dram, q_dram, sums_dram, total)
            attention_out(nc, total, x, eps, a["out"])


def kernel(**inputs):
    import concourse.bacc as bacc
    from concourse.bass_utils import run_bass_kernel_spmd

    given = {k: np.asarray(v) for k, v in inputs.items()}

    def edge_list(values, fill):
        padded = np.full((EPAD,), fill, values.dtype)
        padded[:E] = values
        return padded

    src, dst, w = edge_list(given["src"], 0), edge_list(given["dst"], N), edge_list(given["edge_weight"], 0)
    attr = np.zeros((D, EPAD), np.float32)
    attr[:, :E] = given["edge_attr_96"].T
    x = np.zeros((NPAD, D), np.float32)
    x[:N] = given["x"]
    arrays = {
        "src_cols": np.ascontiguousarray(src.reshape(ET, P).T),
        "dst_cols": np.ascontiguousarray(dst.reshape(ET, P).T),
        "w_cols": np.ascontiguousarray(w.reshape(ET, P).T),
        "src_flat": src.reshape(P, ET),
        "dst_flat": dst.reshape(P, ET),
        "attr_T": attr,
        "x_nm": np.ascontiguousarray(x.reshape(NT, P, D).transpose(1, 0, 2)),
        "we": np.concatenate([given["L3_gnn_We"], given["L3_gnn_be"][None]]),
        "kvq_w": np.concatenate([given["L3_gnn_Wk"], given["L3_gnn_Wv"], given["L3_gnn_Wq"]], axis=1),
        "kvq_b": np.concatenate([given["L3_gnn_bk"], given["L3_gnn_bv"], given["L3_gnn_bq"]])[None],
    }
    for name, value in given.items():
        if name.startswith(("L0", "L1", "L2")):
            arrays[name] = np.ascontiguousarray(value)
    nc = bacc.Bacc("TRN2", target_bir_lowering=False, num_devices=1)
    aps = {}
    for name, value in arrays.items():
        aps[name] = nc.dram_tensor(f"in_{name}", value.shape, mybir.dt.from_np(value.dtype), kind="ExternalInput").ap()
    aps["out"] = nc.dram_tensor("out_x", (N, D), F32, kind="ExternalOutput").ap()
    build(nc, aps)
    result = run_bass_kernel_spmd(nc, [{f"in_{k}": v for k, v in arrays.items()}], core_ids=[0])
    return result.results[0]["out_x"]
```

```python
from contextlib import ExitStack

import numpy as np

import concourse.bass as bass
from concourse import mybir

F32 = mybir.dt.float32
BF16 = mybir.dt.bfloat16
I32 = mybir.dt.int32
ALU = mybir.AluOpType
ACT = mybir.ActivationFunctionType
AX = mybir.AxisListType

P = 128
HALF_P = P // 2
N = 3125
D = 96
E = 103125
HEADS = 8
HD = D // HEADS
NT = -(-N // P)
NPAD = NT * P
LAST = N - (NT - 1) * P
COLS = 3136
BANK = 512
NB = -(-N // BANK)
BLOCKS = [(b * BANK, min(N, (b + 1) * BANK)) for b in range(NB)]
HALF = (NB // 2) * BANK
PB = 5

G = 8
NG = -(-E // (P * G))
ET = NG * G
EPAD = ET * P
DUMP = NPAD * COLS
CELLS = DUMP + 2 * P * G
NPAIR = ET // 2
WINDOW = 12
PLACES = NT * WINDOW
CENTRE = PLACES // 2
BLOCK = 124
HALF_BLOCK = BLOCK // 2
SLOTS_B = 4
RING = SLOTS_B * BLOCK
ROUND = 16
NROUND = -(-NPAIR // ROUND)
AHEAD = 2
Q4 = 4
NQ = ET // Q4
SLOTS = 4
ROUNDS = NQ // SLOTS
ROWW = D + HEADS
NACC = 2
Q_ROWS = NPAD + P
ACC_ROWS = NPAD + P
LN_EPS = 1e-5
GN_EPS = 1e-5

assert NG % 2 == 1 and NT % 5 == 0 and NQ - SLOTS * ROUNDS == 2 and CELLS < 1 << 24
assert CENTRE <= 256 and ROUND % SLOTS == 0 and NROUND % SLOTS_B == 2 and BLOCK * NROUND - HALF_BLOCK > N + 3


class Phase:

    def __init__(self, nc, stack, name):
        self.nc, self.stack, self.name, self.sems = nc, stack, name, []
        stack.callback(self.end)

    def end(self):
        self.nc.clear_and_free_semaphores(self.sems)
        self.nc.all_engine_barrier()

    def sb(self, name, shape, dt=F32):
        return self.stack.enter_context(self.nc.sbuf_tensor(f"{self.name}_{name}", shape, dt))

    def ps(self, name, shape):
        return self.stack.enter_context(self.nc.psum_tensor(f"{self.name}_{name}", shape, F32))

    def sem(self, name):
        self.sems.append(self.nc.alloc_semaphore(f"{self.name}_{name}"))
        return self.sems[-1]


def node_major(psum):
    return psum[:, 0:PB * BANK].rearrange("p (b c) -> p b c", c=BANK)[:, :, 0:PB * D]


def by_bank(tile):
    return tile[:, :, :].rearrange("p (b j) d -> p b (j d)", j=PB)


def node_major_by_node(psum):
    return node_major(psum).rearrange("p b (j d) -> p b j d", d=D)


def by_node(tile):
    return tile[:, :, :].rearrange("p (b j) d -> p b j d", j=PB)


def per_node_in_bank(column):
    return column.rearrange("p (b j) -> p b j", j=PB).unsqueeze(3).broadcast_to((P, NT // PB, PB, D))


def node_cols(t):
    return (t // PB) * BANK + (t % PB) * D


def per_node(column):
    return column.unsqueeze(2).broadcast_to((P, NT, D))


def per_feature(row):
    return row.unsqueeze(1).broadcast_to((P, NT, D))


def reaches(step, n):
    return not isinstance(step, int) or step >= n


def later(i, s, n):
    return i + (s + n) // SLOTS, (s + n) % SLOTS


def build_adjacency(nc, key, w_cols, src_flat, dst_flat, key_dram, dstf_dram, adj):
    ctx = ExitStack()
    with ctx:
        mem = Phase(nc, ctx, "build_adjacency")
        zero = mem.sb("zero", [P, COLS])
        w = mem.sb("w", [P, ET])
        rest = mem.sb("rest", [P, ET])
        key_off = mem.sb("key_off", [P, ET])
        wv = mem.sb("wv", [P, ET, 5], BF16)
        fsrc_i = mem.sb("fsrc_i", [P, ET], I32)
        fdst_i = mem.sb("fdst_i", [P, ET], I32)
        fsrc = mem.sb("fsrc", [P, ET])
        fdst = mem.sb("fdst", [P, ET])
        fkey = mem.sb("fkey", [P, ET])
        dump_i = mem.sb("dump_i", [P, G], I32)
        dump = mem.sb("dump", [P, G])
        before = mem.sb("before", [P, P], BF16)
        one = mem.sb("one", [P, 1], BF16)
        keyrow = mem.sb("keyrow", [P, 2, G * P])
        SPAN = G * P + P
        eq = mem.sb("eq", [P, 2, G * SPAN], BF16)
        eq_before = mem.sb("eq_before", [P, 2, G, P], BF16)
        first_off = mem.sb("first_off", [P, G])
        cell = [mem.sb(f"cell{s}", [P, G], I32) for s in range(2)]
        pay = [mem.sb(f"pay{s}", [P, G, 2]) for s in range(2)]
        sums = [mem.ps(f"sums{s}", [P, G, 5]) for s in range(2)]

        loaded = mem.sem("loaded")
        zero_ready = mem.sem("zero_ready")
        zeroed = mem.sem("zeroed")
        flat_keys = mem.sem("flat_keys")
        keys_stored = mem.sem("keys_stored")
        consts_ready = mem.sem("consts_ready")
        row_landed = [mem.sem(f"row_landed{s}") for s in range(2)]
        eq_ready = mem.sem("eq_ready")
        sums_ready = mem.sem("sums_ready")
        sums_free = mem.sem("sums_free")
        pay_ready = mem.sem("pay_ready")
        groups_landed = mem.sem("groups_landed")
        cell_landed = [mem.sem(f"cell_landed{k}") for k in range(G)]
        block = ctx.enter_context(nc.Block())

        @block.sync
        def _(sp):
            for tile, source in ((fsrc_i, src_flat), (fdst_i, dst_flat), (w, w_cols)):
                sp.dma_start(tile[:], source).then_inc(loaded, 16)
            sp.wait_ge(flat_keys, 1)
            sp.dma_start(key_dram.rearrange("(p a) -> p a", p=P), fkey[:]).then_inc(keys_stored, 16)
            sp.dma_start(dstf_dram.rearrange("(p a) -> p a", p=P), fdst[:]).then_inc(keys_stored, 16)
            sp.wait_ge(keys_stored, 32)

            def load(g, s):
                keys = key_dram[bass.ds(g * (G * P), G * P)].partition_broadcast(P)
                sp.dma_start(keyrow[:, s, :], keys).then_inc(row_landed[s], 16)

            load(0, 0)
            load(1, 1)
            with sp.Fori(1, NG // 2) as i:
                for s in range(2):
                    sp.wait_ge(eq_ready, 2 * i + s - 1)
                    load(2 * i + s, s)
            sp.wait_ge(eq_ready, NG - 2)
            load(NG - 1, 0)

        @block.scalar
        def _(act):
            act.wait_ge(zero_ready, 1)
            zeros = zero[:, :].unsqueeze(1).broadcast_to((P, 2, COLS))
            rows = adj[0:DUMP, :].rearrange("(t p c) two -> t p (c two)", p=P, c=COLS)
            with act.Fori(0, NT) as t:
                act.dma_start(rows[bass.ds(t, 1)].squeeze(0).rearrange("p (a c) -> p a c", a=2),
                              zeros).then_inc(zeroed, 16)
            act.dma_start(adj[DUMP:CELLS, :].rearrange("(p a) two -> p (a two)", p=P),
                          zero[:, 0:4 * G]).then_inc(zeroed, 16)

        @block.gpsimd
        def _(pool):
            nc.gpsimd.iota(dump_i[:], pattern=[[P, G]], base=DUMP, channel_multiplier=1).then_inc(consts_ready, 1)
            nc.gpsimd.memset(before[:], 1.0)
            pool.drain()
            nc.gpsimd.affine_select(out=before[:], in_=before[:], compare_op=ALU.is_gt, fill=0.0, base=0,
                                    pattern=[[1, P]], channel_multiplier=-1).then_inc(consts_ready, 1)
            pool.wait_ge(zeroed, 16 * (NT + 1))
            last_cell = pool.to_reg(CELLS - 1)

            def scatter(g, s, first=False):
                pool.wait_ge(pay_ready, g + 1)
                if not first:
                    for k in range(G):
                        pool.wait_ge(cell_landed[k], 16 * g)
                pool.sem_inc(groups_landed, 1)
                for k in range(G):
                    nc.gpsimd.indirect_dma_start(
                        out=adj, out_offset=bass.IndirectOffsetOnAxis(ap=cell[s][:, k:k + 1], axis=0),
                        in_=pay[s][:, k, :], in_offset=None, bounds_check=last_cell, oob_is_err=True,
                        compute_op=ALU.add).then_inc(cell_landed[k], 16)

            scatter(0, 0, True)
            with pool.Fori(0, NG // 2) as i:
                scatter(2 * i + 1, 1)
                scatter(2 * i + 2, 0)
            for k in range(G):
                pool.wait_ge(cell_landed[k], 16 * NG)

        @block.tensor
        def _(pe):
            pe.wait_ge(consts_ready, 2)

            def add_equals(g, s):
                pe.wait_ge(eq_ready, g + 1)
                pe.wait_ge(sums_free, g + 1)
                eqs = eq[:, s, :].rearrange("p (k e) -> p k e", e=SPAN)
                flat = eq[:, s, :]
                for i in range(G):
                    out = sums[s][:, i, :]

                    def equals(j):
                        at = j * G * P + i * P
                        return flat[:, at:at + P]

                    def values(j, lo):
                        return wv[:, bass.ds(g * G + j, 1), lo:5].squeeze(1)

                    nc.tensor.matmul(out[:, 0:1], eq_before[:, s, i, :], one[:], start=True, stop=False)
                    nc.tensor.matmul(out[:, 1:5], equals(i), values(i, 1), start=False, stop=False)
                    for n, j in enumerate(j for j in range(G) if j != i):
                        lo = 0 if j < i else 1
                        last = nc.tensor.matmul(out[:, lo:5], equals(j), values(j, lo),
                                                start=False, stop=n == G - 2)
                last.then_inc(sums_ready, 1)

            add_equals(0, 0)
            with pe.Fori(0, NG // 2) as i:
                add_equals(2 * i + 1, 1)
                add_equals(2 * i + 2, 0)

        @block.vector
        def _(dve):
            nc.vector.memset(zero[:], 0.0).then_inc(zero_ready, 1)
            nc.vector.memset(one[:], 1.0)
            nc.vector.memset(wv[:, :, 0:2], 1.0)
            dve.wait_ge(loaded, 48)
            nc.vector.tensor_copy(fsrc[:], fsrc_i[:])
            nc.vector.tensor_copy(fdst[:], fdst_i[:])
            dve.drain()
            nc.vector.scalar_tensor_tensor(fkey[:], fsrc[:], float(COLS), fdst[:], ALU.mult, ALU.add).then_inc(flat_keys, 1)
            dve.wait_ge(consts_ready, 2)
            nc.vector.tensor_copy(dump[:], dump_i[:])
            nc.vector.tensor_copy(wv[:, :, 2], w[:])
            dve.drain()
            nc.vector.tensor_tensor(key_off[:].rearrange("p (g k) -> p g k", k=G),
                                    key[:].rearrange("p (g k) -> p g k", k=G),
                                    dump[:].unsqueeze(1).broadcast_to((P, NG, G)), ALU.subtract)
            nc.vector.tensor_tensor(rest[:], w[:], wv[:, :, 2], ALU.subtract)
            dve.drain()
            nc.vector.tensor_copy(wv[:, :, 3], rest[:])
            dve.drain()
            nc.vector.tensor_tensor(w[:], rest[:], wv[:, :, 3], ALU.subtract)
            dve.drain()
            nc.vector.tensor_copy(wv[:, :, 4], w[:])
            dve.sem_inc(sums_free, 2)

            def compare(g, s, use, first=False):
                dve.wait_ge(row_landed[s], 16 * (use + 1))
                if not first:
                    dve.wait_ge(sums_ready, g - 1)
                for k in range(G):
                    nc.vector.tensor_scalar(eq[:, s, k * G * P:(k + 1) * G * P], keyrow[:, s, :],
                                            key[:, bass.ds(g * G + k, 1)], None, ALU.is_equal)
                dve.drain()
                own = eq[:, s, :].rearrange("p (k e) -> p k e", e=SPAN)[:, :, 0:P]
                nc.vector.tensor_tensor(eq_before[:, s, :, :], own,
                                        before[:].unsqueeze(1).broadcast_to((P, G, P)),
                                        ALU.mult).then_inc(eq_ready, 1)

            def finish(g, s, first=False):
                dve.wait_ge(sums_ready, g + 1)
                if not first:
                    dve.wait_ge(groups_landed, g)
                nc.vector.tensor_copy(pay[s][:, :, 0], sums[s][:, :, 1])
                nc.vector.reduce_sum(pay[s][:, :, 1], sums[s][:, :, 2:5], axis=AX.X)
                nc.vector.scalar_tensor_tensor(first_off[:], sums[s][:, :, 0], 0.5,
                                               key_off[:, bass.ds(g * G, G)], ALU.is_lt,
                                               ALU.mult).then_inc(sums_free, 1)
                dve.drain()
                nc.vector.tensor_tensor(cell[s][:], first_off[:], dump[:], ALU.add).then_inc(pay_ready, 1)
                dve.drain()

            compare(0, 0, 0, True)
            compare(1, 1, 0, True)
            finish(0, 0, True)
            with dve.Fori(0, NG // 2 - 1) as i:
                compare(2 * i + 2, 0, i + 1)
                finish(2 * i + 1, 1)
                compare(2 * i + 3, 1, i + 1)
                finish(2 * i + 2, 0)
            compare(NG - 1, 0, NG // 2)
            finish(NG - 2, 1)
            finish(NG - 1, 0)


def layer_norm_stats(nc, dve, act_mem, x, mean, sd, var_ready, sd_ready, n):
    st, dif, var = act_mem
    for t in range(NT):
        nc.vector.bn_stats(st[:, t, :], x[:, t, :])
    dve.drain()
    nc.vector.tensor_tensor(mean[:], st[:, :, 1], st[:, :, 4], ALU.add)
    nc.vector.tensor_tensor(dif[:], st[:, :, 1], st[:, :, 4], ALU.subtract)
    nc.vector.tensor_tensor(var[:], st[:, :, 2], st[:, :, 5], ALU.add)
    dve.drain()
    nc.vector.tensor_scalar(mean[:], mean[:], 0.5, None, ALU.mult)
    nc.vector.tensor_tensor(dif[:], dif[:], dif[:], ALU.mult)
    nc.vector.tensor_scalar(var[:], var[:], 1.0 / D, None, ALU.mult)
    dve.drain()
    nc.vector.scalar_tensor_tensor(var[:], dif[:], 0.25, var[:], ALU.mult, ALU.add).then_inc(var_ready, 1)
    dve.wait_ge(sd_ready, n)
    nc.vector.reciprocal(sd[:], sd[:])
    dve.drain()


def layer_norm(nc, dve, act_mem, x, out, mean, sd, var_ready, sd_ready, n):
    layer_norm_stats(nc, dve, act_mem, x, mean, sd, var_ready, sd_ready, n)
    for t in range(NT):
        last = nc.vector.tensor_scalar(out[:, t, :], x[:, t, :], mean[:, t:t + 1], sd[:, t:t + 1], ALU.subtract, ALU.mult)
    return last


def first_pass(nc, x_nm, adj, adj_count, adj_weight, x, agg):
    ctx = ExitStack()
    with ctx:
        mem = Phase(nc, ctx, "first_pass")
        pair = mem.sb("pair", [P, 2, COLS, 2])
        count = mem.sb("count", [P, 2, COLS])
        weight = mem.sb("weight", [P, 2, COLS])
        lhs = [mem.sb(f"lhs{s}", [P, D + 2]) for s in range(2)]
        lhs_w = mem.sb("lhs_w", [P, D + 2])
        odeg = [mem.sb(f"odeg{s}", [P, 1]) for s in range(2)]
        osd = [mem.sb(f"osd{s}", [P, 1]) for s in range(2)]
        acc = mem.ps("acc", [P, NB * BANK])

        loaded = mem.sem("loaded")
        pair_landed = [mem.sem(f"pair_landed{s}") for s in range(2)]
        stored = [mem.sem(f"stored{s}") for s in range(2)]
        counts_ready = mem.sem("counts_ready")
        weights_ready = mem.sem("weights_ready")
        odeg_ready = mem.sem("odeg_ready")
        osd_ready = mem.sem("osd_ready")
        lhs_ready = mem.sem("lhs_ready")
        tiles_done = mem.sem("tiles_done")
        block = ctx.enter_context(nc.Block())
        rows = adj[0:DUMP, :].rearrange("(t p c) two -> t p c two", p=P, c=COLS)
        count_rows = adj_count.rearrange("(t p) c -> t p c", p=P)
        weight_rows = adj_weight.rearrange("(t p) c -> t p c", p=P)

        @block.sync
        def _(sp):
            sp.dma_start(x[:], x_nm).then_inc(loaded, 16)

            def load(t, s):
                sp.dma_start(pair[:, s], rows[bass.ds(t, 1)].squeeze(0)).then_inc(pair_landed[s], 16)

            def store(t, s):
                sp.wait_ge(counts_ready, t + 1)
                sp.dma_start(count_rows[bass.ds(t, 1)].squeeze(0), count[:, s]).then_inc(stored[s], 16)
                sp.wait_ge(weights_ready, t + 1)
                sp.dma_start(weight_rows[bass.ds(t, 1)].squeeze(0), weight[:, s]).then_inc(stored[s], 16)

            load(0, 0)
            load(1, 1)
            with sp.Fori(0, NT // 2 - 1) as i:
                for s in range(2):
                    store(2 * i + s, s)
                    load(2 * i + s + 2, s)
            store(NT - 3, 0)
            load(NT - 1, 0)
            store(NT - 2, 1)
            store(NT - 1, 0)
            sp.wait_ge(stored[0], 32 * (NT // 2 + 1))
            sp.wait_ge(stored[1], 32 * (NT // 2))

        @block.scalar
        def _(act):
            def split(t, s, use, first=False):
                act.wait_ge(pair_landed[s], 16 * (use + 1))
                if not first:
                    act.wait_ge(stored[s], 32 * use)
                    act.wait_ge(tiles_done, t - 1)
                nc.scalar.activation(count[:, s, :], pair[:, s, :, 0], ACT.Copy).then_inc(counts_ready, 1)
                act.wait_ge(odeg_ready, t + 1)
                nc.scalar.activation(osd[s][:], odeg[s][:], ACT.Sqrt).then_inc(osd_ready, 1)

            split(0, 0, 0, True)
            split(1, 1, 0, True)
            with act.Fori(1, NT // 2) as i:
                for s in range(2):
                    split(2 * i + s, s, i)
            split(NT - 1, 0, NT // 2)
            act.wait_ge(tiles_done, NT)
            nc.scalar.copy(agg[0:D + 2, 0:HALF], acc[0:D + 2, 0:HALF])

        @block.tensor
        def _(pe):
            def multiply(t, s, first=False, ends=False):
                pe.wait_ge(lhs_ready, t + 1)
                pe.wait_ge(counts_ready, t + 1)
                pe.wait_ge(weights_ready, t + 1)
                for lo, hi in BLOCKS:
                    nc.tensor.matmul(acc[0:D + 2, lo:hi], lhs[s][:], count[:, s, lo:hi], start=first, stop=False)
                for lo, hi in BLOCKS:
                    last = nc.tensor.matmul(acc[0:D + 2, lo:hi], lhs_w[:], weight[:, s, lo:hi], start=False, stop=ends)
                last.then_inc(tiles_done, 1)

            multiply(0, 0, True)
            multiply(1, 1)
            with pe.Fori(1, NT // 2) as i:
                for s in range(2):
                    multiply(2 * i + s, s)
            multiply(NT - 1, 0, ends=True)

        @block.vector
        def _(dve):
            for s in range(2):
                nc.vector.memset(lhs[s][:, D:D + 1], 1.0)
                nc.vector.memset(lhs[s][:, D + 1:D + 2], 0.0)
            nc.vector.memset(lhs_w[:, 0:D + 1], 0.0)
            nc.vector.memset(lhs_w[:, D + 1:D + 2], 1.0)
            dve.wait_ge(loaded, 16)

            def scale(t, s, use, first=False):
                dve.wait_ge(pair_landed[s], 16 * (use + 1))
                if not first:
                    dve.wait_ge(stored[s], 32 * use)
                    dve.wait_ge(tiles_done, t - 1)
                nc.vector.tensor_copy(weight[:, s, :], pair[:, s, :, 1]).then_inc(weights_ready, 1)
                dve.wait_ge(counts_ready, t + 1)
                nc.vector.reduce_sum(odeg[s][:], count[:, s, 0:N], axis=AX.X)
                dve.drain()
                nc.vector.tensor_scalar(odeg[s][:], odeg[s][:], 1.0, None, ALU.max).then_inc(odeg_ready, 1)
                dve.wait_ge(osd_ready, t + 1)
                nc.vector.reciprocal(osd[s][:], osd[s][:])
                dve.drain()
                nc.vector.tensor_scalar(lhs[s][:, 0:D], x[:, bass.ds(t, 1), :].squeeze(1), osd[s][:], None,
                                        ALU.mult).then_inc(lhs_ready, 1)

            scale(0, 0, 0, True)
            scale(1, 1, 0, True)
            with dve.Fori(1, NT // 2) as i:
                for s in range(2):
                    scale(2 * i + s, s, i)
            scale(NT - 1, 0, NT // 2)
            dve.wait_ge(tiles_done, NT)
            nc.vector.tensor_copy(agg[0:D + 2, HALF:N], acc[0:D + 2, HALF:N])


def edge_tables(nc, src_i, key, dst_f, w_cols, x_nm, ident, x, lhs_all, weight_parts, ring_col, strip):
    ctx = ExitStack()
    with ctx:
        mem = Phase(nc, ctx, "edge_tables")
        w = mem.sb("w", [P, ET])
        rest = mem.sb("rest", [P, ET])
        part_i = mem.sb("part_i", [P, ET], I32)
        low_i = mem.sb("low_i", [P, ET], I32)
        src_hi = mem.sb("src_hi", [P, ET])
        piece = mem.sb("piece", [P, ET], BF16)
        ones = mem.sb("ones", [1, P])
        count_i = mem.sb("count_i", [P, HALF_P, G], I32)
        count_b = mem.sb("count_b", [P, HALF_P, G], BF16)
        low = mem.sb("low", [P, ET], BF16)
        high = mem.sb("high", [P, ET], BF16)
        hot_lo = [mem.sb(f"hot_lo{s}", [P, HALF_P, G], BF16) for s in range(SLOTS)]
        hot_hi = [mem.sb(f"hot_hi{s}", [P, 2 * NT, G], BF16) for s in range(SLOTS)]
        zero = mem.sb("zero", [P, 1])
        upper = mem.sb("upper", [HALF_P, P])
        halves = mem.sb("halves", [HALF_P, NT, 2])
        start = mem.sb("start", [1, NPAIR])
        turn = mem.sb("turn", [1, NPAIR])
        osd = mem.sb("osd", [P, NT])
        ps_deg = mem.ps("ps_deg", [HALF_P, 2 * NT])
        ps_odeg = mem.ps("ps_odeg", [P, NT])
        ps_base = mem.ps("ps_base", [P, NPAIR])

        loaded = mem.sem("loaded")
        consts_ready = mem.sem("consts_ready")
        ones_ready = mem.sem("ones_ready")
        base_ps = mem.sem("base_ps")
        zero_ready = mem.sem("zero_ready")
        upper_ready = mem.sem("upper_ready")
        hot_ready = mem.sem("hot_ready")
        counted = mem.sem("counted")
        halves_ready = mem.sem("halves_ready")
        odeg_ps = mem.sem("odeg_ps")
        osd_ready = mem.sem("osd_ready")
        block = ctx.enter_context(nc.Block())
        pair_first = dst_f[:].rearrange("p (q k) -> p q k", k=2)[:, :, 0]

        def groups(eng, work):
            for s in range(SLOTS):
                work(s, s)
            with eng.Fori(1, NG // SLOTS) as i:
                for s in range(SLOTS):
                    work(SLOTS * i + s, s)
            for s in range(NG % SLOTS):
                work(NG - NG % SLOTS + s, s)

        @block.sync
        def _(sp):
            sp.dma_start(w[:], w_cols).then_inc(loaded, 16)
            sp.dma_start(x[:], x_nm).then_inc(loaded, 16)

        @block.gpsimd
        def _(pool):
            nc.gpsimd.iota(count_i[:], pattern=[[1, HALF_P], [0, G]], base=0, channel_multiplier=0).then_inc(consts_ready, 1)
            nc.gpsimd.memset(upper[:], 0.0)
            pool.drain()
            nc.gpsimd.affine_select(out=upper[:], in_=upper[:], compare_op=ALU.not_equal, fill=1.0, base=HALF_P,
                                    pattern=[[-1, P]], channel_multiplier=1).then_inc(upper_ready, 1)

        @block.scalar
        def _(act):
            act.wait_ge(zero_ready, 1)
            for t in range(NT):
                nc.scalar.activation(strip[:, :, t, :], zero[:].unsqueeze(2).broadcast_to((P, 2, RING + WINDOW)), ACT.Copy)
            act.wait_ge(odeg_ps, 1)
            nc.scalar.activation(osd[:], ps_odeg[:], ACT.Sqrt).then_inc(osd_ready, 1)

        @block.tensor
        def _(pe):
            pe.wait_ge(ones_ready, 1)
            nc.tensor.matmul(ps_base[:], ones[:], pair_first[0:1], start=True, stop=True).then_inc(base_ps, 1)

            def count(g, s):
                pe.wait_ge(hot_ready, g + 1)
                for k in range(G):
                    first = isinstance(g, int) and g == 0 and k == 0
                    last = isinstance(g, int) and g == NG - 1 and k == G - 1
                    done = nc.tensor.matmul(ps_deg[:], hot_lo[s][:, :, k], hot_hi[s][:, :, k], start=first, stop=last)
                done.then_inc(counted, 1)

            groups(pe, count)
            pe.wait_ge(upper_ready, 1)
            pe.wait_ge(halves_ready, 1)
            nc.tensor.matmul(ps_odeg[:], ident[0:HALF_P, :], halves[:, :, 0], start=True, stop=False)
            nc.tensor.matmul(ps_odeg[:], upper[:], halves[:, :, 1], start=False, stop=True).then_inc(odeg_ps, 1)

        @block.vector
        def _(dve):
            nc.vector.memset(zero[:], 0.0).then_inc(zero_ready, 1)
            nc.vector.memset(ones[:], 1.0).then_inc(ones_ready, 1)
            nc.vector.tensor_scalar(part_i[:], src_i[:], 6, None, ALU.logical_shift_right)
            nc.vector.tensor_scalar(low_i[:], src_i[:], HALF_P - 1, None, ALU.bitwise_and)
            dve.wait_ge(consts_ready, 1)
            nc.vector.tensor_copy(count_b[:], count_i[:])
            dve.drain()
            nc.vector.tensor_copy(high[:], part_i[:])
            nc.vector.tensor_copy(low[:], low_i[:])
            dve.drain()

            def hot_sources(g, s):
                if reaches(g, SLOTS):
                    dve.wait_ge(counted, g - SLOTS + 1)
                for hot, bits, width in ((hot_lo, low, HALF_P), (hot_hi, high, 2 * NT)):
                    last = nc.vector.tensor_tensor(hot[s][:], count_b[:, 0:width, :],
                                                   bits[:, bass.ds(g * G, G)].unsqueeze(1).broadcast_to((P, width, G)), ALU.is_equal)
                last.then_inc(hot_ready, 1)

            groups(dve, hot_sources)
            nc.vector.memset(lhs_all[:, :, D:D + 1], 1.0)
            nc.vector.memset(lhs_all[:, :, D + 1:D + 2], 0.0)
            nc.vector.tensor_scalar(part_i[:], src_i[:], 7, None, ALU.logical_shift_right)
            nc.vector.tensor_scalar(low_i[:], src_i[:], P - 1, None, ALU.bitwise_and)
            nc.vector.tensor_scalar(start[:], pair_first[0:1], float(HALF_BLOCK), None, ALU.add)
            nc.vector.memset(turn[:], 0.0)
            dve.drain()
            nc.vector.tensor_copy(src_hi[:], part_i[:])
            for j in range(1, -(-(N + 3 + HALF_BLOCK) // RING)):
                nc.vector.scalar_tensor_tensor(turn[:], start[:], float(j * RING), turn[:], ALU.is_ge, ALU.add)
                dve.drain()
            nc.vector.scalar_tensor_tensor(start[:], turn[:], -float(RING), start[:], ALU.mult, ALU.add)
            dve.drain()
            nc.vector.tensor_copy(ring_col[:], start[:])
            dve.wait_ge(base_ps, 1)
            nc.vector.tensor_tensor(key[:].rearrange("p (q k) -> p q k", k=2), dst_f[:].rearrange("p (q k) -> p q k", k=2),
                                    ps_base[:].unsqueeze(2).broadcast_to((P, NPAIR, 2)), ALU.subtract)
            dve.drain()
            nc.vector.scalar_tensor_tensor(key[:], src_hi[:], float(WINDOW), key[:], ALU.mult, ALU.add)
            nc.vector.tensor_copy(dst_f[:], low_i[:])
            dve.drain()
            nc.vector.tensor_scalar(key[:], key[:], -float(CENTRE), None, ALU.add)
            dve.wait_ge(counted, NG)
            nc.vector.tensor_scalar(halves[:].rearrange("p t h -> p (t h)"), ps_deg[:], 1.0, None, ALU.max).then_inc(halves_ready, 1)
            dve.wait_ge(loaded, 32)
            nc.vector.tensor_copy(piece[:], w[:])
            dve.drain()
            nc.vector.tensor_copy(weight_parts[:, 0, :], piece[:])
            nc.vector.tensor_tensor(rest[:], w[:], piece[:], ALU.subtract)
            dve.drain()
            nc.vector.tensor_copy(piece[:], rest[:])
            dve.drain()
            nc.vector.tensor_copy(weight_parts[:, 1, :], piece[:])
            nc.vector.tensor_tensor(weight_parts[:, 2, :], rest[:], piece[:], ALU.subtract)
            dve.wait_ge(osd_ready, 1)
            nc.vector.reciprocal(osd[:], osd[:])
            dve.drain()
            nc.vector.tensor_tensor(lhs_all[:, :, 0:D], x[:], per_node(osd[:]), ALU.mult)


def add_edges(nc, place, src_lo, weight_parts, ring_col, lhs_all, strip, adj_count, adj_weight, agg):
    ctx = ExitStack()
    with ctx:
        mem = Phase(nc, ctx, "add_edges")
        lane_i = mem.sb("lane_i", [P, P], I32)
        lane_of = mem.sb("lane_of", [P, P], BF16)
        place_i = mem.sb("place_i", [P, PLACES], I32)
        place_of = mem.sb("place_of", [P, PLACES], BF16)
        hot_lo = [mem.sb(f"hot_lo{s}", [P, 2, 4, P], BF16) for s in range(SLOTS)]
        hot = [mem.sb(f"hot{s}", [P, 2, PLACES], BF16) for s in range(SLOTS)]
        lhs_w = mem.sb("lhs_w", [P, D + 2])
        ps_pair = [mem.ps(f"ps_pair{s}", [P, 2, BANK]) for s in range(2)]
        acc = [mem.ps(f"acc{s}", [D + 2, BANK]) for s in range(2)]

        iota_ready = mem.sem("iota_ready")
        lo_ready = mem.sem("lo_ready")
        hot_ready = mem.sem("hot_ready")
        parts_ready = mem.sem("parts_ready")
        multiplied = mem.sem("multiplied")
        added = mem.sem("added")
        block_done = mem.sem("block_done")
        block_multiplied = mem.sem("block_multiplied")
        acc_read = mem.sem("acc_read")
        stored = [mem.sem(f"stored{q}") for q in range(SLOTS_B)]
        cleared = mem.sem("cleared")
        past_waits = mem.sem("past_waits")
        block = ctx.enter_context(nc.Block())
        count_rows = adj_count.rearrange("(t p) c -> p t c", p=P)
        weight_rows = adj_weight.rearrange("(t p) c -> p t c", p=P)

        def nothing(*_):
            pass

        def rounds(eng, begin, pair, step):
            def one(i, r, pairs, drains):
                begin(i, r)
                for u in range(pairs):
                    pair(i, r, u)
                    if drains:
                        for t in range(NT * u // pairs, NT * (u + 1) // pairs):
                            step(i, r, t)

            for r in range(SLOTS_B):
                one(0, r, ROUND, r > 0)
            with eng.Fori(1, NROUND // SLOTS_B) as i:
                for r in range(SLOTS_B):
                    one(i, r, ROUND, True)
            i = NROUND // SLOTS_B
            for r in range(NROUND % SLOTS_B):
                one(i, r, min(ROUND, NPAIR - (SLOTS_B * i + r) * ROUND), True)
            r = NROUND % SLOTS_B
            begin(i, r)
            for t in range(NT):
                step(i, r, t)

        def slot(q):
            return slice(q * BLOCK, (q + 1) * BLOCK)

        def nodes(b):
            if not isinstance(b, int):
                return BLOCK * b - HALF_BLOCK, BLOCK, 0
            lo = max(0, BLOCK * b - HALF_BLOCK)
            return lo, min(COLS, BLOCK * b + HALF_BLOCK) - lo, lo - (BLOCK * b - HALF_BLOCK)

        @block.sync
        def _(sp):
            def store(i, q):
                b = SLOTS_B * i + q
                lo, width, off = nodes(b)
                sp.wait_ge(block_done, b + 1)
                for table, rows in ((0, count_rows), (1, weight_rows)):
                    sp.dma_start(rows[:, :, bass.ds(lo, width)],
                                 strip[:, table, :, q * BLOCK + off:q * BLOCK + off + width]).then_inc(stored[q], 16)

            for q in range(SLOTS_B):
                store(0, q)
            with sp.Fori(1, NROUND // SLOTS_B) as i:
                for q in range(SLOTS_B):
                    store(i, q)
            for q in range(NROUND % SLOTS_B):
                store(NROUND // SLOTS_B, q)
            for q in range(SLOTS_B):
                sp.wait_ge(stored[q], 32 * -(-(NROUND - q) // SLOTS_B))

        @block.gpsimd
        def _(pool):
            nc.gpsimd.iota(lane_i[:], pattern=[[1, P]], base=0, channel_multiplier=0)
            nc.gpsimd.iota(place_i[:], pattern=[[1, PLACES]], base=-CENTRE, channel_multiplier=0).then_inc(iota_ready, 1)

            def clear(i, q):
                pool.wait_ge(stored[q], 32 * (i + 1))
                pool.wait_ge(block_multiplied, SLOTS_B * i + q + 1)
                pool.sem_inc(past_waits, 1)
                nc.gpsimd.memset(strip[:, :, :, slot(q)], 0.0).then_inc(cleared, 1)

            full, left = divmod(NROUND - SLOTS_B, SLOTS_B)
            with pool.Fori(0, full) as i:
                for q in range(SLOTS_B):
                    clear(i, q)
            for q in range(left):
                clear(full, q)

        @block.scalar
        def _(act):
            def read_sums(i, r):
                b = SLOTS_B * i + r - 2
                lo, width, off = nodes(b)
                if isinstance(b, int):
                    width = min(N, lo + width) - lo
                act.wait_ge(block_multiplied, b + 1)
                nc.scalar.activation(agg[0:D + 2, bass.ds(lo, width)], acc[r % 2][:, off:off + width], ACT.Copy).then_inc(acc_read, 1)

            def pair(i, r, u):
                p = (SLOTS_B * i + r) * ROUND + u
                s = u % SLOTS
                act.wait_ge(lo_ready, p + 1)
                for k in range(2):
                    for part in range(3 - u % 2 * k):
                        last = nc.scalar.activation(hot_lo[s][:, k, 1 + part, :], hot_lo[s][:, k, 0, :], ACT.Copy,
                                                    scale=weight_parts[:, part, bass.ds(2 * p + k, 1)])
                last.then_inc(parts_ready, 1)
                if u == 1 and reaches(SLOTS_B * i + r, 2):
                    read_sums(i, r)

            rounds(act, nothing, pair, nothing)
            i, r = divmod(NROUND, SLOTS_B)
            read_sums(i, r)
            read_sums(i, r + 1)

        @block.tensor
        def _(pe):
            def pair(i, r, u):
                p = (SLOTS_B * i + r) * ROUND + u
                s = u % SLOTS
                pe.wait_ge(hot_ready, p + 1)
                pe.wait_ge(parts_ready, p + 1)
                if reaches(p, 2):
                    pe.wait_ge(added, p - 1)
                out = ps_pair[u % 2]
                for k in range(2):
                    nc.tensor.matmul(out[:, 0, 0:PLACES], hot_lo[s][:, k, 0, :], hot[s][:, k, :], start=k == 0, stop=k == 1)
                    for part in range(3):
                        last = nc.tensor.matmul(out[:, 1, 0:PLACES], hot_lo[s][:, k, 1 + part, :], hot[s][:, k, :],
                                                start=k == 0 and part == 0, stop=k == 1 and part == 2)
                last.then_inc(multiplied, 1)

            def step(i, r, t):
                b = SLOTS_B * i + r - 1
                out = acc[(r - 1) % 2]
                if t == 0:
                    pe.wait_ge(block_done, b + 1)
                    if reaches(b, 2):
                        pe.wait_ge(acc_read, b - 1)
                nc.tensor.matmul(out[:, 0:BLOCK], lhs_all[:, t, :], strip[:, 0, t, slot((r - 1) % SLOTS_B)], start=t == 0, stop=False)
                last = nc.tensor.matmul(out[:, 0:BLOCK], lhs_w[:], strip[:, 1, t, slot((r - 1) % SLOTS_B)], start=False, stop=t == NT - 1)
                if t == NT - 1:
                    last.then_inc(block_multiplied, 1)

            rounds(pe, nothing, pair, step)

        @block.vector
        def _(dve):
            nc.vector.memset(lhs_w[:, 0:D + 1], 0.0)
            nc.vector.memset(lhs_w[:, D + 1:D + 2], 1.0)
            dve.wait_ge(iota_ready, 1)
            nc.vector.tensor_copy(lane_of[:], lane_i[:])
            nc.vector.tensor_copy(place_of[:], place_i[:])
            dve.drain()

            def one_hots(p, s):
                if reaches(p, SLOTS):
                    dve.wait_ge(multiplied, p - SLOTS + 1)
                for k in range(2):
                    last = nc.vector.tensor_scalar(hot_lo[s][:, k, 0, :], lane_of[:], src_lo[:, bass.ds(2 * p + k, 1)], None, ALU.is_equal)
                last.then_inc(lo_ready, 1)
                if s % 2 == 1:
                    nc.vector.tensor_scalar(hot_lo[s][:, 1, 3, :], lane_of[:], src_lo[:, bass.ds(2 * p + 1, 1)],
                                            weight_parts[:, 2, bass.ds(2 * p + 1, 1)], ALU.is_equal, ALU.mult)
                for k in range(2):
                    last = nc.vector.tensor_scalar(hot[s][:, k, :], place_of[:], place[:, bass.ds(2 * p + k, 1)], None, ALU.is_equal)
                last.then_inc(hot_ready, 1)

            def begin(i, r):
                w = SLOTS_B * i + r
                if reaches(w, 1):
                    dve.drain()
                    if r == 1:
                        nc.vector.tensor_tensor(strip[:, :, :, 0:WINDOW], strip[:, :, :, 0:WINDOW], strip[:, :, :, RING:RING + WINDOW], ALU.add)
                        dve.drain()
                        nc.vector.memset(strip[:, :, :, RING:RING + WINDOW], 0.0)
                        dve.drain()
                    dve.sem_inc(block_done, 1)
                if reaches(w, SLOTS_B - 1) and not (isinstance(w, int) and w >= NROUND - 1):
                    dve.wait_ge(cleared, w - SLOTS_B + 2)

            def pair(i, r, u):
                p = (SLOTS_B * i + r) * ROUND + u
                if not isinstance(p, int) or p + AHEAD < NPAIR:
                    one_hots(p + AHEAD, (u + AHEAD) % SLOTS)
                at = dve.value_load(ring_col[0:1, bass.ds(p, 1)], min_val=0, max_val=RING - 1)
                cells = strip[:, :, :, bass.ds(at, WINDOW)]
                if reaches(p, 1):
                    dve.wait_ge(added, p)
                dve.wait_ge(multiplied, p + 1)
                nc.vector.tensor_tensor(cells, cells, ps_pair[u % 2][:, :, 0:PLACES].rearrange("p c (t n) -> p c t n", n=WINDOW),
                                        ALU.add).then_inc(added, 1)

            for p in range(AHEAD):
                one_hots(p, p)
            rounds(dve, begin, pair, nothing)


def first_layer_out(nc, ws, biases, ident, adj_weight, x, agg, w_deg, eps):
    ctx = ExitStack()
    with ctx:
        mem = Phase(nc, ctx, "first_layer_out")
        xT = mem.sb("xT", [D, NPAD])
        xw = mem.sb("xw", [P, NT, D])
        w0 = mem.sb("w0", [D, D])
        bias = mem.sb("bias0", [P, D])
        degs = mem.sb("degs", [P, NT, 2])
        loop = mem.sb("loop", [P, NT, P])
        has_in = mem.sb("has_in", [P, NT])
        no_in = mem.sb("no_in", [P, NT])
        cj = mem.sb("cj", [P, NT])
        stats = (mem.sb("st", [P, NT, 6]), mem.sb("dif", [P, NT]), mem.sb("var", [P, NT]))
        mean = mem.sb("mean", [P, NT])
        sd = mem.sb("sd", [P, NT])
        acc = mem.ps("acc", [P, NB * BANK])
        small = mem.ps("small", [P, NT, 2])
        loaded = mem.sem("loaded")
        set_up = mem.sem("set_up")
        loop_landed = mem.sem("loop_landed")
        loop_ready = mem.sem("loop_ready")
        loop_stored = mem.sem("loop_stored")
        xT_ps = mem.sem("xT_ps")
        xT_ready = mem.sem("xT_ready")
        xw_ps = mem.sem("xw_ps")
        xw_ready = mem.sem("xw_ready")
        deg_ps = mem.sem("deg_ps")
        cj_max = mem.sem("cj_max")
        cj_sqrt = mem.sem("cj_sqrt")
        out_ps = mem.sem("out_ps")
        var_ready = mem.sem("var_ready")
        sd_ready = mem.sem("sd_ready")
        block = ctx.enter_context(nc.Block())

        @block.sync
        def _(sp):
            sp.dma_start(w0[:], ws).then_inc(loaded, 16)
            sp.dma_start(bias[:], biases.partition_broadcast(P)).then_inc(loaded, 16)
            blocks = adj_weight.rearrange("n c -> (n c)")[0:(NT - 1) * (P * COLS + P)].rearrange("(t m) -> t m", t=NT - 1)
            whole = blocks[:, 0:P * COLS].rearrange("t (p c) -> p t c", p=P)[:, :, 0:P]
            rest = adj_weight[N - LAST:N, N - LAST:N]
            sp.dma_start(loop[:, 0:NT - 1, :], whole).then_inc(loop_landed, 16)
            sp.dma_start(loop[0:LAST, NT - 1, 0:LAST], rest).then_inc(loop_landed, 16)
            sp.wait_ge(loop_ready, 1)
            sp.dma_start(whole, loop[:, 0:NT - 1, :]).then_inc(loop_stored, 16)
            sp.dma_start(rest, loop[0:LAST, NT - 1, 0:LAST]).then_inc(loop_stored, 16)
            sp.wait_ge(loop_stored, 32)

        @block.scalar
        def _(act):
            act.wait_ge(xT_ps, 1)
            nc.scalar.copy(xT[:], acc[0:D, 0:NPAD]).then_inc(xT_ready, 1)
            act.wait_ge(cj_max, 1)
            nc.scalar.activation(cj[:], cj[:], ACT.Sqrt).then_inc(cj_sqrt, 1)
            act.wait_ge(var_ready, 1)
            nc.scalar.activation(sd[:], stats[2][:], ACT.Sqrt, bias=eps[:, 0:1]).then_inc(sd_ready, 1)

        @block.tensor
        def _(pe):
            for t in range(NT):
                last = nc.tensor.transpose(acc[0:D, t * P:(t + 1) * P], x[:, t, :], ident[:])
            last.then_inc(xT_ps, 1)
            pe.wait_ge(set_up, 1)
            for t in range(NT):
                last = nc.tensor.matmul(small[:, t, :], agg[D:D + 2, t * P:(t + 1) * P], ident[D:D + 2, D:D + 2],
                                        start=True, stop=True)
            last.then_inc(deg_ps, 1)
            pe.wait_ge(loaded, 32)
            pe.wait_ge(xT_ready, 1)
            for t in range(NT):
                at = node_cols(t)
                last = nc.tensor.matmul(acc[:, at:at + D], xT[:, t * P:(t + 1) * P], w0[:], start=True, stop=True)
            last.then_inc(xw_ps, 1)
            pe.wait_ge(xw_ready, 1)
            for t in range(NT):
                at = node_cols(t)
                last = nc.tensor.matmul(acc[:, at:at + D], agg[0:D, t * P:(t + 1) * P], w0[:], start=True, stop=True)
            last.then_inc(out_ps, 1)

        @block.vector
        def _(dve):
            nc.vector.memset(agg[0:D + 2, N:NPAD], 0.0).then_inc(set_up, 1)
            dve.wait_ge(loaded, 32)
            dve.wait_ge(deg_ps, 1)
            nc.vector.tensor_copy(degs[:], small[:])
            dve.drain()
            nc.vector.tensor_copy(w_deg[:], degs[:, :, 1])
            nc.vector.tensor_scalar(has_in[:], degs[:, :, 0], 0.0, None, ALU.is_gt)
            nc.vector.tensor_scalar(no_in[:], degs[:, :, 0], 0.0, None, ALU.is_le)
            nc.vector.tensor_scalar(cj[:], degs[:, :, 0], 1.0, None, ALU.max).then_inc(cj_max, 1)
            dve.drain()
            dve.wait_ge(xw_ps, 1)
            nc.vector.tensor_tensor(by_node(xw), node_major_by_node(acc), per_node_in_bank(no_in[:]), ALU.mult).then_inc(xw_ready, 1)
            nc.vector.tensor_tensor(x[:], x[:], per_feature(bias[:]), ALU.add)
            dve.wait_ge(loop_landed, 32)
            nc.vector.tensor_tensor(loop[:, 0:NT - 1, :], loop[:, 0:NT - 1, :], ident[:].unsqueeze(1).broadcast_to((P, NT - 1, P)), ALU.add)
            nc.vector.tensor_tensor(loop[0:LAST, NT - 1, 0:LAST], loop[0:LAST, NT - 1, 0:LAST], ident[0:LAST, 0:LAST],
                                    ALU.add).then_inc(loop_ready, 1)
            dve.drain()
            nc.vector.tensor_tensor(x[:], xw[:], x[:], ALU.add)
            dve.wait_ge(cj_sqrt, 1)
            nc.vector.reciprocal(cj[:], cj[:])
            dve.drain()
            nc.vector.tensor_tensor(cj[:], cj[:], has_in[:], ALU.mult)
            dve.drain()
            dve.wait_ge(out_ps, 1)
            nc.vector.tensor_tensor(by_node(xw), node_major_by_node(acc), per_node_in_bank(cj[:]), ALU.mult)
            dve.drain()
            nc.vector.tensor_tensor(xw[:], xw[:], x[:], ALU.add)
            dve.drain()
            layer_norm(nc, dve, stats, xw, x, mean, sd, var_ready, sd_ready, 1)
            dve.drain()


def convolutions(nc, adj_count, adj_weight, weights, rows, columns, ident, x, w_deg, eps):
    W_PASSES, C_PASSES = 3, 2
    C_SLOTS = PB
    NG_READY = NT // PB
    ctx = ExitStack()
    with ctx:
        mem = Phase(nc, ctx, "convolutions")
        table = mem.sb("table", [P, C_SLOTS, COLS])
        g = mem.sb("g", [P, NT, D])
        tmp = mem.sb("tmp", [P, NT, D])
        agg = mem.sb("agg2", [D, NPAD])
        xT = mem.sb("xT2", [D, NPAD])
        lhs = [mem.sb(f"clhs{j}", [P, D]) for j in range(C_SLOTS)]
        wsb = [mem.sb(f"cw{k}", [D, D]) for k in range(W_PASSES + C_PASSES)]
        bias_row = [mem.sb(f"cb{k}", [P, D]) for k in range(W_PASSES)]
        cols = mem.sb("cols", [D, 8])
        zero = mem.sb("zero2", [P, BANK], BF16)
        dis = mem.sb("dis", [P, NT])
        pos = mem.sb("pos", [P, NT])
        stats = (mem.sb("st2", [P, NT, 6]), mem.sb("dif2", [P, NT]), mem.sb("var2", [P, NT]))
        mean = mem.sb("mean2", [P, NT])
        sd = mem.sb("sd2", [P, NT])
        gst = mem.sb("gst", [D, NB, 6])
        gmv = mem.sb("gmv", [D, 2])
        gs = mem.sb("gs", [D, 8])
        acc = mem.ps("acc2", [P, NB * BANK])

        loaded = mem.sem("loaded")
        set_up = mem.sem("set_up")
        dis_max = mem.sem("dis_max")
        dis_sqrt = mem.sem("dis_sqrt")
        table_landed = [mem.sem(f"table_landed{j}") for j in range(C_SLOTS)]
        g_ready = mem.sem("g_ready")
        lhs_ready = mem.sem("lhs_ready")
        tiles_done = mem.sem("tiles_done")
        sums_ready = mem.sem("sums_ready")
        agg_ready = mem.sem("agg_ready")
        product_ps = mem.sem("product_ps")
        product_read = mem.sem("product_read")
        gvar_ready = mem.sem("gvar_ready")
        gsd_ready = mem.sem("gsd_ready")
        gscale_ready = mem.sem("gscale_ready")
        relu_ready = mem.sem("relu_ready")
        hT_ready = mem.sem("hT_ready")
        turned_ps = mem.sem("turned_ps")
        turned_read = mem.sem("turned_read")
        var_ready = mem.sem("var_ready")
        sd_ready = mem.sem("sd_ready")
        block = ctx.enter_context(nc.Block())
        PASSES = W_PASSES + C_PASSES
        tables = [adj_weight] * W_PASSES + [adj_count] * C_PASSES

        @block.sync
        def _(sp):
            for k in range(PASSES):
                sp.dma_start(wsb[k][:], weights[k]).then_inc(loaded, 16)
            for k in range(W_PASSES):
                sp.dma_start(bias_row[k][:], rows[k].partition_broadcast(P)).then_inc(loaded, 16)
            for k in range(8):
                sp.dma_start(cols[:, k:k + 1], columns[k].unsqueeze(1)).then_inc(loaded, 16)

            def load(k, i, j):
                tile = tables[k].rearrange("(t p) c -> t p c", p=P)[bass.ds(C_SLOTS * i + j, 1)].squeeze(0)
                sp.dma_start(table[:, j, 0:N], tile[:, 0:N]).then_inc(table_landed[j], 16)

            for j in range(C_SLOTS):
                load(0, 0, j)
            for k in range(PASSES):
                with sp.Fori(1 if k == 0 else 0, NT // C_SLOTS) as i:
                    for j in range(C_SLOTS):
                        sp.wait_ge(tiles_done, k * NT + C_SLOTS * i + j - C_SLOTS + 1)
                        load(k, i, j)

        @block.scalar
        def _(act):
            act.wait_ge(dis_max, 1)
            nc.scalar.activation(dis[:], dis[:], ACT.Sqrt).then_inc(dis_sqrt, 1)

            for k in range(PASSES):
                def hand_over(i):
                    act.wait_ge(g_ready, NG_READY * k + i + 1)
                    for j in range(C_SLOTS):
                        if not (k == 0 and isinstance(i, int)):
                            act.wait_ge(tiles_done, k * NT + C_SLOTS * i + j - C_SLOTS + 1)
                        nc.scalar.copy(lhs[j][:], g[:, bass.ds(C_SLOTS * i + j, 1), :].squeeze(1)).then_inc(lhs_ready, 1)

                hand_over(0)
                with act.Fori(1, NT // C_SLOTS) as i:
                    hand_over(i)
                act.wait_ge(sums_ready, k + 1)
                nc.scalar.copy(agg[:, 0:HALF], acc[0:D, 0:HALF]).then_inc(agg_ready, 1)
                if k >= W_PASSES:
                    n = k - W_PASSES
                    act.wait_ge(gvar_ready, n + 1)
                    nc.scalar.activation(gs[:, 1:2], gs[:, 0:1], ACT.Sqrt, bias=eps[0:D, 1:2]).then_inc(gsd_ready, 1)
                    act.wait_ge(gscale_ready, n + 1)
                    for lo, hi in ((0, HALF), (HALF, N)):
                        nc.scalar.activation(agg[:, lo:hi], acc[0:D, lo:hi], ACT.Relu, bias=gs[:, 4:5],
                                             scale=gs[:, 3:4]).then_inc(relu_ready, 1)
                if k in (W_PASSES - 1, PASSES - 1):
                    act.wait_ge(var_ready, 1 if k < W_PASSES else 2)
                    nc.scalar.activation(sd[:], stats[2][:], ACT.Sqrt, bias=eps[:, 0:1]).then_inc(sd_ready, 1)

        @block.tensor
        def _(pe):
            pe.wait_ge(loaded, 16 * (PASSES + W_PASSES + 8))
            pe.wait_ge(set_up, 1)
            products = turns = 0
            for k in range(PASSES):
                if products:
                    pe.wait_ge(product_read, min(products, W_PASSES))
                if turns:
                    pe.wait_ge(turned_read, turns)
                for lo, hi in BLOCKS:
                    nc.tensor.matmul(acc[0:D, lo:hi], zero[:, 0:D], zero[:, 0:hi - lo], start=True, stop=False)
                with pe.Fori(0, NT // C_SLOTS) as i:
                    for j in range(C_SLOTS):
                        pe.wait_ge(table_landed[j], 16 * (k * (NT // C_SLOTS) + i + 1))
                        pe.wait_ge(lhs_ready, k * NT + C_SLOTS * i + j + 1)
                        for lo, hi in BLOCKS:
                            last = nc.tensor.matmul(acc[0:D, lo:hi], lhs[j][:], table[:, j, lo:hi], start=False, stop=False)
                        last.then_inc(tiles_done, 1)
                for lo, hi in BLOCKS:
                    last = nc.tensor.matmul(acc[0:D, lo:hi], zero[:, 0:D], zero[:, 0:hi - lo], start=False, stop=True)
                last.then_inc(sums_ready, 1)
                pe.wait_ge(agg_ready, 2 * (k + 1))
                products += 1
                if k < W_PASSES:
                    for t in range(NT):
                        at = node_cols(t)
                        last = nc.tensor.matmul(acc[:, at:at + D], agg[:, t * P:(t + 1) * P], wsb[k][:], start=True, stop=True)
                        if t % PB == PB - 1:
                            last.then_inc(product_ps, 1)
                else:
                    for lo, hi in BLOCKS:
                        nc.tensor.matmul(acc[0:D, lo:hi], wsb[k][:], agg[:, lo:hi], start=True, stop=True).then_inc(product_ps, 1)
                if k == W_PASSES - 1:
                    pe.wait_ge(g_ready, NG_READY * (k + 2))
                    pe.wait_ge(product_read, products)
                    for t in range(NT):
                        last = nc.tensor.transpose(acc[0:D, t * P:(t + 1) * P], x[:, t, :], ident[:])
                    last.then_inc(turned_ps, 1)
                    turns += 1
                if k >= W_PASSES:
                    for t in range(NT):
                        if t * P in (0, HALF):
                            pe.wait_ge(hT_ready, 2 * (k - W_PASSES) + 1 + t * P // HALF)
                        at = node_cols(t)
                        last = nc.tensor.transpose(acc[:, at:at + D], agg[:, t * P:(t + 1) * P], ident[0:D, 0:D])
                    last.then_inc(turned_ps, 1)
                    turns += 1

        @block.vector
        def _(dve):
            nc.vector.memset(zero[:], 0.0)
            nc.vector.memset(agg[:, N:NPAD], 0.0)
            nc.vector.tensor_scalar(w_deg[:], w_deg[:], 1.0, None, ALU.add)
            dve.drain()
            nc.vector.tensor_scalar(pos[:], w_deg[:], 0.0, None, ALU.is_gt)
            nc.vector.tensor_scalar(dis[:], w_deg[:], 1e-30, None, ALU.max).then_inc(dis_max, 1)
            dve.drain()
            dve.sem_inc(set_up, 1)
            dve.wait_ge(dis_sqrt, 1)
            nc.vector.reciprocal(dis[:], dis[:])
            dve.drain()
            nc.vector.tensor_tensor(dis[:], dis[:], pos[:], ALU.mult)
            dve.drain()
            nc.vector.tensor_tensor(g[:], x[:], per_node(dis[:]), ALU.mult).then_inc(g_ready, NG_READY)
            dve.wait_ge(loaded, 16 * (PASSES + W_PASSES + 8))

            for k in range(PASSES):
                dve.wait_ge(sums_ready, k + 1)
                nc.vector.tensor_copy(agg[:, HALF:N], acc[0:D, HALF:N]).then_inc(agg_ready, 1)
                if k < W_PASSES:
                    def tiles(tile, b):
                        return tile[:, PB * b:PB * (b + 1), :]

                    def scale(b):
                        dve.wait_ge(product_ps, NT // PB * k + b + 1)
                        done = nc.vector.tensor_tensor(tiles(tmp, b), acc[:, b * BANK:b * BANK + PB * D].rearrange("p (j d) -> p j d", d=D),
                                                       dis[:, PB * b:PB * (b + 1)].unsqueeze(2).broadcast_to((P, PB, D)), ALU.mult)
                        if b == NT // PB - 1:
                            done.then_inc(product_read, 1)

                    def shift(b):
                        nc.vector.tensor_tensor(tiles(tmp, b), tiles(tmp, b), bias_row[k][:].unsqueeze(1).broadcast_to((P, PB, D)), ALU.add)

                    def finish(b):
                        if k < W_PASSES - 1:
                            nc.vector.scalar_tensor_tensor(tiles(g, b), tiles(tmp, b), 0.0,
                                                           dis[:, PB * b:PB * (b + 1)].unsqueeze(2).broadcast_to((P, PB, D)),
                                                           ALU.max, ALU.mult).then_inc(g_ready, 1)
                        else:
                            nc.vector.tensor_tensor(tiles(tmp, b), tiles(tmp, b), tiles(x, b), ALU.add)

                    for b in range(NT // PB + 2):
                        if b < NT // PB:
                            scale(b)
                        if 1 <= b <= NT // PB:
                            shift(b - 1)
                        if b >= 2:
                            finish(b - 2)
                        dve.drain()
                    if k == W_PASSES - 1:
                        layer_norm(nc, dve, stats, tmp, x, mean, sd, var_ready, sd_ready, 1)
                        dve.drain()
                        nc.vector.tensor_copy(g[:], x[:]).then_inc(g_ready, NG_READY)
                        dve.wait_ge(turned_ps, 1)
                        nc.vector.tensor_copy(xT[:], acc[0:D, 0:NPAD]).then_inc(turned_read, 1)
                        dve.drain()
                    continue
                n = k - W_PASSES
                b, gw, gb, ga = (cols[:, 4 * n + c:4 * n + c + 1] for c in range(4))
                for c, (lo, hi) in enumerate(BLOCKS):
                    dve.wait_ge(product_ps, NT // PB * W_PASSES + NB * n + c + 1)
                    nc.vector.bn_stats(gst[:, c, :], acc[0:D, lo:hi])
                dve.drain()
                nc.vector.bn_aggr(gmv[:], gst[:].rearrange("p c s -> p (c s)"))
                dve.drain()
                nc.vector.tensor_tensor(gs[:, 5:6], gmv[:, 0:1], b, ALU.add)
                dve.drain()
                nc.vector.tensor_tensor(gs[:, 6:7], gs[:, 5:6], ga, ALU.mult)
                dve.drain()
                nc.vector.tensor_tensor(gs[:, 7:8], gs[:, 5:6], gs[:, 6:7], ALU.subtract)
                dve.drain()
                nc.vector.tensor_tensor(gs[:, 7:8], gs[:, 7:8], gs[:, 7:8], ALU.mult)
                dve.drain()
                nc.vector.tensor_tensor(gs[:, 0:1], gs[:, 7:8], gmv[:, 1:2], ALU.add).then_inc(gvar_ready, 1)
                dve.wait_ge(gsd_ready, n + 1)
                nc.vector.reciprocal(gs[:, 2:3], gs[:, 1:2])
                dve.drain()
                nc.vector.tensor_tensor(gs[:, 3:4], gs[:, 2:3], gw, ALU.mult)
                nc.vector.tensor_tensor(gs[:, 4:5], b, gs[:, 6:7], ALU.subtract)
                dve.drain()
                nc.vector.tensor_tensor(gs[:, 4:5], gs[:, 4:5], gs[:, 3:4], ALU.mult)
                dve.drain()
                nc.vector.tensor_tensor(gs[:, 4:5], gs[:, 4:5], gb, ALU.add).then_inc(gscale_ready, 1)
                for h, (lo, hi) in enumerate(((0, HALF), (HALF, N))):
                    dve.wait_ge(relu_ready, 2 * n + h + 1)
                    nc.vector.tensor_tensor(agg[:, lo:hi], agg[:, lo:hi], xT[:, lo:hi], ALU.add).then_inc(hT_ready, 1)
                dve.drain()
                if n == 0:
                    nc.vector.tensor_copy(xT[:, 0:N], agg[:, 0:N])
                    dve.wait_ge(turned_ps, 2)
                    nc.vector.tensor_copy(by_bank(g), node_major(acc)).then_inc(turned_read, 1)
                    dve.drain()
                    dve.sem_inc(g_ready, NG_READY)
                else:
                    dve.wait_ge(turned_ps, 3)
                    nc.vector.tensor_copy(by_bank(tmp), node_major(acc)).then_inc(turned_read, 1)
                    dve.drain()
                    nc.vector.tensor_tensor(tmp[:], tmp[:], x[:], ALU.add)
                    dve.drain()
                    layer_norm(nc, dve, stats, tmp, x, mean, sd, var_ready, sd_ready, 2)
                    dve.drain()


def examine_edges(nc, src_i, dst_i, dst_cols, src_cols, dst_flat, dstf_dram, key, dst_f, rel, node_in_window, first_node, is_sorted, ident, eps):
    ctx = ExitStack()
    with ctx:
        mem = Phase(nc, ctx, "examine_edges")
        srcf = mem.sb("srcf", [P, ET])
        fdst_i = mem.sb("fdst_i", [P, ET], I32)
        fdst = mem.sb("fdst", [P, ET])
        lane_i = mem.sb("lane_i", [P, 1], I32)
        lane = mem.sb("lane", [P, 1])
        block_i = mem.sb("block_i", [P, NROUND, 2 * ROUND], I32)
        block_f = mem.sb("block_f", [P, NROUND, 2 * ROUND])
        ones = mem.sb("wones", [P, P])
        first = mem.sb("first", [P, ET])
        slack = mem.sb("slack", [P, 6, ET])
        least = mem.sb("least", [P, 6])
        outside = mem.sb("outside", [P, 6])
        ps_first = mem.ps("ps_first", [P, 2 * BANK])
        ps_out = mem.ps("ps_out", [1, 6])
        loaded = mem.sem("loaded")
        consts_ready = mem.sem("consts_ready")
        dst_ready = mem.sem("dst_ready")
        flat_loaded = mem.sem("flat_loaded")
        flat_ready = mem.sem("flat_ready")
        flat_stored = mem.sem("flat_stored")
        first_ps = mem.sem("first_ps")
        outside_ready = mem.sem("outside_ready")
        out_ps = mem.sem("out_ps")
        block = ctx.enter_context(nc.Block())

        @block.sync
        def _(sp):
            sp.dma_start(dst_i[:], dst_cols).then_inc(loaded, 16)
            sp.dma_start(src_i[:], src_cols).then_inc(loaded, 16)
            sp.dma_start(fdst_i[:], dst_flat).then_inc(flat_loaded, 16)
            sp.wait_ge(flat_ready, 1)
            sp.dma_start(dstf_dram.rearrange("(p a) -> p a", p=P), fdst[:]).then_inc(flat_stored, 16)
            sp.wait_ge(flat_stored, 16)

        @block.gpsimd
        def _(pool):
            nc.gpsimd.iota(lane_i[:], pattern=[[1, 1]], base=0, channel_multiplier=1)
            nc.gpsimd.iota(block_i[:], pattern=[[BLOCK, NROUND], [0, 2 * ROUND]], base=0, channel_multiplier=0)
            nc.gpsimd.memset(ident[:], 0.0)
            pool.drain()
            nc.gpsimd.affine_select(out=ident[:], in_=ident[:], compare_op=ALU.not_equal, fill=1.0, base=0,
                                    pattern=[[-1, P]], channel_multiplier=1).then_inc(consts_ready, 1)

        @block.tensor
        def _(pe):
            pe.wait_ge(dst_ready, 1)
            nc.tensor.matmul(ps_first[:, 0:BANK], ones[0:1, :], dst_f[0:1, 0:BANK], start=True, stop=True)
            nc.tensor.matmul(ps_first[:, BANK:ET], ones[0:1, :], dst_f[0:1, BANK:ET], start=True, stop=True).then_inc(first_ps, 1)
            pe.wait_ge(outside_ready, 1)
            nc.tensor.matmul(ps_out[:], ones[:, 0:1], outside[:], start=True, stop=True).then_inc(out_ps, 1)

        @block.vector
        def _(dve):
            nc.vector.memset(ones[:], 1.0)
            nc.vector.memset(eps[:, 0:1], LN_EPS)
            nc.vector.memset(eps[:, 1:2], GN_EPS)
            nc.vector.memset(slack[:], 0.0)
            dve.wait_ge(loaded, 32)
            nc.vector.tensor_copy(srcf[:], src_i[:])
            nc.vector.tensor_copy(dst_f[:], dst_i[:]).then_inc(dst_ready, 1)
            dve.wait_ge(flat_loaded, 16)
            nc.vector.tensor_copy(fdst[:], fdst_i[:]).then_inc(flat_ready, 1)
            dve.wait_ge(consts_ready, 1)
            nc.vector.tensor_copy(lane[:], lane_i[:])
            nc.vector.tensor_copy(block_f[:], block_i[:])
            dve.wait_ge(first_ps, 1)
            nc.vector.tensor_copy(first[:], ps_first[:, 0:ET])
            dve.drain()
            nc.vector.scalar_tensor_tensor(key[:], srcf[:], float(COLS), dst_f[:], ALU.mult, ALU.add)
            steps = first[:].rearrange("p (q k) -> p q k", k=Q4)[:, :, 0]
            nc.vector.tensor_copy(first_node[:], steps[0:1])
            nc.vector.tensor_scalar(node_in_window[:], steps, lane[:], None, ALU.add)
            nc.vector.tensor_tensor(rel[:].rearrange("p (q k) -> p q k", k=Q4), dst_f[:].rearrange("p (q k) -> p q k", k=Q4),
                                    steps.unsqueeze(2).broadcast_to((P, NQ, Q4)), ALU.subtract)
            nc.vector.tensor_tensor(slack[:, 0, :], dst_f[:], first[:], ALU.subtract)
            nc.vector.tensor_tensor(slack[:, 1, 0:ET - 1], first[:, 1:ET], dst_f[:, 0:ET - 1], ALU.subtract)
            nc.vector.tensor_tensor(slack[:, 2, :].rearrange("p (q k) -> p q k", k=2),
                                    first[:].rearrange("p (q k) -> p q k", k=2)[:, :, 0].unsqueeze(2).broadcast_to((P, NPAIR, 2)),
                                    dst_f[:].rearrange("p (q k) -> p q k", k=2), ALU.subtract)
            nc.vector.tensor_tensor(slack[:, 4, :], dst_f[:], block_f[:].rearrange("p w k -> p (w k)")[:, 0:ET], ALU.subtract)
            dve.drain()
            nc.vector.tensor_scalar(slack[:, 3, :], rel[:], -1.0, P - 1.0, ALU.mult, ALU.add)
            nc.vector.tensor_scalar(slack[:, 5, :], slack[:, 4, :], -1.0, 2.0 * BLOCK - HALF_BLOCK - 1.0, ALU.mult, ALU.add)
            nc.vector.tensor_scalar(slack[:, 2, :], slack[:, 2, :], WINDOW - 1.0, None, ALU.add)
            dve.drain()
            nc.vector.tensor_scalar(slack[:, 4, :], slack[:, 4, :], float(HALF_BLOCK), None, ALU.add)
            dve.drain()
            nc.vector.tensor_reduce(least[:], slack[:], AX.X, ALU.min)
            dve.drain()
            nc.vector.tensor_scalar(outside[:], least[:], 0.0, None, ALU.is_lt).then_inc(outside_ready, 1)
            dve.wait_ge(out_ps, 1)
            nc.vector.reduce_sum(least[0:1, 0:1], ps_out[:], axis=AX.X)
            dve.drain()
            nc.vector.tensor_scalar(is_sorted[:], least[0:1, 0:1], 0.5, None, ALU.is_lt)


def attention_tables(nc, kvq_w, kvq_b, kv_dram, q_dram, ident, x):
    ctx = ExitStack()
    with ctx:
        mem = Phase(nc, ctx, "attention_tables")
        xT = mem.sb("axT", [D + 1, NPAD])
        wkvq = mem.sb("awkvq", [D + 1, 3 * D])
        kvq = mem.sb("akvq", [P, NT, 3 * D])
        zero = mem.sb("tzero", [P, D])
        acc = mem.ps("acc3", [P, 4 * BANK])
        loaded = mem.sem("loaded")
        ones_ready = mem.sem("ones_ready")
        xT_ps = mem.sem("xT_ps")
        xT_ready = mem.sem("xT_ready")
        kvq_ps = mem.sem("kvq_ps")
        kvq_read = [mem.sem("kvq_read_act"), mem.sem("kvq_read_dve")]
        tables_stored = mem.sem("tables_stored")
        block = ctx.enter_context(nc.Block())
        H = 4 * BANK // P

        @block.sync
        def _(sp):
            sp.dma_start(wkvq[0:D, :], kvq_w).then_inc(loaded, 16)
            sp.dma_start(wkvq[D:D + 1, :], kvq_b).then_inc(loaded, 16)
            sp.wait_ge(ones_ready, 1)
            sp.dma_start(q_dram[NPAD:Q_ROWS, :], zero[:]).then_inc(tables_stored, 16)
            sp.wait_ge(kvq_read[0], NT // 2 + 1)
            sp.wait_ge(kvq_read[1], NT // 2)
            sp.dma_start(kv_dram.rearrange("(t p) c -> p t c", p=P), kvq[:, :, 0:2 * D]).then_inc(tables_stored, 16)
            sp.dma_start(q_dram[0:NPAD, :].rearrange("(t p) c -> p t c", p=P), kvq[:, :, 2 * D:3 * D]).then_inc(tables_stored, 16)
            sp.wait_ge(tables_stored, 48)

        @block.scalar
        def _(act):
            act.wait_ge(xT_ps, 1)
            nc.scalar.copy(xT[0:D, 0:H * P], acc[0:D, 0:H * P]).then_inc(xT_ready, 1)
            act.wait_ge(xT_ps, 2)
            nc.scalar.copy(xT[0:D, H * P:NPAD], acc[0:D, 0:NPAD - H * P]).then_inc(xT_ready, 1)
            for t in range(0, NT, 2):
                act.wait_ge(kvq_ps, t + 1)
                at = (t % 4) * BANK
                nc.scalar.copy(kvq[:, t, :], acc[:, at:at + 3 * D]).then_inc(kvq_read[0], 1)

        @block.tensor
        def _(pe):
            for t in range(NT):
                if t == H:
                    last.then_inc(xT_ps, 1)
                    pe.wait_ge(xT_ready, 1)
                at = t % H * P
                last = nc.tensor.transpose(acc[0:D, at:at + P], x[:, t, :], ident[:])
            last.then_inc(xT_ps, 1)
            pe.wait_ge(xT_ready, 2)
            pe.wait_ge(ones_ready, 1)
            pe.wait_ge(loaded, 32)
            for t in range(NT):
                if t >= 4:
                    pe.wait_ge(kvq_read[t % 2], t // 2 - 1)
                at = (t % 4) * BANK
                nc.tensor.matmul(acc[:, at:at + 3 * D], xT[:, t * P:(t + 1) * P], wkvq[:], start=True, stop=True).then_inc(kvq_ps, 1)

        @block.vector
        def _(dve):
            nc.vector.memset(zero[:], 0.0)
            nc.vector.memset(xT[D:D + 1, :], 1.0).then_inc(ones_ready, 1)
            for t in range(1, NT, 2):
                dve.wait_ge(kvq_ps, t + 1)
                at = (t % 4) * BANK
                nc.vector.tensor_copy(kvq[:, t, :], acc[:, at:at + 3 * D]).then_inc(kvq_read[1], 1)


def attention_windowed(nc, attr_T, we, src_i, rel, node_in_window, first_node, dstf_dram, kv_dram, q_dram, ident, total):
    ctx = ExitStack()
    with ctx:
        mem = Phase(nc, ctx, "attention_windowed")
        iota_i = mem.sb("viota_i", [P, P], I32)
        iota = mem.sb("viota", [P, P])
        wes = mem.sb("vwe", [D + 1, D])
        attr = mem.sb("vattr", [D + 1, SLOTS, Q4 * P])
        drow = mem.sb("vdrow", [P, SLOTS, Q4 * P])
        q_rows = mem.sb("q_rows", [P, SLOTS, D])
        hot = [mem.sb(f"hot{s}", [P, Q4, P]) for s in range(SLOTS)]
        hot_T = [mem.sb(f"hot_T{s}", [P, Q4, P]) for s in range(SLOTS)]
        src4 = [mem.sb(f"vsrc4_{s}", [P, Q4], I32) for s in range(SLOTS)]
        kv = [mem.sb(f"vkv{s}", [P, Q4, 2 * D]) for s in range(SLOTS)]
        prod = mem.sb("vprod", [P, Q4, D])
        score = mem.sb("vscore", [P, Q4, HEADS])
        msg = [mem.sb(f"vmsg{s}", [P, Q4, ROWW]) for s in range(SLOTS)]
        sums_T = mem.sb("sums_T", [ROWW, Q_ROWS])
        ps_e = [mem.ps(f"vps_e{s}", [P, Q4, D]) for s in range(2)]
        ps_q = [mem.ps(f"vps_q{s}", [P, Q4, D]) for s in range(2)]
        ps_s = [mem.ps(f"vps_s{s}", [ROWW, P]) for s in range(2)]
        ps_t = mem.ps("vps_t", [P, 2, BANK])

        loaded = mem.sem("loaded")
        iota_ready = mem.sem("iota_ready")
        ones_ready = mem.sem("ones_ready")
        edges_landed = [mem.sem(f"edges_landed{s}") for s in range(SLOTS)]
        src_ready = mem.sem("src_ready")
        kv_landed = [mem.sem(f"kv_landed{s}") for s in range(SLOTS)]
        hot_ready = mem.sem("hot_ready")
        eq_ready = mem.sem("eq_ready")
        clip_ready = mem.sem("clip_ready")
        exp_ready = mem.sem("exp_ready")
        msg_ready = mem.sem("msg_ready")
        sums_ready = mem.sem("sums_ready")
        sums_added = mem.sem("sums_added")
        turned_ps = mem.sem("turned_ps")
        turned_read = mem.sem("turned_read")
        past_waits = mem.sem("past_waits")
        block = ctx.enter_context(nc.Block())
        CLIP = 5.0 * float(np.sqrt(np.float32(HD)))

        @block.sync
        def _(sp):
            sp.dma_start(wes[:], we).then_inc(loaded, 16)
            sp.wait_ge(ones_ready, 1)

            def load(i, s):
                q = SLOTS * i + s
                if reaches(q, SLOTS):
                    sp.wait_ge(hot_ready, q - SLOTS + 1)
                    sp.wait_ge(eq_ready, q - SLOTS + 1)
                sp.dma_start(attr[0:D, s, :], attr_T[:, bass.ds(q * (Q4 * P), Q4 * P)]).then_inc(edges_landed[s], 16)
                sp.dma_start(drow[:, s, :], dstf_dram[bass.ds(q * (Q4 * P), Q4 * P)].partition_broadcast(P)).then_inc(edges_landed[s], 16)
                at = sp.value_load(first_node[0:1, bass.ds(q, 1)], min_val=0, max_val=N)
                sp.dma_start(q_rows[:, s, :], q_dram[bass.ds(at, P), :]).then_inc(edges_landed[s], 16)

            for s in range(SLOTS):
                load(0, s)
            with sp.Fori(1, ROUNDS) as i:
                for s in range(SLOTS):
                    load(i, s)
            for s in range(NQ - SLOTS * ROUNDS):
                load(ROUNDS, s)

        @block.gpsimd
        def _(pool):
            nc.gpsimd.iota(iota_i[:], pattern=[[1, P]], base=0, channel_multiplier=0).then_inc(iota_ready, 1)
            last_node = pool.to_reg(NPAD - 1)

            def gather(i, s):
                q = SLOTS * i + s
                pool.wait_ge(src_ready, q + 1)
                if reaches(q, SLOTS):
                    pool.wait_ge(msg_ready, q - SLOTS + 1)
                pool.sem_inc(past_waits, 1)
                for k in range(Q4):
                    nc.gpsimd.indirect_dma_start(
                        out=kv[s][:, k, :], out_offset=None, in_=kv_dram,
                        in_offset=bass.IndirectOffsetOnAxis(ap=src4[s][:, k:k + 1], axis=0),
                        bounds_check=last_node, oob_is_err=True).then_inc(kv_landed[s], 16)

            for s in range(SLOTS):
                gather(0, s)
            with pool.Fori(1, ROUNDS) as i:
                for s in range(SLOTS):
                    gather(i, s)
            for s in range(NQ - SLOTS * ROUNDS):
                gather(ROUNDS, s)

        @block.scalar
        def _(act):
            def indices(i, s):
                q = SLOTS * i + s
                if reaches(q, SLOTS):
                    act.wait_ge(kv_landed[s], 16 * Q4 * i)
                nc.scalar.activation(src4[s][:], src_i[:, bass.ds(q * Q4, Q4)], ACT.Copy).then_inc(src_ready, 1)

            def weigh(i, s):
                act.wait_ge(clip_ready, SLOTS * i + s + 1)
                nc.scalar.activation(msg[s][:, :, D:ROWW], score[:], ACT.Exp,
                                     scale=1.0 / float(np.sqrt(np.float32(HD)))).then_inc(exp_ready, 1)

            for s in range(SLOTS):
                indices(0, s)
            with act.Fori(0, ROUNDS - 1) as i:
                for s in range(SLOTS):
                    weigh(i, s)
                    indices(i + 1, s)
            for s in range(SLOTS):
                weigh(ROUNDS - 1, s)
                if SLOTS * ROUNDS + s < NQ:
                    indices(ROUNDS, s)
            for s in range(NQ - SLOTS * ROUNDS):
                weigh(ROUNDS, s)

        @block.tensor
        def _(pe):
            pe.wait_ge(loaded, 16)

            def edges(i, s):
                q = SLOTS * i + s
                pe.wait_ge(edges_landed[s], 48 * (i + 1))
                pe.wait_ge(hot_ready, q + 1)
                if reaches(q, 2):
                    pe.wait_ge(clip_ready, q - 1)
                for k in range(Q4):
                    nc.tensor.matmul(ps_e[s % 2][:, k, :], attr[:, s, k * P:(k + 1) * P], wes[:], start=True, stop=True)
                for k in range(Q4):
                    last = nc.tensor.matmul(ps_q[s % 2][:, k, :], hot_T[s][:, k, :], q_rows[:, s, :], start=True, stop=True)
                last.then_inc(eq_ready, 1)

            def add_up(i, s):
                q = SLOTS * i + s
                pe.wait_ge(msg_ready, q + 1)
                if reaches(q, 2):
                    pe.wait_ge(sums_added, q - 1)
                for k in range(Q4):
                    last = nc.tensor.matmul(ps_s[s % 2][:], msg[s][:, k, :], hot[s][:, k, :], start=k == 0, stop=k == Q4 - 1)
                last.then_inc(sums_ready, 1)

            edges(0, 0)
            for s in range(SLOTS):
                edges(*later(0, s, 1))
                add_up(0, s)
            with pe.Fori(1, ROUNDS) as i:
                for s in range(SLOTS):
                    edges(*later(i, s, 1))
                    add_up(i, s)
            for s in range(NQ - SLOTS * ROUNDS):
                if SLOTS * ROUNDS + s + 1 < NQ:
                    edges(ROUNDS, s + 1)
                add_up(ROUNDS, s)
            pe.wait_ge(sums_added, NQ)
            for n, t in enumerate(range(0, NT, 4)):
                if n >= 2:
                    pe.wait_ge(turned_read, n - 1)
                for u in range(t, min(t + 4, NT)):
                    last = nc.tensor.transpose(ps_t[:, n % 2, (u - t) * ROWW:(u - t + 1) * ROWW], sums_T[:, u * P:(u + 1) * P],
                                               ident[0:ROWW, 0:ROWW])
                last.then_inc(turned_ps, 1)

        @block.vector
        def _(dve):
            nc.vector.memset(attr[D:D + 1, :, :], 1.0).then_inc(ones_ready, 1)
            nc.vector.memset(sums_T[:], 0.0)
            dve.wait_ge(iota_ready, 1)
            nc.vector.tensor_copy(iota[:], iota_i[:])
            dve.drain()

            def prepare(i, s):
                q = SLOTS * i + s
                dve.wait_ge(edges_landed[s], 48 * (i + 1))
                if reaches(q, SLOTS):
                    dve.wait_ge(sums_ready, q - SLOTS + 1)
                nc.vector.tensor_scalar(hot_T[s][:].rearrange("p k e -> p (k e)"), drow[:, s, :], node_in_window[:, bass.ds(q, 1)],
                                        None, ALU.is_equal)
                nc.vector.tensor_tensor(hot[s][:], iota[:].unsqueeze(1).broadcast_to((P, Q4, P)),
                                        rel[:, bass.ds(q * Q4, Q4)].unsqueeze(2).broadcast_to((P, Q4, P)),
                                        ALU.is_equal).then_inc(hot_ready, 1)

            def attend(i, s):
                q = SLOTS * i + s
                dve.wait_ge(kv_landed[s], 16 * Q4 * (i + 1))
                dve.wait_ge(eq_ready, q + 1)
                nc.vector.tensor_tensor(prod[:], kv[s][:, :, 0:D], ps_q[s % 2][:], ALU.mult)
                dve.drain()
                nc.vector.tensor_tensor(prod[:], prod[:], ps_e[s % 2][:], ALU.mult)
                dve.drain()
                nc.vector.reduce_sum(score[:].rearrange("p k h -> p (k h)"), prod[:].rearrange("p k (h c) -> p (k h) c", c=HD), axis=AX.X)
                dve.drain()
                nc.vector.tensor_scalar(score[:], score[:], CLIP, -CLIP, ALU.min, ALU.max).then_inc(clip_ready, 1)

            def weigh(i, s):
                dve.wait_ge(exp_ready, SLOTS * i + s + 1)
                nc.vector.tensor_tensor(msg[s][:, :, 0:D].rearrange("p k (h c) -> p k h c", c=HD),
                                        kv[s][:, :, D:2 * D].rearrange("p k (h c) -> p k h c", c=HD),
                                        msg[s][:, :, D:ROWW].unsqueeze(3).broadcast_to((P, Q4, HEADS, HD)),
                                        ALU.mult).then_inc(msg_ready, 1)

            def add(i, s):
                q = SLOTS * i + s
                at = dve.value_load(first_node[0:1, bass.ds(q, 1)], min_val=0, max_val=N)
                dve.wait_ge(sums_ready, q + 1)
                nc.vector.tensor_tensor(sums_T[:, bass.ds(at, P)], sums_T[:, bass.ds(at, P)], ps_s[s % 2][:], ALU.add).then_inc(sums_added, 1)

            prepare(0, 0)
            prepare(0, 1)
            for s in range(SLOTS):
                attend(0, s)
                prepare(*later(0, s, 2))
                if s > 0:
                    add(0, s - 1)
                weigh(0, s)
            with dve.Fori(1, ROUNDS) as i:
                for s in range(SLOTS):
                    attend(i, s)
                    prepare(*later(i, s, 2))
                    add(*later(i, s, -1))
                    weigh(i, s)
            for s in range(NQ - SLOTS * ROUNDS):
                attend(ROUNDS, s)
                add(*later(ROUNDS, s, -1))
                weigh(ROUNDS, s)
            add(*later(ROUNDS, NQ - SLOTS * ROUNDS, -1))
            for n, t in enumerate(range(0, NT, 4)):
                m = min(4, NT - t)
                dve.wait_ge(turned_ps, n + 1)
                nc.vector.tensor_copy(total[:, t:t + m, :].rearrange("p t c -> p (t c)"), ps_t[:, n % 2, 0:m * ROWW]).then_inc(turned_read, 1)


def attention_general(nc, attr_T, we, src_i, dst_i, dstf_dram, kv_dram, q_dram, sums_dram, total):
    ctx = ExitStack()
    with ctx:
        mem = Phase(nc, ctx, "attention_general")
        dstf = mem.sb("adstf", [P, ET])
        dst_off = mem.sb("adst_off", [P, ET])
        dump_i = mem.sb("adump_i", [P, 1], I32)
        dump = mem.sb("adump", [P, 1])
        before = mem.sb("abefore", [P, P])
        zero = mem.sb("azero", [P, 26 * ROWW])
        wes = mem.sb("awe", [D + 1, D])
        attr = mem.sb("attr", [D + 1, 2, Q4 * P])
        drow = mem.sb("drow", [P, 2, Q4 * P])
        eq = mem.sb("aeq", [P, 2, Q4, P])
        eqb = mem.sb("aeqb", [P, Q4, P])
        earlier = mem.sb("aearlier", [P, Q4])
        first_off = mem.sb("afirst_off", [P, Q4])
        src4 = [mem.sb(f"src4_{s}", [P, Q4], I32) for s in range(2)]
        dst4 = [mem.sb(f"dst4_{s}", [P, Q4], I32) for s in range(2)]
        row4 = [mem.sb(f"row4_{s}", [P, Q4], I32) for s in range(2)]
        kv = [mem.sb(f"kv{s}", [P, Q4, 2 * D]) for s in range(2)]
        qg = [mem.sb(f"qg{s}", [P, Q4, D]) for s in range(2)]
        prod = mem.sb("prod", [P, Q4, D])
        score = mem.sb("score", [P, Q4, HEADS])
        msg = [mem.sb(f"msg{s}", [P, Q4, ROWW]) for s in range(2)]
        pay = [mem.sb(f"apay{s}", [P, Q4, ROWW]) for s in range(2)]
        other = mem.sb("other", [P, NT, ROWW])
        ps_e = [mem.ps(f"ps_e{s}", [P, Q4, D]) for s in range(2)]
        ps_m = [mem.ps(f"ps_m{s}", [P, Q4, ROWW]) for s in range(2)]

        loaded = mem.sem("loaded")
        consts_ready = mem.sem("consts_ready")
        zero_ready = mem.sem("zero_ready")
        zeroed = mem.sem("zeroed")
        attr_ones = mem.sem("attr_ones")
        edges_landed = [mem.sem(f"edges_landed{s}") for s in range(2)]
        kv_landed = [mem.sem(f"kv_landed{s}") for s in range(2)]
        prep_ready = mem.sem("prep_ready")
        e_ready = mem.sem("e_ready")
        clip_ready = mem.sem("clip_ready")
        exp_ready = mem.sem("exp_ready")
        msg_ready = mem.sem("msg_ready")
        sums_ready = mem.sem("sums_ready")
        pay_ready = mem.sem("pay_ready")
        row_landed = [mem.sem(f"arow_landed{k}") for k in range(Q4)]
        sums_back = mem.sem("sums_back")
        past_waits = mem.sem("past_waits")
        block = ctx.enter_context(nc.Block())
        CLIP = 5.0 * float(np.sqrt(np.float32(HD)))

        @block.sync
        def _(sp):
            sp.dma_start(wes[:], we).then_inc(loaded, 16)
            sp.wait_ge(attr_ones, 1)

            def load(q, s, first=False):
                if not first:
                    sp.wait_ge(prep_ready, q - 1)
                    sp.wait_ge(e_ready, q - 1)
                sp.dma_start(attr[0:D, s, :], attr_T[:, bass.ds(q * (Q4 * P), Q4 * P)]).then_inc(edges_landed[s], 16)
                sp.dma_start(drow[:, s, :], dstf_dram[bass.ds(q * (Q4 * P), Q4 * P)].partition_broadcast(P)).then_inc(edges_landed[s], 16)

            load(0, 0, True)
            load(1, 1, True)
            with sp.Fori(1, NQ // 2) as i:
                for s in range(2):
                    load(2 * i + s, s)
            for k in range(Q4):
                sp.wait_ge(row_landed[k], 16 * NQ)
            for tile, sums in ((total, sums_dram[0]), (other, sums_dram[1])):
                sp.dma_start(tile[:], sums[0:NPAD, :].rearrange("(t p) c -> p t c", p=P)).then_inc(sums_back, 16)

        @block.gpsimd
        def _(pool):
            nc.gpsimd.iota(dump_i[:], pattern=[[1, 1]], base=NPAD, channel_multiplier=1)
            nc.gpsimd.memset(before[:], 1.0)
            pool.drain()
            nc.gpsimd.affine_select(out=before[:], in_=before[:], compare_op=ALU.is_gt, fill=0.0, base=0,
                                    pattern=[[-1, P]], channel_multiplier=1).then_inc(consts_ready, 1)
            pool.wait_ge(zeroed, 16 * NACC)
            last_node = pool.to_reg(NPAD - 1)
            last_row = pool.to_reg(ACC_ROWS - 1)

            def gather(q, s, k):
                nc.gpsimd.indirect_dma_start(
                    out=kv[s][:, k, :], out_offset=None, in_=kv_dram,
                    in_offset=bass.IndirectOffsetOnAxis(ap=src4[s][:, k:k + 1], axis=0),
                    bounds_check=last_node, oob_is_err=True).then_inc(kv_landed[s], 16)
                nc.gpsimd.indirect_dma_start(
                    out=qg[s][:, k, :], out_offset=None, in_=q_dram,
                    in_offset=bass.IndirectOffsetOnAxis(ap=dst4[s][:, k:k + 1], axis=0),
                    bounds_check=last_node, oob_is_err=True).then_inc(kv_landed[s], 16)

            def scatter(q, s, k):
                if k >= NACC:
                    pool.wait_ge(row_landed[k - NACC], 16 * (q + 1))
                elif not isinstance(q, int) or q > 0:
                    pool.wait_ge(row_landed[k + Q4 - NACC], 16 * q)
                pool.sem_inc(past_waits, 1)
                nc.gpsimd.indirect_dma_start(
                    out=sums_dram[k % NACC], out_offset=bass.IndirectOffsetOnAxis(ap=row4[s][:, k:k + 1], axis=0),
                    in_=pay[s][:, k, :], in_offset=None, bounds_check=last_row, oob_is_err=True,
                    compute_op=ALU.add).then_inc(row_landed[k], 16)

            def step(q, s, first=False):
                pool.wait_ge(prep_ready, q + 1)
                if not first:
                    pool.wait_ge(msg_ready, q - 1)
                pool.sem_inc(past_waits, 1)
                for k in range(Q4):
                    gather(q, s, k)
                    if not isinstance(q, int) or q > 0:
                        if k == 0:
                            pool.wait_ge(pay_ready, q)
                        scatter(q - 1, 1 - s, k)

            step(0, 0, True)
            step(1, 1, True)
            with pool.Fori(1, NQ // 2) as i:
                for s in range(2):
                    step(2 * i + s, s)
            pool.wait_ge(pay_ready, NQ)
            for k in range(Q4):
                scatter(NQ - 1, 1, k)

        @block.scalar
        def _(act):
            act.wait_ge(zero_ready, 1)
            for a in range(NACC):
                act.dma_start(sums_dram[a].rearrange("(p r) c -> p (r c)", p=P), zero[:]).then_inc(zeroed, 16)
            def step(q, s, first=False):
                act.wait_ge(clip_ready, q + 1)
                nc.scalar.activation(msg[s][:, :, D:ROWW], score[:], ACT.Exp, scale=1.0 / float(np.sqrt(np.float32(HD)))).then_inc(exp_ready, 1)
                act.wait_ge(sums_ready, q + 1)
                if not first:
                    for k in range(Q4):
                        act.wait_ge(row_landed[k], 16 * (q - 1))
                nc.scalar.copy(pay[s][:], ps_m[s][:]).then_inc(pay_ready, 1)

            step(0, 0, True)
            step(1, 1, True)
            with act.Fori(1, NQ // 2) as i:
                for s in range(2):
                    step(2 * i + s, s)

        @block.tensor
        def _(pe):
            pe.wait_ge(loaded, 16)

            def edges(q, s, use, first=False):
                pe.wait_ge(edges_landed[s], 32 * (use + 1))
                if not first:
                    pe.wait_ge(msg_ready, q - 1)
                for k in range(Q4):
                    last = nc.tensor.matmul(ps_e[s][:, k, :], attr[:, s, k * P:(k + 1) * P], wes[:], start=True, stop=True)
                last.then_inc(e_ready, 1)

            def add_up(q, s, first=False):
                pe.wait_ge(msg_ready, q + 1)
                if not first:
                    pe.wait_ge(pay_ready, q - 1)
                for k in range(Q4):
                    last = nc.tensor.matmul(ps_m[s][:, k, :], eq[:, s, k, :], msg[s][:, k, :], start=True, stop=True)
                last.then_inc(sums_ready, 1)

            edges(0, 0, 0, True)
            edges(1, 1, 0, True)
            add_up(0, 0, True)
            edges(2, 0, 1)
            add_up(1, 1, True)
            with pe.Fori(1, NQ // 2 - 1) as i:
                edges(2 * i + 1, 1, i)
                add_up(2 * i, 0)
                edges(2 * i + 2, 0, i + 1)
                add_up(2 * i + 1, 1)
            edges(NQ - 1, 1, NQ // 2 - 1)
            add_up(NQ - 2, 0)
            add_up(NQ - 1, 1)

        @block.vector
        def _(dve):
            nc.vector.memset(zero[:], 0.0).then_inc(zero_ready, 1)
            nc.vector.memset(attr[D:D + 1, :, :], 1.0).then_inc(attr_ones, 1)
            dve.wait_ge(consts_ready, 1)
            nc.vector.tensor_copy(dstf[:], dst_i[:])
            nc.vector.tensor_copy(dump[:], dump_i[:])
            dve.drain()
            nc.vector.tensor_scalar(dst_off[:], dstf[:], dump[:], None, ALU.subtract)

            def prepare(q, s, use, first=False):
                dve.wait_ge(edges_landed[s], 32 * (use + 1))
                if not first:
                    dve.wait_ge(sums_ready, q - 1)
                    for k in range(Q4):
                        dve.wait_ge(row_landed[k], 16 * (q - 1))
                nc.vector.tensor_copy(src4[s][:], src_i[:, bass.ds(q * Q4, Q4)])
                nc.vector.tensor_copy(dst4[s][:], dst_i[:, bass.ds(q * Q4, Q4)])
                for k in range(Q4):
                    nc.vector.tensor_scalar(eq[:, s, k, :], drow[:, s, k * P:(k + 1) * P], dstf[:, bass.ds(q * Q4 + k, 1)],
                                            None, ALU.is_equal)
                dve.drain()
                nc.vector.tensor_tensor(eqb[:], eq[:, s, :, :], before[:].unsqueeze(1).broadcast_to((P, Q4, P)), ALU.mult)
                dve.drain()
                nc.vector.reduce_sum(earlier[:], eqb[:], axis=AX.X)
                dve.drain()
                nc.vector.scalar_tensor_tensor(first_off[:], earlier[:], 0.5, dst_off[:, bass.ds(q * Q4, Q4)], ALU.is_lt, ALU.mult)
                dve.drain()
                nc.vector.tensor_scalar(row4[s][:], first_off[:], dump[:], None, ALU.add).then_inc(prep_ready, 1)

            def attend(q, s, use, first=False):
                dve.wait_ge(kv_landed[s], 32 * Q4 * (use + 1))
                nc.vector.tensor_tensor(prod[:], kv[s][:, :, 0:D], qg[s][:], ALU.mult)
                dve.drain()
                dve.wait_ge(e_ready, q + 1)
                nc.vector.tensor_tensor(prod[:], prod[:], ps_e[s][:], ALU.mult)
                dve.drain()
                nc.vector.reduce_sum(score[:].rearrange("p k h -> p (k h)"), prod[:].rearrange("p k (h c) -> p (k h) c", c=HD), axis=AX.X)
                dve.drain()
                nc.vector.tensor_scalar(score[:], score[:], CLIP, -CLIP, ALU.min, ALU.max).then_inc(clip_ready, 1)
                dve.wait_ge(exp_ready, q + 1)
                nc.vector.tensor_tensor(msg[s][:, :, 0:D].rearrange("p k (h c) -> p k h c", c=HD),
                                        kv[s][:, :, D:2 * D].rearrange("p k (h c) -> p k h c", c=HD),
                                        msg[s][:, :, D:ROWW].unsqueeze(3).broadcast_to((P, Q4, HEADS, HD)),
                                        ALU.mult).then_inc(msg_ready, 1)

            prepare(0, 0, 0, True)
            prepare(1, 1, 0, True)
            attend(0, 0, 0)
            prepare(2, 0, 1)
            attend(1, 1, 0)
            with dve.Fori(1, NQ // 2 - 1) as i:
                prepare(2 * i + 1, 1, i)
                attend(2 * i, 0, i)
                prepare(2 * i + 2, 0, i + 1)
                attend(2 * i + 1, 1, i)
            prepare(NQ - 1, 1, NQ // 2 - 1)
            attend(NQ - 2, 0, NQ // 2 - 1)
            attend(NQ - 1, 1, NQ // 2 - 1)

            dve.wait_ge(sums_back, 16 * NACC)
            nc.vector.tensor_tensor(total[:], total[:], other[:], ALU.add)


def attention_out(nc, total, x, eps, out):
    ctx = ExitStack()
    with ctx:
        mem = Phase(nc, ctx, "attention_out")
        stats = (mem.sb("st3", [P, NT, 6]), mem.sb("dif3", [P, NT]), mem.sb("var3", [P, NT]))
        mean = mem.sb("mean3", [P, NT])
        sd = mem.sb("sd3", [P, NT])
        z = mem.sb("z", [P, NT, HEADS])
        res = mem.sb("res", [P, NT, D])
        result = mem.sb("result", [P, NT, D])
        var_ready = mem.sem("var_ready")
        sd_ready = mem.sem("sd_ready")
        out_ready = mem.sem("out_ready")
        out_stored = mem.sem("out_stored")
        block = ctx.enter_context(nc.Block())

        @block.sync
        def _(sp):
            sp.wait_ge(out_ready, 1)
            sp.dma_start(out[0:(NT - 1) * P, :].rearrange("(t p) d -> p t d", p=P), result[:, 0:NT - 1, :]).then_inc(out_stored, 16)
            sp.dma_start(out[(NT - 1) * P:N, :], result[0:LAST, NT - 1, :]).then_inc(out_stored, 16)
            sp.wait_ge(out_stored, 32)

        @block.scalar
        def _(act):
            act.wait_ge(var_ready, 1)
            nc.scalar.activation(sd[:], stats[2][:], ACT.Sqrt, bias=eps[:, 0:1]).then_inc(sd_ready, 1)

        @block.vector
        def _(dve):
            nc.vector.tensor_scalar(z[:], total[:, :, D:ROWW], 1e-6, None, ALU.add)
            dve.drain()
            nc.vector.reciprocal(z[:], z[:])
            dve.drain()
            nc.vector.tensor_tensor(res[:].rearrange("p t (h c) -> p t h c", c=HD),
                                    total[:, :, 0:D].rearrange("p t (h c) -> p t h c", c=HD),
                                    z[:].unsqueeze(3).broadcast_to((P, NT, HEADS, HD)), ALU.mult)
            dve.drain()
            nc.vector.tensor_tensor(x[:], x[:], res[:], ALU.add)
            dve.drain()
            layer_norm(nc, dve, stats, x, result, mean, sd, var_ready, sd_ready, 1).then_inc(out_ready, 1)


def build(nc, a):
    def dram(name, shape):
        return nc.dram_tensor(name, shape, F32).ap()

    adj = dram("adj", [CELLS, 2])
    adj_count = dram("adj_count", [NPAD, COLS])
    adj_weight = dram("adj_weight", [NPAD, COLS])
    key_dram = dram("key_dram", [EPAD])
    dstf_dram = dram("dstf_dram", [EPAD])
    kv_dram = dram("kv_dram", [NPAD, 2 * D])
    q_dram = dram("q_dram", [Q_ROWS, D])
    sums_dram = [dram(f"sums_dram{i}", [ACC_ROWS, ROWW]) for i in range(NACC)]
    with (
        nc.sbuf_tensor("ident", [P, P], F32) as ident,
        nc.sbuf_tensor("x", [P, NT, D], F32) as x,
        nc.sbuf_tensor("w_deg", [P, NT], F32) as w_deg,
        nc.sbuf_tensor("eps", [P, 2], F32) as eps,
        nc.sbuf_tensor("src_i", [P, ET], I32) as src_i,
        nc.sbuf_tensor("dst_i", [P, ET], I32) as dst_i,
        nc.sbuf_tensor("rel", [P, ET], F32) as rel,
        nc.sbuf_tensor("node_in_window", [P, NQ], F32) as node_in_window,
        nc.sbuf_tensor("first_node", [1, NQ], I32) as first_node,
        nc.sbuf_tensor("is_sorted", [1, 1], I32) as is_sorted,
        nc.sbuf_tensor("key", [P, ET], F32) as key,
        nc.sbuf_tensor("dst_f", [P, ET], F32) as dst_f,
    ):
        examine_edges(nc, src_i, dst_i, a["dst_cols"], a["src_cols"], a["dst_flat"], dstf_dram, key, dst_f, rel, node_in_window, first_node, is_sorted,
                      ident, eps)
        in_order = nc.values_load(is_sorted[0:1, 0:1], min_val=0, max_val=1)
        with nc.sbuf_tensor("agg", [P, NPAD], F32) as agg:
            with nc.If(in_order == 1):
                with (
                    nc.sbuf_tensor("lhs_all", [P, NT, D + 2], F32) as lhs_all,
                    nc.sbuf_tensor("weight_parts", [P, 3, ET], F32) as weight_parts,
                    nc.sbuf_tensor("ring_col", [1, NPAIR], I32) as ring_col,
                    nc.sbuf_tensor("strip", [P, 2, NT, RING + WINDOW], F32) as strip,
                ):
                    edge_tables(nc, src_i, key, dst_f, a["w_cols"], a["x_nm"], ident, x, lhs_all, weight_parts, ring_col, strip)
                    add_edges(nc, key, dst_f, weight_parts, ring_col, lhs_all, strip, adj_count, adj_weight, agg)
            with nc.Else():
                build_adjacency(nc, key, a["w_cols"], a["src_flat"], a["dst_flat"], key_dram, dstf_dram, adj)
                first_pass(nc, a["x_nm"], adj, adj_count, adj_weight, x, agg)
            first_layer_out(nc, a["L0_gnn_weight"], a["L0_gnn_bias"], ident, adj_weight, x, agg, w_deg, eps)
        convolutions(nc, adj_count, adj_weight,
                     [a[k] for k in ("L1_gnn_W1", "L1_gnn_W2", "L1_gnn_W3", "L2_gnn_W1", "L2_gnn_W2")],
                     [a[k] for k in ("L1_gnn_b1", "L1_gnn_b2", "L1_gnn_b3")],
                     [a[f"L2_gnn_{k}"] for k in ("b1", "gn1_w", "gn1_b", "gn1_a", "b2", "gn2_w", "gn2_b", "gn2_a")],
                     ident, x, w_deg, eps)
        attention_tables(nc, a["kvq_w"], a["kvq_b"], kv_dram, q_dram, ident, x)
        with nc.sbuf_tensor("total", [P, NT, ROWW], F32) as total:
            in_order = nc.values_load(is_sorted[0:1, 0:1], min_val=0, max_val=1)
            with nc.If(in_order == 1):
                attention_windowed(nc, a["attr_T"], a["we"], src_i, rel, node_in_window, first_node, dstf_dram, kv_dram, q_dram,
                                   ident, total)
            with nc.Else():
                attention_general(nc, a["attr_T"], a["we"], src_i, dst_i, dstf_dram, kv_dram, q_dram, sums_dram, total)
            attention_out(nc, total, x, eps, a["out"])


def kernel(**inputs):
    import concourse.bacc as bacc
    from concourse.bass_utils import run_bass_kernel_spmd

    given = {k: np.asarray(v) for k, v in inputs.items()}

    def edge_list(values, fill):
        padded = np.empty((EPAD,), values.dtype)
        padded[:E] = values
        padded[E:] = fill
        return padded

    past = N + np.arange(E, EPAD) // P - E // P
    src, dst, w = edge_list(given["src"], N), edge_list(given["dst"], past), edge_list(given["edge_weight"], 0)
    attr = np.zeros((D, EPAD), np.float32)
    attr[:, :E] = given["edge_attr_96"].T
    x = np.zeros((NPAD, D), np.float32)
    x[:N] = given["x"]
    arrays = {
        "src_cols": np.ascontiguousarray(src.reshape(ET, P).T),
        "dst_cols": np.ascontiguousarray(dst.reshape(ET, P).T),
        "w_cols": np.ascontiguousarray(w.reshape(ET, P).T),
        "src_flat": src.reshape(P, ET),
        "dst_flat": dst.reshape(P, ET),
        "attr_T": attr,
        "x_nm": np.ascontiguousarray(x.reshape(NT, P, D).transpose(1, 0, 2)),
        "we": np.concatenate([given["L3_gnn_We"], given["L3_gnn_be"][None]]),
        "kvq_w": np.concatenate([given["L3_gnn_Wk"], given["L3_gnn_Wv"], given["L3_gnn_Wq"]], axis=1),
        "kvq_b": np.concatenate([given["L3_gnn_bk"], given["L3_gnn_bv"], given["L3_gnn_bq"]])[None],
    }
    for name, value in given.items():
        if name.startswith(("L0", "L1", "L2")):
            arrays[name] = np.ascontiguousarray(value)
    nc = bacc.Bacc("TRN2", target_bir_lowering=False, num_devices=1)
    aps = {}
    for name, value in arrays.items():
        aps[name] = nc.dram_tensor(f"in_{name}", value.shape, mybir.dt.from_np(value.dtype), kind="ExternalInput").ap()
    aps["out"] = nc.dram_tensor("out_x", (N, D), F32, kind="ExternalOutput").ap()
    build(nc, aps)
    result = run_bass_kernel_spmd(nc, [{f"in_{k}": v for k, v in arrays.items()}], core_ids=[0])
    return result.results[0]["out_x"]
```
